# Optimizing a Trainium2 kernel written in Bass

```python
import numpy as np
import jax
import jax.numpy as jnp

def _softmax(x, axis=-1):
    return jax.nn.softmax(x, axis=axis)

def _gelu(x):
    return jax.nn.gelu(x, approximate=True)

def _silu(x):
    return jax.nn.silu(x)

def _sigmoid(x):
    return jax.nn.sigmoid(x)

def _layernorm(x, axis=-1, eps=1e-05):
    m = jnp.mean(x, axis=axis, keepdims=True)
    v = jnp.var(x, axis=axis, keepdims=True)
    return (x - m) / jnp.sqrt(v + eps)

def _scatter_add(tgt, idx, src, axis=0):
    return tgt.at[idx].add(src)

def _segment_sum(src, seg, n):
    return jax.ops.segment_sum(src, seg, n)
kernel_name = 'mk_flamingo_gated_d2_seqx_r4_4ac92a'

def setup_inputs(seed: int=0):
    np.random.seed(seed)
    _w = jnp.asarray

    def _rec_inputs():
        import jax
        import jax.numpy as jnp
        _rk = jax.random.key(seed)
        x = -0.0002928 + 1 * jax.random.normal(jax.random.fold_in(_rk, 1), (8, 256, 256), jnp.float32)
        _lenS = 256 - jax.random.randint(jax.random.fold_in(_rk, 7), (8,), 0, max(1, 256 // 4) + 1, jnp.int32)
        _lenS2 = 120 - jax.random.randint(jax.random.fold_in(_rk, 8), (8,), 0, max(1, 120 // 4) + 1, jnp.int32)
        _ctx_1024P = jax.random.normal(jax.random.fold_in(_rk, 11), (8, 16, 256), jnp.float32)
        _ctx_1024c = jax.random.dirichlet(jax.random.fold_in(_rk, 511), 0.3 * jnp.ones((16,), jnp.float32), (8, 120))
        _ctx_1024t = jnp.einsum('bsk,bkd->bsd', _ctx_1024c, _ctx_1024P)
        _ctx_1024t = _ctx_1024t * jax.lax.rsqrt(jnp.mean(jnp.square(_ctx_1024t)) + 1e-12) * 0.953939
        ctx_1024 = -1.39393e-06 + 0.999914 * (_ctx_1024t + 0.3 * jax.random.normal(jax.random.fold_in(_rk, 611), (8, 120, 256), jnp.float32))
        _validS = jnp.arange(256)[None, :] < _lenS[:, None]
        _validS2 = jnp.arange(120)[None, :] < _lenS2[:, None]
        _causal = jnp.tril(jnp.ones((256, 256), dtype=bool))
        mask_Bx1xS2_bk0 = jnp.logical_not(jnp.broadcast_to(_validS2[:, None, :], (8, 1, 120)))
        mask_SxS2_fk0 = jnp.where(jnp.broadcast_to(_validS2[0:1, :], (256, 120)), -1000000000.0, 0.0).astype(jnp.float32)
        mask_BxS2_bf0 = jnp.logical_not(jnp.ones((8, 120), dtype=bool))
        _g = jax.random.normal(jax.random.fold_in(_rk, 9001), (2, 2), jnp.float32)
        _g = jnp.sign(_g) * jnp.maximum(jnp.abs(_g), 1.0) + (_g == 0) * 1.0
        g_xattn = _g[0]
        g_ffn = _g[1]
        return (x, ctx_1024, mask_Bx1xS2_bk0, mask_SxS2_fk0, mask_BxS2_bf0, g_xattn, g_ffn)
    x, ctx_1024, mask_Bx1xS2_bk0, mask_SxS2_fk0, mask_BxS2_bf0, g_xattn, g_ffn = _rec_inputs()

    def _L0_xattn_setup():
        import jax, jax.numpy as jnp
        import numpy as np
        D_MODEL = 256
        NUM_HEADS = 16
        D_K = D_MODEL // NUM_HEADS
        SCALE = float(np.sqrt(D_K))
        key = jax.random.key(seed)
        ks = jax.random.split(key, 12)
        B, Lq, Lk = (2, 512, 512)
        inp = {'query': jax.random.normal(ks[0], (B, Lq, D_MODEL), jnp.float32), 'key': jax.random.normal(ks[1], (B, Lk, D_MODEL), jnp.float32), 'value': jax.random.normal(ks[2], (B, Lk, D_MODEL), jnp.float32), 'mask': jax.random.randint(ks[3], (B, 1, Lk), 0, 2).astype(bool), 'Wq': jax.random.normal(ks[4], (D_MODEL, D_MODEL), jnp.float32) * 0.02, 'bq': jnp.zeros((D_MODEL,), jnp.float32), 'Wk': jax.random.normal(ks[5], (D_MODEL, D_MODEL), jnp.float32) * 0.02, 'bk': jnp.zeros((D_MODEL,), jnp.float32), 'Wv': jax.random.normal(ks[6], (D_MODEL, D_MODEL), jnp.float32) * 0.02, 'bv': jnp.zeros((D_MODEL,), jnp.float32), 'Wo': jax.random.normal(ks[7], (D_MODEL, D_MODEL), jnp.float32) * 0.02, 'bo': jnp.zeros((D_MODEL,), jnp.float32)}
        return inp
    _L0_xattn_all = _L0_xattn_setup()
    _L0_xattn_in = {k: v for k, v in _L0_xattn_all.items() if k in ('Wq', 'bq', 'Wk', 'bk', 'Wv', 'bv', 'Wo', 'bo')}
    del _L0_xattn_all

    def _L0_ffn_setup():
        import jax, jax.numpy as jnp
        import numpy as np
        B, T, DIM = (2, 512, 256)
        H, DH, E, K = (16, 64, 8, 2)
        key = jax.random.key(seed)
        ks = jax.random.split(key, 7)
        s = 0.02
        return {'x': jax.random.normal(ks[0], (B, T, DIM), jnp.float32), 'Wq': jax.random.normal(ks[1], (H, DH, DIM), jnp.float32) * s, 'Wk': jax.random.normal(ks[2], (H, DH, DIM), jnp.float32) * s, 'Wv': jax.random.normal(ks[3], (E, DH, DIM), jnp.float32) * s, 'Ws': jax.random.normal(ks[4], (H, E, DIM), jnp.float32) * s, 'Wd': jax.random.normal(ks[5], (H, E, DIM), jnp.float32) * s, 'Wo': jax.random.normal(ks[6], (E, DIM, DH), jnp.float32) * s}
    _L0_ffn_all = _L0_ffn_setup()
    _L0_ffn_in = {k: v for k, v in _L0_ffn_all.items() if k in ('Wq', 'Wk', 'Wv', 'Ws', 'Wd', 'Wo')}
    del _L0_ffn_all

    def _L1_xattn_setup():
        import jax, jax.numpy as jnp
        import numpy as np
        B, S, E, H = (2, 512, 256, 16)
        D = E // H
        NEG = -1000000000.0
        key = jax.random.key(seed)
        ks = jax.random.split(key, 12)

        def xavier(k, shape):
            fan_in, fan_out = (shape[1], shape[0])
            lim = jnp.sqrt(6.0 / (fan_in + fan_out))
            return jax.random.uniform(k, shape, jnp.float32, -lim, lim)
        inp = {'Q_input': jax.random.normal(ks[0], (B, S, E), jnp.float32), 'K_input': jax.random.normal(ks[1], (B, S, E), jnp.float32), 'V_input': jax.random.normal(ks[2], (B, S, E), jnp.float32), 'causal_mask': jnp.where(jnp.tril(jnp.ones((S, S), bool)), 0.0, NEG).astype(jnp.float32), 'padding_mask': jnp.zeros((B, S), bool), 'W_q': xavier(ks[3], (E, E)), 'b_q': jnp.zeros((E,), jnp.float32), 'W_k': xavier(ks[4], (E, E)), 'b_k': jnp.zeros((E,), jnp.float32), 'W_v': xavier(ks[5], (E, E)), 'b_v': jnp.zeros((E,), jnp.float32), 'W_o': xavier(ks[6], (E, E)), 'b_o': jnp.zeros((E,), jnp.float32)}
        return inp
    _L1_xattn_all = _L1_xattn_setup()
    _L1_xattn_in = {k: v for k, v in _L1_xattn_all.items() if k in ('W_q', 'b_q', 'W_k', 'b_k', 'W_v', 'b_v', 'W_o', 'b_o')}
    del _L1_xattn_all

    def _L1_ffn_setup():
        import jax, jax.numpy as jnp
        import numpy as np
        D = 256
        H = 1024
        E = 12
        K = 3
        B, S = (1, 512)
        key = jax.random.key(seed)
        ks = jax.random.split(key, 6)
        scale = 0.02
        x = jax.random.normal(ks[0], (B, S, D), dtype=jnp.float32)
        Wg = jax.random.normal(ks[1], (D, E), dtype=jnp.float32) * scale
        Wup = jax.random.normal(ks[2], (E, D, H), dtype=jnp.float32) * scale
        bup = jax.random.normal(ks[3], (E, H), dtype=jnp.float32) * scale
        Wdown = jax.random.normal(ks[4], (E, H, D), dtype=jnp.float32) * scale
        bdown = jax.random.normal(ks[5], (E, D), dtype=jnp.float32) * scale
        return {'x': x, 'Wg': Wg, 'Wup': Wup, 'bup': bup, 'Wdown': Wdown, 'bdown': bdown}
    _L1_ffn_all = _L1_ffn_setup()
    _L1_ffn_in = {k: v for k, v in _L1_ffn_all.items() if k in ('Wg', 'Wup', 'bup', 'Wdown', 'bdown')}
    del _L1_ffn_all
    return {'x': x, 'ctx_1024': ctx_1024, 'mask_Bx1xS2_bk0': mask_Bx1xS2_bk0, 'mask_SxS2_fk0': mask_SxS2_fk0, 'mask_BxS2_bf0': mask_BxS2_bf0, 'g_xattn': g_xattn, 'g_ffn': g_ffn, 'L0_xattn_Wq': _L0_xattn_in['Wq'], 'L0_xattn_bq': _L0_xattn_in['bq'], 'L0_xattn_Wk': _L0_xattn_in['Wk'], 'L0_xattn_bk': _L0_xattn_in['bk'], 'L0_xattn_Wv': _L0_xattn_in['Wv'], 'L0_xattn_bv': _L0_xattn_in['bv'], 'L0_xattn_Wo': _L0_xattn_in['Wo'], 'L0_xattn_bo': _L0_xattn_in['bo'], 'L0_ffn_Wq': _L0_ffn_in['Wq'], 'L0_ffn_Wk': _L0_ffn_in['Wk'], 'L0_ffn_Wv': _L0_ffn_in['Wv'], 'L0_ffn_Ws': _L0_ffn_in['Ws'], 'L0_ffn_Wd': _L0_ffn_in['Wd'], 'L0_ffn_Wo': _L0_ffn_in['Wo'], 'L1_xattn_W_q': _L1_xattn_in['W_q'], 'L1_xattn_b_q': _L1_xattn_in['b_q'], 'L1_xattn_W_k': _L1_xattn_in['W_k'], 'L1_xattn_b_k': _L1_xattn_in['b_k'], 'L1_xattn_W_v': _L1_xattn_in['W_v'], 'L1_xattn_b_v': _L1_xattn_in['b_v'], 'L1_xattn_W_o': _L1_xattn_in['W_o'], 'L1_xattn_b_o': _L1_xattn_in['b_o'], 'L1_ffn_Wg': _L1_ffn_in['Wg'], 'L1_ffn_Wup': _L1_ffn_in['Wup'], 'L1_ffn_bup': _L1_ffn_in['bup'], 'L1_ffn_Wdown': _L1_ffn_in['Wdown'], 'L1_ffn_bdown': _L1_ffn_in['bdown']}

def reference(x, ctx_1024, mask_Bx1xS2_bk0, mask_SxS2_fk0, mask_BxS2_bf0, g_xattn, g_ffn, L0_xattn_Wq, L0_xattn_bq, L0_xattn_Wk, L0_xattn_bk, L0_xattn_Wv, L0_xattn_bv, L0_xattn_Wo, L0_xattn_bo, L0_ffn_Wq, L0_ffn_Wk, L0_ffn_Wv, L0_ffn_Ws, L0_ffn_Wd, L0_ffn_Wo, L1_xattn_W_q, L1_xattn_b_q, L1_xattn_W_k, L1_xattn_b_k, L1_xattn_W_v, L1_xattn_b_v, L1_xattn_W_o, L1_xattn_b_o, L1_ffn_Wg, L1_ffn_Wup, L1_ffn_bup, L1_ffn_Wdown, L1_ffn_bdown):
    import jax
    import jax.numpy as jnp

    def _L0_xattn_ref(query, key, value, mask, Wq, bq, Wk, bk, Wv, bv, Wo, bo):
        import jax, jax.numpy as jnp
        import numpy as np
        D_MODEL = 256
        NUM_HEADS = 16
        D_K = D_MODEL // NUM_HEADS
        SCALE = float(np.sqrt(D_K))
        B, Lq, _ = query.shape
        Lk = key.shape[1]
        Q = (query @ Wq + bq).reshape(B, Lq, NUM_HEADS, D_K).transpose(0, 2, 1, 3)
        K = (key @ Wk + bk).reshape(B, Lk, NUM_HEADS, D_K).transpose(0, 2, 1, 3)
        V = (value @ Wv + bv).reshape(B, Lk, NUM_HEADS, D_K).transpose(0, 2, 1, 3)
        scores = jnp.einsum('bhqd,bhkd->bhqk', Q, K) / SCALE
        m = mask[:, None, :, :]
        scores = jnp.where(m, -jnp.inf, scores)
        fully_masked = jnp.all(m, axis=-1, keepdims=True)
        scores = jnp.where(fully_masked, 0.0, scores)
        attn = jax.nn.softmax(scores, axis=-1)
        attn = jnp.where(fully_masked, 0.0, attn)
        out = jnp.einsum('bhqk,bhkd->bhqd', attn, V)
        out = out.transpose(0, 2, 1, 3).reshape(B, Lq, D_MODEL)
        return out @ Wo + bo

    def _L0_ffn_ref(x, Wq, Wk, Wv, Ws, Wd, Wo):
        import jax, jax.numpy as jnp
        import numpy as np
        B, T, DIM = (2, 512, 256)
        H, DH, E, K = (16, 64, 8, 2)
        scale = DH ** (-0.5)
        q = jnp.einsum('btc,hdc->bhtd', x, Wq)
        k = jnp.einsum('btc,hdc->bhtd', x, Wk)
        gate_v = jnp.einsum('btc,hec->bthe', x, Ws)
        w, sel = jax.lax.top_k(gate_v, K)
        wsig = jax.nn.sigmoid(w)
        oh = jax.nn.one_hot(sel, E, dtype=x.dtype)
        mix_v = jnp.einsum('bthk,bthke->bthe', wsig, oh)
        proj_v = jnp.einsum('btc,edc->bted', x, Wv)
        v = jnp.einsum('bthe,bted->bhtd', mix_v, proj_v)
        scores = jnp.einsum('bhid,bhjd->bhij', q * scale, k)
        probs = jax.nn.softmax(scores, axis=-1)
        attn = jnp.einsum('bhij,bhjd->bihd', probs, v)
        gate_o = jnp.einsum('btc,hec->bthe', x, Wd)
        _, sel_o = jax.lax.top_k(gate_o, K)
        mask_o = jax.nn.one_hot(sel_o, E, dtype=x.dtype).sum(axis=3)
        res = jnp.einsum('bthe,bthd,efd->bthf', mask_o, attn, Wo)
        return res.sum(axis=2)

    def _L1_xattn_ref(Q_input, K_input, V_input, causal_mask, padding_mask, W_q, b_q, W_k, b_k, W_v, b_v, W_o, b_o):
        import jax, jax.numpy as jnp
        import numpy as np
        B, S, E, H = (2, 512, 256, 16)
        D = E // H
        NEG = -1000000000.0
        b = Q_input.shape[0]

        def proj(x, W, bias):
            y = x @ W.T + bias
            return y.reshape(b, -1, H, D).transpose(0, 2, 1, 3)
        Q = proj(Q_input, W_q, b_q)
        K = proj(K_input, W_k, b_k)
        V = proj(V_input, W_v, b_v)
        scale = 1.0 / jnp.sqrt(jnp.float32(D))
        scores = jnp.einsum('bhqd,bhkd->bhqk', Q, K) * scale
        scores = jnp.where(padding_mask[:, None, None, :], NEG, scores)
        scores = scores + causal_mask
        attn = jax.nn.softmax(scores, axis=-1)
        ctx = jnp.einsum('bhqk,bhkd->bhqd', attn, V)
        ctx = ctx.transpose(0, 2, 1, 3).reshape(b, -1, E)
        return ctx @ W_o.T + b_o

    def _L1_ffn_ref(x, Wg, Wup, bup, Wdown, bdown):
        import jax, jax.numpy as jnp
        import numpy as np
        D = 256
        H = 1024
        E = 12
        K = 3
        B, S = (1, 512)
        gate_logits = jnp.einsum('bsd,de->bse', x, Wg)
        topw, sel = jax.lax.top_k(gate_logits, K)
        topw = jax.nn.softmax(topw.astype(jnp.float32), axis=-1).astype(x.dtype)
        cw = jnp.einsum('bsk,bske->bse', topw, jax.nn.one_hot(sel, E, dtype=x.dtype))
        h = jax.nn.gelu(jnp.einsum('bsd,edh->ebsh', x, Wup) + bup[:, None, None, :], approximate=False)
        y = jnp.einsum('ebsh,ehd->ebsd', h, Wdown) + bdown[:, None, None, :]
        return jnp.einsum('bse,ebsd->bsd', cw, y)
    x = x + jnp.tanh(g_xattn[0]) * _L0_xattn_ref(_layernorm(x, axis=-1), ctx_1024, ctx_1024, mask_Bx1xS2_bk0, L0_xattn_Wq, L0_xattn_bq, L0_xattn_Wk, L0_xattn_bk, L0_xattn_Wv, L0_xattn_bv, L0_xattn_Wo, L0_xattn_bo)
    x = x + jnp.tanh(g_ffn[0]) * _L0_ffn_ref(_layernorm(x, axis=-1), L0_ffn_Wq, L0_ffn_Wk, L0_ffn_Wv, L0_ffn_Ws, L0_ffn_Wd, L0_ffn_Wo)
    x = x + jnp.tanh(g_xattn[1]) * _L1_xattn_ref(_layernorm(x, axis=-1), ctx_1024, ctx_1024, mask_SxS2_fk0, mask_BxS2_bf0, L1_xattn_W_q, L1_xattn_b_q, L1_xattn_W_k, L1_xattn_b_k, L1_xattn_W_v, L1_xattn_b_v, L1_xattn_W_o, L1_xattn_b_o)
    x = x + jnp.tanh(g_ffn[1]) * _L1_ffn_ref(_layernorm(x, axis=-1), L1_ffn_Wg, L1_ffn_Wup, L1_ffn_bup, L1_ffn_Wdown, L1_ffn_bdown)
    return x

_drawn_inputs = setup_inputs


def setup_inputs(seed=0):
    import zlib

    import numpy as np

    out = dict(_drawn_inputs(seed))
    spreads = {'g_ffn': (-1.0, 0.6),
     'L0_xattn_bq': (0.0, 0.8),
     'L0_xattn_bk': (0.0, 2.0),
     'L0_xattn_bv': (0.0, 0.387),
     'L0_xattn_bo': (0.0, 0.1),
     'L1_xattn_b_q': (0.0, 0.355),
     'L1_xattn_b_k': (0.0, 2.0),
     'L1_xattn_b_v': (0.0, 0.1),
     'L1_xattn_b_o': (0.0, 0.1)}
    factors = {'L0_xattn_Wq': 8.0,
     'L0_xattn_Wk': 8.0,
     'L0_ffn_Wq': 8.0,
     'L0_ffn_Wk': 8.0,
     'L0_ffn_Wv': 3.109,
     'L0_ffn_Ws': 5.699,
     'L0_ffn_Wd': 5.109,
     'L0_ffn_Wo': 2.88,
     'L1_ffn_bup': 32.891,
     'L1_ffn_bdown': 7.813}
    for name, (base, spread) in spreads.items():
        noise = np.random.default_rng([zlib.crc32(name.encode()), seed]).standard_normal(out[name].shape)
        drawn = base * np.exp(spread * noise) if base else spread * noise
        out[name] = jnp.asarray(drawn.astype(out[name].dtype))
    for name, factor in factors.items():
        out[name] = (out[name] * factor).astype(out[name].dtype)
    return out
```

```python
from contextlib import ExitStack

import numpy as np

import concourse.bass as bass
from concourse import mybir
from concourse.alu_op_type import AluOpType as ALU

ACT = mybir.ActivationFunctionType
AX_X = mybir.AxisListType.X
F32 = mybir.dt.float32
F16 = mybir.dt.float16
I32 = mybir.dt.int32
U8 = mybir.dt.uint8

P = 128
SPLIT = 64.0
UNSPLIT = 1.0 / SPLIT ** 2
NEG = -1.0e9
MASKED = -1.0e30
EPS = 1e-5
RSQRT_SEED = float(0x5F3759DF)
NEWTON_STEPS = 3

B, SQ, D = 8, 256, 256
SK = 120
H = 16
DK = D // H
DH = 64
E0 = 8
TOP0 = 2
E1, TOP1, HID = 12, 3, 1024
TILES = B * SQ // P
TPB = SQ // P
C = D // P


class Chain:

    def __init__(self, eng, sem, per=0, turn=0):
        self.eng, self.sem, self.base, self.per, self.n = eng, sem, turn * per, per, 0

    def count(self, instruction):
        self.n += 1
        instruction.then_inc(self.sem, 1)

    def __call__(self, instruction):
        self.count(instruction)
        self.eng.wait_ge(self.sem, self.base + self.n)

    def close(self):
        assert self.n == self.per, (self.n, self.per)


def bcast(ap, n):
    return ap.unsqueeze(2).to_broadcast([ap.shape[0], ap.shape[1], n])


def bcast_mid(ap, n):
    return ap.unsqueeze(1).to_broadcast([ap.shape[0], n, ap.shape[1]])


def matmul3(pe, out, terms):
    last = None
    for n, (lhs, rhs) in enumerate(terms):
        pe.matmul(out, lhs[0], rhs[0], start=(n == 0), stop=False)
        pe.matmul(out, lhs[0], rhs[1], start=False, stop=False)
        last = pe.matmul(out, lhs[1], rhs[0], start=False, stop=(n == len(terms) - 1))
    return last


def rsqrt_all(dve, chain, s):
    chain(dve.tensor_scalar(s.var[:], s.mv[:, :, 1], EPS, None, ALU.add))
    chain(dve.tensor_scalar(s.nt[:].bitcast(I32), s.var[:].bitcast(I32), 1, None, ALU.logical_shift_right))
    chain(dve.tensor_scalar(s.rstd[:].bitcast(I32), s.nt[:].bitcast(I32), -1.0, RSQRT_SEED, ALU.mult, ALU.add))
    for _ in range(NEWTON_STEPS):
        chain(dve.tensor_tensor(s.nt[:], s.rstd[:], s.rstd[:], ALU.mult))
        chain(dve.scalar_tensor_tensor(s.nt[:], s.nt[:], -0.5, s.var[:], ALU.mult, ALU.mult))
        chain(dve.scalar_tensor_tensor(s.rstd[:], s.nt[:], 1.5, s.rstd[:], ALU.add, ALU.mult))


def choose_top(dve, chain, g, rank, k, work, hit, top, sel):
    groups, e = g.shape[1], g.shape[2]
    src = g
    for r in range(k):
        chain(dve.tensor_reduce(top[:, min(r, 1), :], src, AX_X, ALU.max))
        chain(dve.tensor_tensor(hit, src, bcast(top[:, min(r, 1), :], e), ALU.is_equal))
        chain(dve.tensor_tensor(hit, hit, bcast_mid(rank, groups), ALU.mult))
        chain(dve.tensor_reduce(top[:, 2, :], hit, AX_X, ALU.max))
        chain(dve.tensor_tensor(hit, hit, bcast(top[:, 2, :], e), ALU.is_equal))
        if r < k - 1:
            chain(dve.scalar_tensor_tensor(work, hit, MASKED, src, ALU.mult, ALU.add))
            src = work
        if r == 0:
            chain(dve.tensor_copy(sel, hit))
        else:
            chain(dve.tensor_tensor(sel, sel, hit, ALU.add))


def top_links(k):
    return 7 * k - 1


def keep_tile(dve, chain, s, tile):
    one = bass.ds(tile, 1)
    chain(dve.bn_stats(s.bn[:], s.xs[:]))
    chain.count(dve.tensor_scalar(s.x[:, one, :], s.xs[:].unsqueeze(1), 1.0, None, ALU.mult))
    chain(dve.bn_aggr(s.mvs[:], s.bn[:]))
    return dve.tensor_scalar(s.mv[:, one, :], s.mvs[:].unsqueeze(1), 1.0, None, ALU.mult)


def tile_stats(dve, chain, s, tile):
    chain(dve.bn_stats(s.bn[:], s.x[:, tile, :]))
    chain(dve.bn_aggr(s.mv[:, tile, :], s.bn[:]))


class Store:
    pass


def setup_stage(nc, a, s):
    with ExitStack() as ctx:
        sb = lambda name, shape, dt=F32: ctx.enter_context(nc.sbuf_tensor(name, shape, dt))
        sem = lambda name: ctx.enter_context(nc.semaphore(name))
        raw0 = [sb(f"raw0_{n}", [P, C, D]) for n in "qkvo"]
        raw1 = [sb(f"raw1_{n}", [P, C, D]) for n in "qkvo"]
        rawq, rawk = sb("rawq", [P, 8, D]), sb("rawk", [P, 8, D])
        rawv = sb("rawv", [P, 4, D])
        rawg = sb("rawg", [P, 2, D])
        rawo = sb("rawo", [P, C, E0, DH])
        rows = sb("bias_rows", [8, P])
        rowsu = sb("bup_rows", [E1 * 8, P])
        rawwg = sb("rawwg", [P, C, E1])
        gates = sb("gates_raw", [P, 4])
        ps = ctx.enter_context(nc.psum_tensor("setup_psum", [P, 4, 512], F32))
        x_loaded = [sem(f"x_loaded{i}") for i in range(4)]
        w_loaded = [sem(f"w_loaded{i}") for i in range(11)]
        small_loaded = sem("small_loaded")
        ones_set, ident_made, transposed, hi_made, bank_done = (
            sem("ones_set"), sem("ident_made"), sem("setup_transposed"), sem("setup_hi"), sem("setup_done"))
        dve_step, act_step, pool_step, tanh_done = (
            sem("setup_dve_step"), sem("setup_act_step"), sem("setup_pool_step"), sem("tanh_done"))
        block = ctx.enter_context(nc.Block())

        groups = []
        for n in range(4):
            groups.append(([raw1[n][:, o, c * P:(c + 1) * P] for c in range(C) for o in range(C)],
                           [s.w1[n][:, hl] for hl in range(2)], 0))
        for raw, dst, load in ((rawq, s.fq, 1), (rawk, s.fk, 2)):
            for c in range(C):
                for og in range(2):
                    groups.append(([raw[:, og * 4 + o, c * P:(c + 1) * P] for o in range(4)],
                                   [dst[:, hl, c, og * 512:(og + 1) * 512] for hl in range(2)], load))
        for c in range(C):
            groups.append(([rawv[:, o, c * P:(c + 1) * P] for o in range(4)],
                           [s.fv[:, hl, c, :] for hl in range(2)], 3))
        groups.append(([rawg[:, o, c * P:(c + 1) * P] for c in range(C) for o in range(2)],
                       [s.fg[:, hl] for hl in range(2)], 4))
        for half in range(2):
            groups.append(([rawo[:, fc, 2 * ec:2 * ec + 2, :].rearrange("p e d -> p (e d)")
                            for ec in (2 * half, 2 * half + 1) for fc in range(C)],
                           [s.fo[:, hl, 2 * half:2 * half + 2, :] for hl in range(2)], 5))
        flat = lambda ap: ap.rearrange("p a b -> p (a b)") if len(ap.shape) == 3 else ap

        @block.sync
        def _(sp):
            x = a["x"].rearrange("b (t p) d -> p (b t) d", p=P)
            n = TILES // 4
            for i in range(4):
                sp.dma_start(s.x[:, n * i:n * i + n, :], x[:, n * i:n * i + n, :]).then_inc(x_loaded[i], 16)
            for n, k in enumerate(("Wq", "Wk", "Wv", "Wo")):
                sp.dma_start(raw0[n][:], a["L0_xattn_" + k].rearrange("(c p) o -> p c o", p=P)).then_inc(w_loaded[6], 16)
            sp.dma_start(rawwg[:], a["L1_ffn_Wg"].rearrange("(c p) o -> p c o", p=P)).then_inc(w_loaded[7], 16)
            sp.wait_ge(w_loaded[6], 64)

        @block.scalar
        def _(act):
            for n, k in enumerate(("W_q", "W_k", "W_v", "W_o")):
                act.dma_start(raw1[n][:], a["L1_xattn_" + k].rearrange("(o p) i -> p o i", p=P)).then_inc(w_loaded[0], 16)
            act.dma_start(rawq[:], a["L0_ffn_Wq"].rearrange("(g h) d c -> (h d) g c", h=2)).then_inc(w_loaded[1], 16)
            act.dma_start(rawk[:], a["L0_ffn_Wk"].rearrange("(g h) d c -> (h d) g c", h=2)).then_inc(w_loaded[2], 16)
            act.dma_start(rawv[:], a["L0_ffn_Wv"].rearrange("(g h) d c -> (h d) g c", h=2)).then_inc(w_loaded[3], 16)
            act.dma_start(rawg[:, 0, :], a["L0_ffn_Ws"].rearrange("h e c -> (h e) c")).then_inc(w_loaded[4], 16)
            act.dma_start(rawg[:, 1, :], a["L0_ffn_Wd"].rearrange("h e c -> (h e) c")).then_inc(w_loaded[4], 16)
            act.dma_start(rawo[:, 0], a["L0_ffn_Wo"][:, 0:P, :].rearrange("e p d -> p e d")).then_inc(w_loaded[5], 16)
            act.dma_start(rawo[:, 1], a["L0_ffn_Wo"][:, P:2 * P, :].rearrange("e p d -> p e d")).then_inc(w_loaded[5], 16)
            act.wait_ge(small_loaded, 16 * SMALL_LOADS)
            act.activation(s.tg[:], gates[:], ACT.Tanh).then_inc(tanh_done, 1)
            act.wait_ge(w_loaded[6], 64)
            for n in range(4):
                act.activation(s.w0[n][:, 0], raw0[n][:], ACT.Copy, scale=SPLIT).then_inc(act_step, 1)
            act.wait_ge(w_loaded[7], 16)
            act.activation(s.wg[:, 0], rawwg[:], ACT.Copy, scale=SPLIT).then_inc(act_step, 1)
            for g, (_, dst, _) in enumerate(groups):
                act.wait_ge(transposed, g + 1)
                act.activation(flat(dst[0]), ps[:, g % 2, :], ACT.Copy, scale=SPLIT).then_inc(hi_made, 1)

        @block.gpsimd
        def _(pool):
            b2 = lambda k: a[k].rearrange("(m p) -> m p", p=P)
            for n, k in enumerate(("L0_xattn_bq", "L0_xattn_bk", "L1_xattn_b_q", "L1_xattn_b_k")):
                pool.dma_start(rows[2 * n:2 * n + 2, :], b2(k)).then_inc(small_loaded, 16)
            row = lambda k: a[k].rearrange("(o n) -> o n", o=1)
            for n, k in enumerate(("L0_xattn_bv", "L1_xattn_b_v")):
                pool.dma_start(s.bv[:, n, :], row(k).partition_broadcast(P)).then_inc(small_loaded, 16)
            for n, k in enumerate(("L0_xattn_bo", "L1_xattn_b_o")):
                pool.dma_start(s.bo[:, n, :], row(k).partition_broadcast(P)).then_inc(small_loaded, 16)
            pool.dma_start(gates[:, 0:2], row("g_xattn").partition_broadcast(P)).then_inc(small_loaded, 16)
            pool.dma_start(gates[:, 2:4], row("g_ffn").partition_broadcast(P)).then_inc(small_loaded, 16)
            pool.dma_start(rowsu[:], a["L1_ffn_bup"].rearrange("e (m p) -> (e m) p", p=P)).then_inc(small_loaded, 16)
            pool.dma_start(s.bdown[:], a["L1_ffn_bdown"]).then_inc(small_loaded, 16)
            pool.dma_start(s.causal[:], a["mask_SxS2_fk0"].rearrange("(t p) k -> p t k", p=P)).then_inc(small_loaded, 16)
            chain = Chain(pool, pool_step)
            chain(pool.memset(s.ident[:], 0.0))
            pool.affine_select(out=s.ident[:], in_=s.ident[:], compare_op=ALU.not_equal, fill=1.0, base=0,
                               pattern=[[-1, P]], channel_multiplier=1).then_inc(ident_made, 1)
            chain(pool.memset(s.head_of[:], 1.0))
            chain(pool.affine_select(out=s.head_of[:], in_=s.head_of[:], compare_op=ALU.is_ge, fill=0.0, base=0,
                                     pattern=[[-DK, 8]], channel_multiplier=1))
            chain(pool.affine_select(out=s.head_of[:], in_=s.head_of[:], compare_op=ALU.is_ge, fill=0.0, base=DK - 1,
                                     pattern=[[DK, 8]], channel_multiplier=-1))

        @block.tensor
        def _(pe):
            pe.wait_ge(ident_made, 1)
            for g, (src, _, load) in enumerate(groups):
                pe.wait_ge(w_loaded[load], 16 * (4, 1, 1, 1, 2, 2)[load])
                if g >= 2:
                    pe.wait_ge(bank_done, g - 1)
                for j in range(4):
                    last = pe.transpose(ps[:, g % 2, j * P:(j + 1) * P], src[j], s.ident[:])
                last.then_inc(transposed, 1)
            pe.wait_ge(small_loaded, 16 * SMALL_LOADS)
            pe.transpose(ps[:, 2, 0:8], rows[:], s.ident[0:8, 0:8])
            pe.transpose(ps[:, 2, 8:8 + E1 * 8], rowsu[:], s.ident[0:E1 * 8, 0:E1 * 8]).then_inc(transposed, 1)

        @block.vector
        def _(dve):
            chain = Chain(dve, dve_step)
            for e in range(E1):
                dve.memset(s.rank[:, e:e + 1], float(E1 - e))
            dve.memset(s.zrow[:], 0.0)
            for i in range(TILES):
                if i % 4 == 0:
                    dve.wait_ge(x_loaded[i // 4], 16)
                tile_stats(dve, chain, s, i)
            for n in range(4):
                dve.wait_ge(act_step, n + 1)
                dve.scalar_tensor_tensor(s.w0[n][:, 1], raw0[n][:], SPLIT, s.w0[n][:, 0], ALU.mult, ALU.subtract)
            dve.wait_ge(act_step, 5)
            dve.scalar_tensor_tensor(s.wg[:, 1], rawwg[:], SPLIT, s.wg[:, 0], ALU.mult, ALU.subtract)
            for g, (_, dst, _) in enumerate(groups):
                dve.wait_ge(hi_made, g + 1)
                dve.scalar_tensor_tensor(flat(dst[1]), ps[:, g % 2, :], SPLIT, flat(dst[0]),
                                         ALU.mult, ALU.subtract).then_inc(bank_done, 1)
            dve.wait_ge(transposed, len(groups) + 1)
            dve.tensor_scalar(s.bqk[:], ps[:, 2, 0:8], SPLIT, None, ALU.mult)
            dve.tensor_copy(s.bup[:], ps[:, 2, 8:8 + E1 * 8].rearrange("p (e m) -> p e m", e=E1))
            dve.wait_ge(tanh_done, 1)
            dve.tensor_scalar(s.tgu[:], s.tg[:], UNSPLIT, None, ALU.mult)
            for n in range(2):
                dve.tensor_scalar(s.bv[:, n, :], s.bv[:, n, :], SPLIT, None, ALU.mult)
                dve.tensor_scalar(s.bo[:, n, :], s.bo[:, n, :], s.tg[:, n:n + 1], None, ALU.mult)
            rsqrt_all(dve, chain, s)


SMALL_LOADS = 13


XA_FRONT = 9
XN_T, CTX_T, Q_T, K_T, V_, BACK = range(6)
XA_ACT = (XN_T, CTX_T, Q_T, K_T, BACK, BACK + 2)
XA_UNITS = 8
HG = 4


def xattn_stage(nc, a, s, layer):
    t = f"x{layer}_"
    w = (s.w0, s.w1)[layer]
    with ExitStack() as ctx:
        sb = lambda name, shape, dt=F32: ctx.enter_context(nc.sbuf_tensor(t + name, shape, dt))
        sem = lambda name: ctx.enter_context(nc.semaphore(t + name))
        two = lambda name, shape, dt=F32: [sb(f"{name}{i}", shape, dt) for i in range(2)]
        c_in = two("ctx", [SK, D])
        m_in = two("mask", [P, SK], U8)
        xn = two("xn", [P, TPB, D])
        xt = two("xt", [P, 2, C, SQ], F16)
        ct = two("ct", [P, 2, C, SK], F16)
        qf, kf = two("qf", [P, C, SQ]), two("kf", [P, C, SK])
        qt = two("qt", [P, 2, C, SQ], F16)
        ks = two("ks", [P, 2, C, SK], F16)
        km = two("km", [P, 2, C, 8, SK], F16)
        vf = two("vf", [SK, D])
        va = two("va", [SK, 2, H, DK + 1], F16)
        mf = two("mf", [P, SK])
        add = two("add", [P, TPB, SK])
        keep = two("keep", [P, SK])
        live = two("live", [P, 1])
        sc = two("sc", [P, HG, SK])
        mx = two("mx", [P, HG])
        pr = two("pr", [P, HG, SK])
        pt = two("pt", [SK, 2, HG, P], F16)
        rs = two("rs", [P, TPB, H])
        cn = two("cn", [P, TPB, D])
        cnt = two("cnt", [P, TPB, 2, C, P], F16)
        ps = ctx.enter_context(nc.psum_tensor(t + "ps", [P, 8, 512], F32))
        front = lambda par, j: ps[:, (XA_FRONT * par + j) % 2, :]
        S = lambda u: ps[:, 2 + u % 2, 0:HG * SK].rearrange("p (h k) -> p h k", h=HG)
        PT = lambda u: ps[0:SK, 4 + u % 2, :].rearrange("p (h q) -> p h q", h=HG)
        O = lambda ti: ps[:, 6 + ti, 0:H * (DK + 1)].rearrange("p (h d) -> p h d", h=H)

        loaded = [sem("loaded0"), sem("loaded1")]
        batch_free = sem("batch_free")
        xn_ready = sem("xn_ready")
        front_ready = sem("front_ready")
        act_front = sem("act_front")
        front_done = sem("front_done")
        km_ready = sem("km_ready")
        s_ready = sem("s_ready")
        s_max = sem("s_max")
        shifted = sem("shifted")
        p_ready = sem("p_ready")
        pt_ready = sem("pt_ready")
        pt_hi = sem("pt_hi")
        pt_done = sem("pt_done")
        pv_done = sem("pv_done")
        o_done = sem("o_done")
        mask_ready = sem("mask_ready")
        dve_step = sem("dve_step")
        dve_core = sem("dve_core")
        pool_step = sem("pool_step")
        block = ctx.enter_context(nc.Block())

        @block.sync
        def _(sp):
            masks = (a["mask_Bx1xS2_bk0"].rearrange("b o k -> b (o k)"), a["mask_BxS2_bf0"])[layer]
            with sp.Fori(0, B // 2) as i:
                for par in range(2):
                    b = 2 * i + par
                    sp.wait_ge(batch_free, b + 1)
                    sp.dma_start(c_in[par][:], a["ctx_1024"][bass.ds(b, 1)].rearrange("o k d -> (o k) d")).then_inc(loaded[par], 16)
                    sp.dma_start(m_in[par][:], masks[bass.ds(b, 1), :].partition_broadcast(P)).then_inc(loaded[par], 16)

        @block.gpsimd
        def _(pool):
            for par in range(2):
                pool.memset(va[par][:, 0, :, DK:DK + 1], 1.0)
                pool.memset(va[par][:, 1, :, DK:DK + 1], 0.0).then_inc(pool_step, 1)
            with pool.Fori(0, B // 2) as i:
                for par in range(2):
                    b = 2 * i + par
                    pool.wait_ge(batch_free, b + 1)
                    pool.wait_ge(front_done, 2 + XA_FRONT * b + K_T + 1)
                    for m in range(C):
                        for hl in range(2):
                            ins = pool.tensor_tensor(km[par][:, hl, m], bcast_mid(ks[par][:, hl, m, :], 8),
                                                     bcast(s.head_of[:], SK), ALU.mult)
                        ins.then_inc(km_ready, 1)
                    for u in range(XA_UNITS):
                        n = XA_UNITS * b + u
                        pool.wait_ge(s_max, 2 + n + 1)
                        pool.tensor_tensor(sc[u % 2][:], sc[u % 2][:], bcast(mx[u % 2][:], SK),
                                           ALU.subtract).then_inc(shifted, 1)

        @block.scalar
        def _(act):
            act.sem_inc(p_ready, 2)

            def hi(par, b, j, dst, src):
                act.wait_ge(front_ready, XA_FRONT * b + j + 1)
                act.activation(dst, src, ACT.Copy, scale=SPLIT).then_inc(act_front, 1)

            def biased(par, b, j, dst, n):
                act.wait_ge(front_ready, XA_FRONT * b + j + 1)
                for m in range(C):
                    src = front(par, j)[:, m * n:(m + 1) * n]
                    col = 4 * layer + (2 if j == K_T else 0) + m
                    ins = act.activation(dst[:, m, :], src, ACT.Identity, bias=s.bqk[:, col:col + 1], scale=1.0 / SPLIT)
                ins.then_inc(act_front, 1)

            def pt_part(b, u):
                act.wait_ge(pt_ready, 2 + XA_UNITS * b + u + 1)
                act.wait_ge(pv_done, XA_UNITS * b + u + 1)
                act.activation(pt[u % 2][:, 0], PT(u), ACT.Copy, scale=SPLIT).then_inc(pt_hi, 1)

            def back(par, b, ti):
                j = BACK + 2 * ti
                act.wait_ge(front_ready, XA_FRONT * b + j + 1)
                act.activation(cnt[par][:, ti, 0], front(par, j)[:, 0:D].rearrange("p (c q) -> p c q", c=C),
                               ACT.Copy).then_inc(act_front, 1)

            with act.Fori(0, B // 2) as i:
                for par in range(2):
                    b = 2 * i + par
                    act.wait_ge(batch_free, b + 1)
                    hi(par, b, XN_T, xt[par][:, 0].rearrange("p c q -> p (c q)"), front(par, XN_T))
                    hi(par, b, CTX_T, ct[par][:, 0].rearrange("p c k -> p (c k)"), front(par, CTX_T)[:, 0:C * SK])
                    biased(par, b, Q_T, qf[par], SQ)
                    biased(par, b, K_T, kf[par], SK)
                    for u in range(XA_UNITS):
                        n = XA_UNITS * b + u
                        act.wait_ge(shifted, n + 1)
                        act.wait_ge(pt_ready, n + 1)
                        act.activation(pr[u % 2][:], sc[u % 2][:], ACT.Exp).then_inc(p_ready, 1)
                        if u >= 1:
                            pt_part(b, u - 1)
                        if u == 5:
                            back(par, b, 0)
                    pt_part(b, XA_UNITS - 1)
                    back(par, b, 1)

        @block.tensor
        def _(pe):
            pe.sem_inc(pt_ready, 2)
            pe.sem_inc(pv_done, 2)

            def start(b, j):
                pe.wait_ge(front_done, XA_FRONT * b + j + 1)

            def operand(b, j):
                pe.wait_ge(front_done, 2 + XA_FRONT * b + j + 1)

            def score(par, b, u):
                pe.wait_ge(s_max, XA_UNITS * b + u + 1)
                ti, m, h0 = u // 4, (u % 4) // 2, HG * (u % 2)
                q = lambda hl: qt[par][:, hl, m, ti * P:(ti + 1) * P]
                k = lambda hl: km[par][:, hl, m, h0:h0 + HG, :]
                matmul3(pe, S(u), [((q(0), q(1)), (k(0), k(1)))]).then_inc(s_ready, 1)

            def transposes(par, b, u):
                n = XA_UNITS * b + u
                pe.wait_ge(p_ready, 2 + n + 1)
                pe.wait_ge(pt_done, n + 1)
                for h in range(HG):
                    last = pe.transpose(PT(u)[:, h, :], pr[u % 2][:, h, :], s.ident[:])
                last.then_inc(pt_ready, 1)

            def times_v(par, b, u):
                ti = u // 4
                if u % 4 == 0:
                    pe.wait_ge(o_done, TPB * b + ti + 1)
                pe.wait_ge(pt_done, 2 + XA_UNITS * b + u + 1)
                for h in range(HG):
                    head = HG * (u % 4) + h
                    last = matmul3(pe, O(ti)[:, head, :],
                                   [(tuple(pt[u % 2][:, hl, h, :] for hl in range(2)),
                                     tuple(va[par][:, hl, head, :] for hl in range(2)))])
                last.then_inc(pv_done, 1)

            def back(par, b, ti):
                j = BACK + 2 * ti
                start(b, j)
                pe.wait_ge(o_done, 2 + TPB * b + ti + 1)
                for c in range(C):
                    last = pe.transpose(front(par, j)[:, c * P:(c + 1) * P], cn[par][:, ti, c * P:(c + 1) * P], s.ident[:])
                last.then_inc(front_ready, 1)
                start(b, j + 1)
                operand(b, j)
                return matmul3(pe, front(par, j + 1)[:, 0:D],
                               [(tuple(cnt[par][:, ti, hl, c, :] for hl in range(2)),
                                 tuple(w[3][:, hl, c, :] for hl in range(2))) for c in range(C)]).then_inc(front_ready, 1)

            with pe.Fori(0, B // 2) as i:
                for par in range(2):
                    b = 2 * i + par
                    start(b, XN_T)
                    pe.wait_ge(xn_ready, b + 1)
                    for c in range(C):
                        for ti in range(TPB):
                            last = pe.transpose(front(par, XN_T)[:, c * SQ + ti * P:c * SQ + (ti + 1) * P],
                                                xn[par][:, ti, c * P:(c + 1) * P], s.ident[:])
                    last.then_inc(front_ready, 1)
                    start(b, CTX_T)
                    pe.wait_ge(loaded[par], 32 * (i + 1))
                    for c in range(C):
                        last = pe.transpose(front(par, CTX_T)[:, c * SK:(c + 1) * SK], c_in[par][:, c * P:(c + 1) * P],
                                            s.ident[0:SK, 0:SK])
                    last.then_inc(front_ready, 1)
                    pair = lambda ap, c, lo, n: tuple(ap[:, hl, c, lo:lo + n] for hl in range(2))
                    for j, wj, src, n in ((Q_T, w[0], xt[par], SQ), (K_T, w[1], ct[par], SK)):
                        start(b, j)
                        operand(b, j - 2)
                        for m in range(C):
                            last = matmul3(pe, front(par, j)[:, m * n:(m + 1) * n],
                                           [(pair(wj, c, m * P, P), pair(src, c, 0, n)) for c in range(C)])
                        last.then_inc(front_ready, 1)
                    start(b, V_)
                    matmul3(pe, front(par, V_)[0:SK, 0:D],
                            [(pair(ct[par], c, 0, SK), pair(w[2], c, 0, D)) for c in range(C)]).then_inc(front_ready, 1)
                    pe.wait_ge(km_ready, C * (b + 1))
                    score(par, b, 0)
                    score(par, b, 1)
                    for u in range(XA_UNITS):
                        transposes(par, b, u)
                        if u >= 1:
                            if u == 1:
                                operand(b, V_)
                            times_v(par, b, u - 1)
                        if u + 2 < XA_UNITS:
                            score(par, b, u + 2)
                        if u == 5:
                            back(par, b, 0)
                    times_v(par, b, XA_UNITS - 1)
                    back(par, b, 1)

        @block.vector
        def _(dve):
            dve.sem_inc(front_done, 2)
            dve.sem_inc(s_max, 2)
            dve.sem_inc(batch_free, 2)
            dve.sem_inc(pt_done, 2)
            dve.sem_inc(o_done, 2)
            for par in range(2):
                dve.memset(live[par][:], 1.0)
            chain = None

            def evacuated(ins):
                ins.then_inc(front_done, 1)

            def lo(par, b, j, dst, src, hi, scale=SPLIT):
                dve.wait_ge(act_front, len(XA_ACT) * b + XA_ACT.index(j) + 1)
                evacuated(dve.scalar_tensor_tensor(dst, src, scale, hi, ALU.mult, ALU.subtract))

            def masks(par, b):
                chain(dve.tensor_copy(mf[par][:], m_in[par][:]))
                if layer == 0:
                    chain(dve.tensor_reduce(live[par][:], mf[par][:], AX_X, ALU.min))
                    chain(dve.tensor_scalar(live[par][:], live[par][:], -1.0, 1.0, ALU.mult, ALU.add))
                    for ti in range(TPB):
                        chain(dve.tensor_scalar(add[par][:, ti, :], mf[par][:], MASKED, None, ALU.mult))
                else:
                    chain(dve.tensor_scalar(keep[par][:], mf[par][:], -1.0, 1.0, ALU.mult, ALU.add))
                    for ti in range(TPB):
                        chain(dve.scalar_tensor_tensor(add[par][:, ti, :], mf[par][:], NEG, s.causal[:, ti, :],
                                                       ALU.mult, ALU.add))

            def soft(par, b, u):
                n = XA_UNITS * b + u
                dve.wait_ge(s_ready, n + 1)
                dve.wait_ge(p_ready, n + 1)
                chain(dve.scalar_tensor_tensor(sc[u % 2][:], S(u), UNSPLIT / DK ** 0.5,
                                               bcast_mid(add[par][:, u // 4, :], HG), ALU.mult, ALU.add))
                dve.tensor_reduce(mx[u % 2][:], sc[u % 2][:], AX_X, ALU.max).then_inc(s_max, 1)

            def pt_part(b, u):
                n = XA_UNITS * b + u
                dve.wait_ge(pt_hi, n + 1)
                dve.scalar_tensor_tensor(pt[u % 2][:, 1], PT(u), SPLIT, pt[u % 2][:, 0],
                                         ALU.mult, ALU.subtract).then_inc(pt_done, 1)

            def normalise(par, b, ti):
                dve.wait_ge(pv_done, 2 + XA_UNITS * b + 4 * ti + 4)
                chain(dve.reciprocal(rs[par][:, ti, :], O(ti)[:, :, DK]))
                if layer == 0:
                    chain(dve.tensor_scalar(rs[par][:, ti, :], rs[par][:, ti, :], live[par][:], None, ALU.mult))
                dve.tensor_tensor(cn[par][:, ti, :].rearrange("p (h d) -> p h d", h=H), O(ti)[:, :, 0:DK],
                                  bcast(rs[par][:, ti, :], DK), ALU.mult).then_inc(o_done, 1)

            def back(par, b, ti):
                j = BACK + 2 * ti
                src = front(par, j)[:, 0:D].rearrange("p (c q) -> p c q", c=C)
                lo(par, b, j, cnt[par][:, ti, 1], src, cnt[par][:, ti, 0], scale=1.0)
                dve.wait_ge(front_ready, XA_FRONT * b + j + 2)
                x = s.x[:, bass.ds(TPB * b + ti, 1), :]
                y = front(par, j + 1)[:, 0:D].unsqueeze(1)
                evacuated(dve.scalar_tensor_tensor(s.xs[:].unsqueeze(1), y, s.tgu[:, layer:layer + 1], x, ALU.mult, ALU.add))
                dve.wait_ge(front_done, 2 + XA_FRONT * b + j + 2)
                chain(dve.tensor_tensor(s.xs[:], s.xs[:], s.bo[:, layer, :], ALU.add))
                return keep_tile(dve, chain, s, TPB * b + ti)

            with dve.Fori(0, B // 2) as i:
                for par in range(2):
                    b = 2 * i + par
                    chain = Chain(dve, dve_step, XA_LINKS[layer], b)
                    dve.wait_ge(batch_free, b + 1)
                    for ti in range(TPB):
                        tile = bass.ds(TPB * b + ti, 1)
                        ins = dve.tensor_scalar(xn[par][:, ti, :], s.x[:, tile, :], s.mv[:, tile, 0], s.rstd[:, tile],
                                                ALU.subtract, ALU.mult)
                    ins.then_inc(xn_ready, 1)
                    dve.wait_ge(loaded[par], 32 * (i + 1))
                    masks(par, b)
                    lo(par, b, XN_T, xt[par][:, 1].rearrange("p c q -> p (c q)"), front(par, XN_T),
                       xt[par][:, 0].rearrange("p c q -> p (c q)"))
                    lo(par, b, CTX_T, ct[par][:, 1].rearrange("p c k -> p (c k)"), front(par, CTX_T)[:, 0:C * SK],
                       ct[par][:, 0].rearrange("p c k -> p (c k)"))
                    dve.wait_ge(act_front, len(XA_ACT) * b + XA_ACT.index(Q_T) + 1)
                    chain(dve.tensor_copy(qt[par][:, 0], qf[par][:]))
                    evacuated(dve.tensor_tensor(qt[par][:, 1], qf[par][:], qt[par][:, 0], ALU.subtract))
                    dve.wait_ge(act_front, len(XA_ACT) * b + XA_ACT.index(K_T) + 1)
                    if layer == 1:
                        chain(dve.tensor_tensor(kf[par][:], kf[par][:], bcast_mid(keep[par][:], C), ALU.mult))
                    chain(dve.tensor_copy(ks[par][:, 0], kf[par][:]))
                    evacuated(dve.tensor_tensor(ks[par][:, 1], kf[par][:], ks[par][:, 0], ALU.subtract))
                    dve.wait_ge(front_ready, XA_FRONT * b + V_ + 1)
                    chain(dve.scalar_tensor_tensor(vf[par][:], front(par, V_)[0:SK, 0:D], 1.0 / SPLIT,
                                                   s.bv[0:SK, layer, :], ALU.mult, ALU.add))
                    v = vf[par][:].rearrange("k (h d) -> k h d", h=H)
                    chain(dve.tensor_copy(va[par][:, 0, :, 0:DK], v))
                    evacuated(dve.tensor_tensor(va[par][:, 1, :, 0:DK], v, va[par][:, 0, :, 0:DK], ALU.subtract))
                    for u in range(XA_UNITS):
                        soft(par, b, u)
                        if u >= 1:
                            pt_part(b, u - 1)
                        if u == 5:
                            normalise(par, b, 0)
                            chain(back(par, b, 0))
                    pt_part(b, XA_UNITS - 1)
                    normalise(par, b, 1)
                    back(par, b, 1).then_inc(batch_free, 1)
                    chain.close()
            chain = Chain(dve, dve_core)
            dve.wait_ge(batch_free, 2 + B)
            rsqrt_all(dve, chain, s)


XA_LINKS = (30, 28)



FF_FRONT = 16
F_XN, F_Q, F_K, F_GATES, F_V, F_BACK = 0, 1, 5, 9, 10, 12
FF_ACT = (F_XN, *range(F_Q, F_GATES), F_BACK, F_BACK + 2)
GATES = 2 * H


def ffn_stage(nc, a, s):
    t = "f_"
    with ExitStack() as ctx:
        sb = lambda name, shape, dt=F32: ctx.enter_context(nc.sbuf_tensor(t + name, shape, dt))
        sem = lambda name: ctx.enter_context(nc.semaphore(t + name))
        two = lambda name, shape, dt=F32: [sb(f"{name}{i}", shape, dt) for i in range(2)]
        xn = two("xn", [P, TPB, D])
        xt = two("xt", [P, 2, C, SQ], F16)
        qt = two("qt", [P, 2, H // 2, SQ], F16)
        kz = [sb(f"kz{i}", [P, 2, H, SQ], F16) for i in range(2)]
        g = sb("g", [P, TPB * GATES, E0])
        work, hit = sb("work", [P, TPB * GATES, E0]), sb("hit", [P, TPB * GATES, E0])
        sel = sb("sel", [P, TPB, 2, H, E0])
        top = sb("top", [P, 3, TPB * GATES])
        mix = sb("mix", [P, TPB, H, E0])
        pv = sb("pv", [P, TPB, E0, DH])
        tmp = two("tmp", [P, H, DH])
        vf = sb("vf", [P, H, DH])
        vh = two("vh", [P, 2, TPB, H, DH + 1], F16)
        mx, nb = two("mx", [P, TPB]), two("nb", [P, TPB])
        pr = two("pr", [P, TPB, SQ])
        pt = two("pt", [P, 2, TPB, TPB, P], F16)
        rs = two("rs", [P, 2 * TPB])
        at = sb("at", [P, TPB, H, DH])
        z = sb("z", [P, TPB, E0, DH])
        zt = two("zt", [P, TPB, 2, E0 // 2, P], F16)
        ps = ctx.enter_context(nc.psum_tensor(t + "ps", [P, 8, 512], F32))
        front = lambda j: ps[:, j % 2, :]
        S = lambda h: ps[:, 2 + h % 2, :].rearrange("p (t k) -> p t k", t=TPB)
        PT = lambda h: ps[:, 4 + h % 2, :]
        O = lambda h: ps[:, 6 + (h // 2) % 2, 0:4 * (DH + 1)].rearrange("p (h t d) -> p h t d", h=2, t=TPB)

        batch_free = sem("batch_free")
        xn_ready = sem("xn_ready")
        front_ready = sem("front_ready")
        act_front = sem("act_front")
        front_done = sem("front_done")
        gates_ready = sem("gates_ready")
        gates_exp = sem("gates_exp")
        part_ready = sem("part_ready")
        part_used = sem("part_used")
        v_sum = sem("v_sum")
        v_hi = sem("v_hi")
        v_done = sem("v_done")
        at_ready = sem("at_ready")
        z_ready = sem("z_ready")
        s_ready = sem("s_ready")
        s_max = sem("s_max")
        p_ready = sem("p_ready")
        pt_ready = sem("pt_ready")
        pt_hi = sem("pt_hi")
        pt_done = sem("pt_done")
        pv_done = sem("pv_done")
        o_done = sem("o_done")
        zeroed = sem("zeroed")
        dve_step = sem("dve_step")
        block = ctx.enter_context(nc.Block())

        @block.gpsimd
        def _(pool):
            chain = Chain(pool, zeroed)
            for par in range(2):
                chain(pool.memset(vh[par][:, 0, :, :, DH:DH + 1], 1.0))
                chain(pool.memset(vh[par][:, 1, :, :, DH:DH + 1], 0.0))
                chain(pool.memset(kz[par][:].rearrange("p l h k -> p (l h k)").bitcast(F32), 0.0))
            with pool.Fori(0, B // 2) as i:
                for par in range(2):
                    b = 2 * i + par
                    pool.wait_ge(gates_ready, 2 * b + 2)
                    pool.wait_ge(front_done, 2 + FF_FRONT * b + F_V + TPB)
                    for ti in range(TPB):
                        for e in range(E0):
                            n = ti * E0 + e
                            pool.wait_ge(part_used, PARTS * b + n + 1)
                            pool.tensor_tensor(tmp[n % 2][:], bcast_mid(pv[:, ti, e, :], H), bcast(mix[:, ti, :, e], DH),
                                               ALU.mult).then_inc(part_ready, 1)
                    pool.wait_ge(at_ready, b + 1)
                    for ti in range(TPB):
                        for e in range(E0):
                            n = (TPB + ti) * E0 + e
                            pool.wait_ge(part_used, PARTS * b + n + 1)
                            pool.tensor_tensor(tmp[n % 2][:], at[:, ti], bcast(sel[:, ti, 1, :, e], DH),
                                               ALU.mult).then_inc(part_ready, 1)

        @block.scalar
        def _(act):
            act.sem_inc(p_ready, 2)

            def arrive(b, j):
                act.wait_ge(front_ready, FF_FRONT * b + j + 1)

            def pt_part(b, h):
                act.wait_ge(pt_ready, 2 + H * b + h + 1)
                act.wait_ge(pv_done, H * b + h + 1)
                act.activation(pt[h % 2][:, 0].rearrange("p c t q -> p (c t q)"), PT(h), ACT.Copy,
                               scale=SPLIT).then_inc(pt_hi, 1)

            act.wait_ge(zeroed, 6)
            with act.Fori(0, B // 2) as i:
                for par in range(2):
                    b = 2 * i + par
                    act.wait_ge(batch_free, b + 1)
                    arrive(b, F_XN)
                    act.activation(xt[par][:, 0].rearrange("p c q -> p (c q)"), front(F_XN), ACT.Copy,
                                   scale=SPLIT).then_inc(act_front, 1)
                    for r in range(4):
                        arrive(b, F_Q + r)
                        act.activation(qt[par][:, 0, 2 * r:2 * r + 2, :].rearrange("p m q -> p (m q)"), front(F_Q + r),
                                       ACT.Copy, scale=1.0 / SPLIT).then_inc(act_front, 1)
                    for r in range(4):
                        arrive(b, F_K + r)
                        for odd in range(2):
                            rows = slice(DH * odd, DH * odd + DH)
                            ins = act.activation(kz[par][rows, 0, 4 * r + odd:4 * r + 4:2, :],
                                                 front(F_K + r)[rows, :].rearrange("p (m k) -> p m k", m=2),
                                                 ACT.Copy, scale=1.0 / SPLIT)
                        ins.then_inc(act_front, 1)
                    act.wait_ge(gates_ready, 2 * b + 1)
                    act.activation(work[:], g[:], ACT.Exp, scale=-1.0).then_inc(gates_exp, 1)
                    for ti in range(TPB):
                        act.wait_ge(v_sum, TPB * b + ti + 1)
                        act.activation(vh[par][:, 0, ti, :, 0:DH], vf[:], ACT.Copy).then_inc(v_hi, 1)
                    for h in range(H):
                        n = H * b + h
                        act.wait_ge(s_max, n + 1)
                        act.wait_ge(pt_ready, n + 1)
                        for ti in range(TPB):
                            ins = act.activation(pr[h % 2][:, ti, :], S(h)[:, ti, :], ACT.Exp, bias=nb[h % 2][:, ti:ti + 1],
                                                 scale=UNSPLIT / DH ** 0.5)
                        ins.then_inc(p_ready, 1)
                        if h >= 1:
                            pt_part(b, h - 1)
                    pt_part(b, H - 1)
                    for ti in range(TPB):
                        arrive(b, F_BACK + 2 * ti)
                        act.activation(zt[par][:, ti, 0].rearrange("p c q -> p (c q)"), front(F_BACK + 2 * ti),
                                       ACT.Copy).then_inc(act_front, 1)

        @block.tensor
        def _(pe):
            pe.sem_inc(pt_ready, 2)
            pe.sem_inc(pv_done, 2)

            def start(b, j):
                pe.wait_ge(front_done, FF_FRONT * b + j + 1)

            def operand(b, j):
                pe.wait_ge(front_done, 2 + FF_FRONT * b + j + 1)

            pair = lambda ap, c, lo, n: tuple(ap[:, hl, c, lo:lo + n] for hl in range(2))

            def score(par, b, h):
                pe.wait_ge(p_ready, H * b + h + 1)
                for ti in range(TPB):
                    last = matmul3(pe, S(h)[:, ti, :],
                                   [(pair(qt[par], h // 2, ti * P, P), pair(kz[par], h, 0, SQ))])
                last.then_inc(s_ready, 1)

            def transposes(b, h):
                n = H * b + h
                pe.wait_ge(p_ready, 2 + n + 1)
                pe.wait_ge(pt_done, n + 1)
                for c in range(TPB):
                    for ti in range(TPB):
                        at_ = (c * TPB + ti) * P
                        last = pe.transpose(PT(h)[:, at_:at_ + P], pr[h % 2][:, ti, c * P:(c + 1) * P], s.ident[:])
                last.then_inc(pt_ready, 1)

            def times_v(par, b, h):
                if h % 2 == 0:
                    pe.wait_ge(o_done, H // 2 * b + h // 2 + 1)
                pe.wait_ge(pt_done, 2 + H * b + h + 1)
                for ti in range(TPB):
                    last = matmul3(pe, O(h)[:, h % 2, ti, :],
                                   [(tuple(pt[h % 2][:, hl, c, ti, :] for hl in range(2)),
                                     tuple(vh[par][:, hl, c, h, :] for hl in range(2))) for c in range(TPB)])
                last.then_inc(pv_done, 1)

            with pe.Fori(0, B // 2) as i:
                for par in range(2):
                    b = 2 * i + par
                    start(b, F_XN)
                    pe.wait_ge(xn_ready, b + 1)
                    for c in range(C):
                        for ti in range(TPB):
                            last = pe.transpose(front(F_XN)[:, c * SQ + ti * P:c * SQ + (ti + 1) * P],
                                                xn[par][:, ti, c * P:(c + 1) * P], s.ident[:])
                    last.then_inc(front_ready, 1)
                    for first, w in ((F_Q, s.fq), (F_K, s.fk)):
                        for r in range(4):
                            start(b, first + r)
                            if r == 0:
                                operand(b, F_XN)
                            for m in range(2):
                                last = matmul3(pe, front(first + r)[:, m * SQ:(m + 1) * SQ],
                                               [(pair(w, c, (2 * r + m) * P, P), pair(xt[par], c, 0, SQ)) for c in range(C)])
                            last.then_inc(front_ready, 1)
                    start(b, F_GATES)
                    for ti in range(TPB):
                        last = matmul3(pe, front(F_GATES)[:, ti * 256:(ti + 1) * 256],
                                       [(pair(xt[par], c, ti * P, P), pair(s.fg, c, 0, 2 * H * E0)) for c in range(C)])
                    last.then_inc(front_ready, 1)
                    for ti in range(TPB):
                        start(b, F_V + ti)
                        matmul3(pe, front(F_V + ti),
                                [(pair(xt[par], c, ti * P, P), pair(s.fv, c, 0, E0 * DH)) for c in range(C)]).then_inc(front_ready, 1)
                    score(par, b, 0)
                    score(par, b, 1)
                    for h in range(H):
                        transposes(b, h)
                        if h >= 1:
                            if h == 1:
                                pe.wait_ge(v_done, TPB * (b + 1))
                            times_v(par, b, h - 1)
                        if h + 2 < H:
                            score(par, b, h + 2)
                    times_v(par, b, H - 1)
                    for ti in range(TPB):
                        j = F_BACK + 2 * ti
                        start(b, j)
                        pe.wait_ge(z_ready, TPB * b + ti + 1)
                        for ec in range(E0 // 2):
                            last = pe.transpose(front(j)[:, ec * P:(ec + 1) * P],
                                                z[:, ti, 2 * ec:2 * ec + 2, :].rearrange("p e d -> p (e d)"), s.ident[:])
                        last.then_inc(front_ready, 1)
                        start(b, j + 1)
                        operand(b, j)
                        matmul3(pe, front(j + 1)[:, 0:D],
                                [(tuple(zt[par][:, ti, hl, ec, :] for hl in range(2)),
                                  tuple(s.fo[:, hl, ec, :] for hl in range(2))) for ec in range(E0 // 2)]).then_inc(front_ready, 1)

        @block.vector
        def _(dve):
            dve.sem_inc(front_done, 2)
            dve.sem_inc(batch_free, 2)
            dve.sem_inc(part_used, 2)
            dve.sem_inc(pt_done, 2)
            dve.sem_inc(o_done, 2)
            chain = None

            def evacuated(ins):
                ins.then_inc(front_done, 1)

            def hi_made(b, j):
                dve.wait_ge(act_front, len(FF_ACT) * b + FF_ACT.index(j) + 1)

            def gate_weights(b):
                dve.wait_ge(front_ready, FF_FRONT * b + F_GATES + 1)
                evacuated(dve.tensor_scalar(g[:].rearrange("p a e -> p (a e)"), front(F_GATES), UNSPLIT, None, ALU.mult))
                dve.wait_ge(front_done, 2 + FF_FRONT * b + F_GATES + 1)
                choose_top(dve, chain, g[:], s.rank[:, E1 - E0:E1], TOP0, work[:], hit[:], top[:],
                           sel[:].rearrange("p t v h e -> p (t v h) e"))
                dve.sem_inc(gates_ready, 1)
                dve.wait_ge(gates_exp, b + 1)
                chain(dve.tensor_scalar(work[:], work[:], 1.0, None, ALU.add))
                chain(dve.reciprocal(hit[:], work[:]))
                dve.scalar_tensor_tensor(mix[:], hit[:].rearrange("p (t v h) e -> p t v h e", t=TPB, v=2)[:, :, 0],
                                         SPLIT, sel[:, :, 0], ALU.mult, ALU.mult).then_inc(gates_ready, 1)

            def mix_v(par, b):
                for ti in range(TPB):
                    if ti:
                        dve.wait_ge(v_hi, TPB * b + ti)
                    for e in range(E0):
                        n = ti * E0 + e
                        dve.wait_ge(part_ready, PARTS * b + n + 1)
                        if e == 0:
                            dve.tensor_copy(vf[:], tmp[n % 2][:]).then_inc(part_used, 1)
                        else:
                            dve.tensor_tensor(vf[:], vf[:], tmp[n % 2][:], ALU.add).then_inc(part_used, 1)
                        dve.wait_ge(part_used, 2 + PARTS * b + n + 1)
                    dve.sem_inc(v_sum, 1)
                    dve.wait_ge(v_hi, TPB * b + ti + 1)
                    dve.tensor_tensor(vh[par][:, 1, ti, :, 0:DH], vf[:], vh[par][:, 0, ti, :, 0:DH],
                                      ALU.subtract).then_inc(v_done, 1)
                    dve.wait_ge(v_done, TPB * b + ti + 1)

            def maxima(b, h):
                dve.wait_ge(s_ready, H * b + h + 1)
                dve.wait_ge(p_ready, H * b + h + 1)
                chain(dve.tensor_reduce(mx[h % 2][:], S(h), AX_X, ALU.max))
                dve.tensor_scalar(nb[h % 2][:], mx[h % 2][:], -UNSPLIT / DH ** 0.5, None, ALU.mult).then_inc(s_max, 1)

            def pt_part(b, h):
                dve.wait_ge(pt_hi, H * b + h + 1)
                dve.scalar_tensor_tensor(pt[h % 2][:, 1].rearrange("p c t q -> p (c t q)"), PT(h), SPLIT,
                                         pt[h % 2][:, 0].rearrange("p c t q -> p (c t q)"),
                                         ALU.mult, ALU.subtract).then_inc(pt_done, 1)

            def normalise(b, hp):
                h = 2 * hp
                dve.wait_ge(pv_done, 2 + H * b + h + 2)
                r = rs[hp % 2][:].rearrange("p (h t) -> p h t", h=2)
                chain(dve.reciprocal(r, O(h)[:, :, :, DH]))
                for ti in range(TPB):
                    ins = dve.tensor_tensor(at[:, ti, h:h + 2, :], O(h)[:, :, ti, 0:DH], bcast(r[:, :, ti], DH), ALU.mult)
                ins.then_inc(o_done, 1)

            with dve.Fori(0, B // 2) as i:
                for par in range(2):
                    b = 2 * i + par
                    chain = Chain(dve, dve_step, FF_LINKS, b)
                    dve.wait_ge(batch_free, b + 1)
                    for ti in range(TPB):
                        tile = bass.ds(TPB * b + ti, 1)
                        ins = dve.tensor_scalar(xn[par][:, ti, :], s.x[:, tile, :], s.mv[:, tile, 0], s.rstd[:, tile],
                                                ALU.subtract, ALU.mult)
                    ins.then_inc(xn_ready, 1)
                    hi_made(b, F_XN)
                    evacuated(dve.scalar_tensor_tensor(xt[par][:, 1].rearrange("p c q -> p (c q)"), front(F_XN), SPLIT,
                                                       xt[par][:, 0].rearrange("p c q -> p (c q)"), ALU.mult, ALU.subtract))
                    for r in range(4):
                        hi_made(b, F_Q + r)
                        m = slice(2 * r, 2 * r + 2)
                        evacuated(dve.scalar_tensor_tensor(qt[par][:, 1, m, :].rearrange("p m q -> p (m q)"), front(F_Q + r),
                                                           1.0 / SPLIT, qt[par][:, 0, m, :].rearrange("p m q -> p (m q)"),
                                                           ALU.mult, ALU.subtract))
                    for r in range(4):
                        hi_made(b, F_K + r)
                        for odd in range(2):
                            rows = slice(DH * odd, DH * odd + DH)
                            hs = slice(4 * r + odd, 4 * r + 4, 2)
                            ins = dve.scalar_tensor_tensor(kz[par][rows, 1, hs, :],
                                                           front(F_K + r)[rows, :].rearrange("p (m k) -> p m k", m=2),
                                                           1.0 / SPLIT, kz[par][rows, 0, hs, :], ALU.mult, ALU.subtract)
                        evacuated(ins)
                    gate_weights(b)
                    for ti in range(TPB):
                        dve.wait_ge(front_ready, FF_FRONT * b + F_V + ti + 1)
                        evacuated(dve.tensor_scalar(pv[:, ti].rearrange("p e d -> p (e d)"), front(F_V + ti), UNSPLIT, None, ALU.mult))
                    mix_v(par, b)
                    for h in range(H):
                        maxima(b, h)
                        if h >= 1:
                            pt_part(b, h - 1)
                        if h % 2 == 1 and h >= 3:
                            normalise(b, (h - 3) // 2)
                    pt_part(b, H - 1)
                    normalise(b, H // 2 - 1)
                    dve.wait_ge(o_done, 2 + H // 2 * (b + 1))
                    dve.sem_inc(at_ready, 1)
                    for ti in range(TPB):
                        for e in range(E0):
                            n = (TPB + ti) * E0 + e
                            dve.wait_ge(part_ready, PARTS * b + n + 1)
                            dve.tensor_reduce(z[:, ti, e, :], tmp[n % 2][:].rearrange("p h d -> p d h"), AX_X,
                                              ALU.add).then_inc(part_used, 1)
                        dve.wait_ge(part_used, 2 + PARTS * b + n + 1)
                        dve.sem_inc(z_ready, 1)
                    for ti in range(TPB):
                        j = F_BACK + 2 * ti
                        hi_made(b, j)
                        evacuated(dve.tensor_tensor(zt[par][:, ti, 1].rearrange("p c q -> p (c q)"), front(j),
                                                    zt[par][:, ti, 0].rearrange("p c q -> p (c q)"), ALU.subtract))
                        dve.wait_ge(front_ready, FF_FRONT * b + j + 2)
                        x = s.x[:, bass.ds(TPB * b + ti, 1), :]
                        evacuated(dve.scalar_tensor_tensor(s.xs[:].unsqueeze(1), front(j + 1)[:, 0:D].unsqueeze(1),
                                                           s.tgu[:, 2:3], x, ALU.mult, ALU.add))
                        dve.wait_ge(front_done, 2 + FF_FRONT * b + j + 2)
                        ins = keep_tile(dve, chain, s, TPB * b + ti)
                        if ti == 0:
                            chain(ins)
                    ins.then_inc(batch_free, 1)
                    chain.close()
            dve.wait_ge(batch_free, 2 + B)
            rsqrt_all(dve, Chain(dve, dve_step, FF_LINKS, B), s)


PARTS = 2 * TPB * E0
FF_LINKS = 46



TN = 512
CHUNKS = TILES * P // TN
TPC = TN // P
M = HID // P
RING = 4


def moe_stage(nc, a, s, out):
    t = "m_"
    with ExitStack() as ctx:
        sb = lambda name, shape, dt=F32: ctx.enter_context(nc.sbuf_tensor(t + name, shape, dt))
        sem = lambda name: ctx.enter_context(nc.semaphore(t + name))
        two = lambda name, shape, dt=F32: [sb(f"{name}{i}", shape, dt) for i in range(2)]
        uraw, draw = two("uraw", [P, C, HID]), two("draw", [P, M, D])
        us, dsp = two("us", [P, 2, C, HID], F16), two("ds", [P, 2, M, D], F16)
        xt = sb("xt", [P, 2, C, TILES * P], F16)
        hs = two("hs", [P, 2, M, TN], F16)
        cwe = two("cwe", [P, TILES])
        bue = two("bue", [P, M])
        ps = ctx.enter_context(nc.psum_tensor(t + "ps", [P, 8, 512], F32))
        cwu = sb("cwu", [P, TILES, E1])
        w_loaded = [sem(f"w_loaded{i}") for i in range(2)]
        w_split = sem("w_split")
        w_hi = sem("w_hi")
        w_free = sem("w_free")
        u_ready = sem("u_ready")
        h_gelu = sem("h_gelu")
        h_done = sem("h_done")
        h_hi = sem("h_hi")
        y_ready = sem("y_ready")
        y_done = sem("y_done")
        stored = sem("stored")
        xn_ready, tr_ready, tr_hi, tr_done = sem("xn_ready"), sem("tr_ready"), sem("tr_hi"), sem("tr_done")
        g_ready, cw_exp, cwt_ready, cwt_done, b_ready, b_done = (
            sem("g_ready"), sem("cw_exp"), sem("cwt_ready"), sem("cwt_done"), sem("b_ready"), sem("b_done"))
        dve_step = sem("dve_step")
        cw_ready, shifted = sem("cw_ready"), sem("shifted")

        def load(sp, e, par):
            sp.wait_ge(w_split, e + 1)
            sp.dma_start(uraw[par][:], a["L1_ffn_Wup"][bass.ds(e, 1)].rearrange("o (c p) h -> (o p) c h", p=P)).then_inc(w_loaded[par], 16)
            sp.dma_start(draw[par][:], a["L1_ffn_Wdown"][bass.ds(e, 1)].rearrange("o (m p) d -> (o p) m d", p=P)).then_inc(w_loaded[par], 16)

        prep = ExitStack()
        with prep:
            psb = lambda name, shape, dt=F32: prep.enter_context(nc.sbuf_tensor(t + name, shape, dt))
            xn = [psb(f"xn{i}", [P, TPB, D]) for i in range(2)]
            g, work, hit = (psb(n, [P, TILES, E1]) for n in ("g", "work", "hit"))
            sel, cw = psb("sel", [P, TILES, E1]), psb("cw", [P, TILES, E1])
            top = psb("top", [P, 3, TILES])
            cwt = psb("cwt", [E1, TILES * P])
            tr = lambda k: ps[:, k % 2, :]
            G = ps[:, 2, 0:TILES * E1].rearrange("p (t e) -> p t e", t=TILES)
            block = prep.enter_context(nc.Block())

            @block.sync
            def _(sp):
                sp.wait_ge(w_split, 2)
                for e in range(2):
                    load(sp, e, e)

            @block.scalar
            def _(act):
                for k in range(B):
                    act.wait_ge(tr_ready, k + 1)
                    act.activation(xt[:, 0, :, k * SQ:(k + 1) * SQ], tr(k).rearrange("p (c q) -> p c q", c=C),
                                   ACT.Copy, scale=SPLIT).then_inc(tr_hi, 1)
                act.wait_ge(shifted, 1)
                act.activation(work[:], work[:], ACT.Exp).then_inc(cw_exp, 1)
                for q in range(CHUNKS):
                    act.wait_ge(cwt_ready, q + 1)
                    act.activation(cwt[:, q * TN:(q + 1) * TN], ps[0:E1, 4 + q, :], ACT.Copy).then_inc(cwt_done, 1)

            @block.tensor
            def _(pe):
                def gate(k):
                    pe.wait_ge(tr_done, k + 1)
                    for ti in range(TPB):
                        tile = TPB * k + ti
                        last = matmul3(pe, G[:, tile, :],
                                       [(tuple(xt[:, hl, c, tile * P:(tile + 1) * P] for hl in range(2)),
                                         tuple(s.wg[:, hl, c, :] for hl in range(2))) for c in range(C)])
                    return last

                for k in range(B):
                    pe.wait_ge(xn_ready, k + 1)
                    if k >= 2:
                        pe.wait_ge(tr_done, k - 1)
                    for c in range(C):
                        for ti in range(TPB):
                            last = pe.transpose(tr(k)[:, c * SQ + ti * P:c * SQ + (ti + 1) * P],
                                                xn[k % 2][:, ti, c * P:(c + 1) * P], s.ident[:])
                    last.then_inc(tr_ready, 1)
                    if k >= 1:
                        gate(k - 1)
                gate(B - 1).then_inc(g_ready, 1)
                pe.wait_ge(cw_ready, 1)
                for q in range(CHUNKS):
                    for ti in range(TPC):
                        last = pe.transpose(ps[0:E1, 4 + q, ti * P:(ti + 1) * P], cw[:, TPC * q + ti, :], s.ident[:])
                    last.then_inc(cwt_ready, 1)
                for tile in range(TILES):
                    if tile % TPC == 0:
                        pe.wait_ge(cwt_done, tile // TPC + 1)
                    if tile >= 2:
                        pe.wait_ge(b_done, tile - 1)
                    pe.matmul(ps[:, 2 + tile % 2, 0:D], cwt[:, tile * P:(tile + 1) * P], s.bdown[:],
                              start=True, stop=True).then_inc(b_ready, 1)

            def lo_part(dve, k):
                dve.wait_ge(tr_hi, k + 1)
                dve.scalar_tensor_tensor(xt[:, 1, :, k * SQ:(k + 1) * SQ], tr(k).rearrange("p (c q) -> p c q", c=C),
                                         SPLIT, xt[:, 0, :, k * SQ:(k + 1) * SQ], ALU.mult, ALU.subtract).then_inc(tr_done, 1)

            @block.vector
            def _(dve):
                dve.sem_inc(w_split, 2)
                chain = Chain(dve, dve_step)
                for k in range(B):
                    if k >= 2:
                        dve.wait_ge(tr_ready, k - 1)
                    for ti in range(TPB):
                        tile = TPB * k + ti
                        ins = dve.tensor_scalar(xn[k % 2][:, ti, :], s.x[:, tile, :], s.mv[:, tile, 0:1],
                                                s.rstd[:, tile:tile + 1], ALU.subtract, ALU.mult)
                    ins.then_inc(xn_ready, 1)
                    if k >= 1:
                        lo_part(dve, k - 1)
                lo_part(dve, B - 1)
                dve.wait_ge(g_ready, 1)
                chain(dve.tensor_scalar(g[:], G, UNSPLIT, None, ALU.mult))
                choose_top(dve, chain, g[:], s.rank[:], TOP1, work[:], hit[:], top[:], sel[:])
                dve.tensor_tensor(work[:], g[:], bcast(top[:, 0, :], E1), ALU.subtract).then_inc(shifted, 1)
                dve.wait_ge(cw_exp, 1)
                chain(dve.tensor_tensor(cw[:], work[:], sel[:], ALU.mult))
                chain(dve.tensor_reduce(top[:, 1, :], cw[:], AX_X, ALU.add))
                chain(dve.reciprocal(top[:, 2, :], top[:, 1, :]))
                chain(dve.tensor_scalar(top[:, 2, :], top[:, 2, :], s.tg[:, 3:4], None, ALU.mult))
                dve.tensor_tensor(cw[:], cw[:], bcast(top[:, 2, :], E1), ALU.mult).then_inc(cw_ready, 1)
                dve.wait_ge(cw_ready, 1)
                chain(dve.tensor_scalar(cwu[:], cw[:], UNSPLIT, None, ALU.mult))
                for tile in range(TILES):
                    dve.wait_ge(b_ready, tile + 1)
                    dve.tensor_tensor(s.x[:, tile, :], s.x[:, tile, :], ps[:, 2 + tile % 2, 0:D], ALU.add).then_inc(b_done, 1)
                dve.wait_ge(b_done, TILES)

        hf = [sb(f"hf{i}", [P, TN]) for i in range(RING)]
        block = ctx.enter_context(nc.Block())
        U = lambda m: ps[:, m % RING, :]
        Y = lambda ti: ps[:, RING + ti % RING, 0:D]

        @block.sync
        def _(sp):
            with sp.Fori(1, E1 // 2) as i:
                for par in range(2):
                    load(sp, 2 * i + par, par)
            for c in range(CHUNKS):
                sp.wait_ge(y_done, RING + ((E1 - 1) * CHUNKS + c + 1) * TPC)
                sp.dma_start(out.rearrange("b (t p) d -> p (b t) d", p=P)[:, TPC * c:TPC * (c + 1), :],
                             s.x[:, TPC * c:TPC * (c + 1), :]).then_inc(stored, 16)
            sp.wait_ge(stored, 16 * CHUNKS)

        @block.scalar
        def _(act):
            act.sem_inc(h_gelu, RING)

            def split(e, par, turn):
                act.wait_ge(w_loaded[par], 32 * (turn + 1))
                act.wait_ge(w_free, e + 1)
                act.activation(us[par][:, 0], uraw[par][:], ACT.Copy, scale=SPLIT)
                act.activation(dsp[par][:, 0], draw[par][:], ACT.Copy, scale=SPLIT).then_inc(w_hi, 1)

            def expert(e, par, turn, last=False):
                for c in range(CHUNKS):
                    for m in range(M):
                        n = (e * CHUNKS + c) * M + m
                        act.wait_ge(u_ready, n + 1)
                        act.wait_ge(h_done, n + 1)
                        act.activation(hf[m % RING][:], U(m), ACT.Gelu, bias=bue[par][:, m:m + 1],
                                       scale=UNSPLIT).then_inc(h_gelu, 1)
                    if c == 1 and not last:
                        split(e + 1, 1 - par, turn + par)

            split(0, 0, 0)
            act.wait_ge(w_split, 2 + 1)
            with act.Fori(0, E1 // 2 - 1) as i:
                for par in range(2):
                    expert(2 * i + par, par, i)
            expert(E1 - 2, 0, E1 // 2 - 1)
            expert(E1 - 1, 1, E1 // 2 - 1, last=True)

        @block.tensor
        def _(pe):
            def up(e, par, c):
                for m in range(M):
                    n = (e * CHUNKS + c) * M + m
                    pe.wait_ge(h_gelu, n + 1)
                    matmul3(pe, U(m),
                            [(tuple(us[par][:, hl, k, m * P:(m + 1) * P] for hl in range(2)),
                              tuple(xt[:, hl, k, c * TN:(c + 1) * TN] for hl in range(2))) for k in range(C)]).then_inc(u_ready, 1)

            def down(e, par, c):
                pe.wait_ge(h_done, RING + (e * CHUNKS + c + 1) * M)
                for ti in range(TPC):
                    n = (e * CHUNKS + c) * TPC + ti
                    pe.wait_ge(y_done, n + 1)
                    matmul3(pe, Y(ti),
                            [(tuple(hs[c % 2][:, hl, m, ti * P:(ti + 1) * P] for hl in range(2)),
                              tuple(dsp[par][:, hl, m, :] for hl in range(2))) for m in range(M)]).then_inc(y_ready, 1)

            def expert(e, par, last=False):
                for c in range(CHUNKS):
                    if c + 1 < CHUNKS:
                        up(e, par, c + 1)
                    elif not last:
                        pe.wait_ge(w_split, 2 + e + 2)
                        up(e + 1, 1 - par, 0)
                    down(e, par, c)

            pe.wait_ge(w_split, 2 + 1)
            up(0, 0, 0)
            with pe.Fori(0, E1 // 2 - 1) as i:
                for par in range(2):
                    expert(2 * i + par, par)
            expert(E1 - 2, 0)
            expert(E1 - 1, 1, last=True)

        @block.vector
        def _(dve):
            dve.sem_inc(w_free, 2)
            dve.sem_inc(h_done, RING)
            dve.sem_inc(y_done, RING)

            def split(e, par):
                dve.wait_ge(w_hi, e + 1)
                one = slice(e, e + 1) if isinstance(e, int) else bass.ds(e, 1)
                dve.tensor_copy(cwe[par][:].unsqueeze(2), cwu[:, :, one])
                dve.tensor_copy(bue[par][:].unsqueeze(1), s.bup[:, one, :])
                dve.scalar_tensor_tensor(us[par][:, 1], uraw[par][:], SPLIT, us[par][:, 0], ALU.mult, ALU.subtract)
                dve.scalar_tensor_tensor(dsp[par][:, 1], draw[par][:], SPLIT, dsp[par][:, 0],
                                         ALU.mult, ALU.subtract).then_inc(w_split, 1)
                dve.wait_ge(w_split, 2 + e + 1)

            def hidden(e, c, m):
                n = (e * CHUNKS + c) * M + m
                dve.wait_ge(h_gelu, RING + n + 1)
                dve.tensor_scalar(hs[c % 2][:, 0, m, :], hf[m % RING][:], SPLIT, None, ALU.mult).then_inc(h_hi, 1)
                dve.wait_ge(h_hi, n + 1)
                dve.scalar_tensor_tensor(hs[c % 2][:, 1, m, :], hf[m % RING][:], SPLIT, hs[c % 2][:, 0, m, :],
                                         ALU.mult, ALU.subtract).then_inc(h_done, 1)

            def add(e, par, c):
                for ti in range(TPC):
                    n = (e * CHUNKS + c) * TPC + ti
                    tile = TPC * c + ti
                    dve.wait_ge(y_ready, n + 1)
                    dve.wait_ge(y_done, n + 1)
                    ins = dve.scalar_tensor_tensor(s.x[:, tile, :], Y(ti), cwe[par][:, tile:tile + 1], s.x[:, tile, :],
                                                   ALU.mult, ALU.add)
                    ins.then_inc(y_done, 1)

            def expert(e, par, last=False):
                for c in range(CHUNKS):
                    if c + 1 < CHUNKS:
                        for m in range(M):
                            hidden(e, c + 1, m)
                    elif not last:
                        for m in range(M):
                            hidden(e + 1, 0, m)
                    add(e, par, c)
                    if c == 1 and not last:
                        split(e + 1, 1 - par)
                dve.wait_ge(y_done, RING + (e + 1) * TILES)
                dve.sem_inc(w_free, 1)

            split(0, 0)
            for m in range(M):
                hidden(0, 0, m)
            with dve.Fori(0, E1 // 2 - 1) as i:
                for par in range(2):
                    expert(2 * i + par, par)
            expert(E1 - 2, 0)
            expert(E1 - 1, 1, last=True)

OUTPUTS = {"out": ((B, SQ, D), F32)}


def build(nc, a, out):
    s = Store()
    with ExitStack() as ctx:
        sb = lambda name, shape, dt=F32: ctx.enter_context(nc.sbuf_tensor(name, shape, dt))
        s.x = sb("x", [P, TILES, D])
        s.w0 = [sb(f"w0_{n}", [P, 2, C, D], F16) for n in "qkvo"]
        s.w1 = [sb(f"w1_{n}", [P, 2, C, D], F16) for n in "qkvo"]
        s.fq, s.fk = sb("fq", [P, 2, C, H * DH], F16), sb("fk", [P, 2, C, H * DH], F16)
        s.fv = sb("fv", [P, 2, C, E0 * DH], F16)
        s.fg = sb("fg", [P, 2, C, 2 * H * E0], F16)
        s.fo = sb("fo", [P, 2, E0 // 2, D], F16)
        s.wg = sb("wg", [P, 2, C, E1], F16)
        s.ident = sb("ident", [P, P])
        s.head_of = sb("head_of", [P, 8], F16)
        s.rank = sb("rank", [P, E1])
        s.zrow = sb("zrow", [P, 1])
        s.bqk = sb("bqk", [P, 8])
        s.bup = sb("bup", [P, E1, HID // P])
        s.bv, s.bo = sb("bv", [P, 2, D]), sb("bo", [P, 2, D])
        s.bdown = sb("bdown", [E1, D])
        s.causal = sb("causal", [P, TPB, SK])
        s.tg, s.tgu = sb("tg", [P, 4]), sb("tgu", [P, 4])
        s.mv, s.mvs, s.bn = sb("mv", [P, TILES, 2]), sb("mvs", [P, 2]), sb("bn", [P, 6])
        s.xs = sb("xs", [P, D])
        s.var, s.nt, s.rstd = sb("var", [P, TILES]), sb("nt", [P, TILES]), sb("rstd", [P, TILES])
        setup_stage(nc, a, s)
        for stage in STAGES:
            if stage in (0, 1):
                xattn_stage(nc, a, s, stage)
            elif stage == "ffn":
                ffn_stage(nc, a, s)
            elif stage == "moe":
                moe_stage(nc, a, s, out)
            else:
                store_stage(nc, a, s, out)


def store_stage(nc, a, s, out):
    with ExitStack() as ctx:
        done = ctx.enter_context(nc.semaphore("out_stored"))
        block = ctx.enter_context(nc.Block())

        @block.sync
        def _(sp):
            sp.dma_start(out.rearrange("b (t p) d -> p (b t) d", p=P), s.x[:]).then_inc(done, 16)
            sp.wait_ge(done, 16)


STAGES = (0, "ffn", 1, "moe")

_INS = ['x', 'ctx_1024', 'mask_Bx1xS2_bk0', 'mask_SxS2_fk0', 'mask_BxS2_bf0', 'g_xattn', 'g_ffn',
        'L0_xattn_Wq', 'L0_xattn_bq', 'L0_xattn_Wk', 'L0_xattn_bk', 'L0_xattn_Wv', 'L0_xattn_bv',
        'L0_xattn_Wo', 'L0_xattn_bo', 'L0_ffn_Wq', 'L0_ffn_Wk', 'L0_ffn_Wv', 'L0_ffn_Ws', 'L0_ffn_Wd',
        'L0_ffn_Wo', 'L1_xattn_W_q', 'L1_xattn_b_q', 'L1_xattn_W_k', 'L1_xattn_b_k', 'L1_xattn_W_v',
        'L1_xattn_b_v', 'L1_xattn_W_o', 'L1_xattn_b_o', 'L1_ffn_Wg', 'L1_ffn_Wup', 'L1_ffn_bup',
        'L1_ffn_Wdown', 'L1_ffn_bdown']


def kernel(**inputs):
    import numpy as _np
    import concourse.bacc as _bacc
    from concourse import mybir as _mybir
    from concourse.bass_utils import run_bass_kernel_spmd as _run

    nc = _bacc.Bacc("TRN2", target_bir_lowering=False, num_devices=1)
    arrays, drams = {}, {}
    for name in _INS:
        v = _np.ascontiguousarray(inputs[name])
        arrays[f"in_{name}"] = v
        drams[name] = nc.dram_tensor(f"in_{name}", v.shape, _mybir.dt.from_np(v.dtype), kind="ExternalInput").ap()
    out = nc.dram_tensor("out_0", (B, SQ, D), F32, kind="ExternalOutput").ap()
    build(nc, drams, out)
    r = _run(nc, [arrays], core_ids=[0])
    return r.results[0]["out_0"]
```

```python
from contextlib import ExitStack

import numpy as np

import concourse.bass as bass
from concourse import mybir
from concourse.alu_op_type import AluOpType as ALU

ACT = mybir.ActivationFunctionType
AX_X = mybir.AxisListType.X
F32 = mybir.dt.float32
F16 = mybir.dt.float16
I32 = mybir.dt.int32
U8 = mybir.dt.uint8

P = 128
SPLIT = 64.0
UNSPLIT = 1.0 / SPLIT ** 2
NEG = -1.0e9
MASKED = -1.0e30
EPS = 1e-5
RSQRT_SEED = float(0x5F3759DF)
NEWTON_STEPS = 3

B, SQ, D = 8, 256, 256
SK = 120
H = 16
DK = D // H
DH = 64
E0 = 8
TOP0 = 2
E1, TOP1, HID = 12, 3, 1024
TILES = B * SQ // P
TPB = SQ // P
C = D // P


class Chain:

    def __init__(self, eng, sem, per=0, turn=0):
        self.eng, self.sem, self.base, self.per, self.n = eng, sem, turn * per, per, 0

    def count(self, instruction):
        self.n += 1
        instruction.then_inc(self.sem, 1)

    def __call__(self, instruction):
        self.count(instruction)
        self.eng.wait_ge(self.sem, self.base + self.n)

    def close(self):
        assert self.n == self.per, (self.n, self.per)


def bcast(ap, n):
    return ap.unsqueeze(2).to_broadcast([ap.shape[0], ap.shape[1], n])


def bcast_mid(ap, n):
    return ap.unsqueeze(1).to_broadcast([ap.shape[0], n, ap.shape[1]])


def matmul3(pe, out, terms):
    last = None
    for n, (lhs, rhs) in enumerate(terms):
        pe.matmul(out, lhs[0], rhs[0], start=(n == 0), stop=False)
        pe.matmul(out, lhs[0], rhs[1], start=False, stop=False)
        last = pe.matmul(out, lhs[1], rhs[0], start=False, stop=(n == len(terms) - 1))
    return last


def rsqrt_all(dve, chain, s):
    chain(dve.tensor_scalar(s.var[:], s.mv[:, :, 1], EPS, None, ALU.add))
    chain(dve.tensor_scalar(s.nt[:].bitcast(I32), s.var[:].bitcast(I32), 1, None, ALU.logical_shift_right))
    chain(dve.tensor_scalar(s.rstd[:].bitcast(I32), s.nt[:].bitcast(I32), -1.0, RSQRT_SEED, ALU.mult, ALU.add))
    for _ in range(NEWTON_STEPS):
        chain(dve.tensor_tensor(s.nt[:], s.rstd[:], s.rstd[:], ALU.mult))
        chain(dve.scalar_tensor_tensor(s.nt[:], s.nt[:], -0.5, s.var[:], ALU.mult, ALU.mult))
        chain(dve.scalar_tensor_tensor(s.rstd[:], s.nt[:], 1.5, s.rstd[:], ALU.add, ALU.mult))


def choose_top(dve, chain, g, rank, k, work, hit, top, sel):
    groups, e = g.shape[1], g.shape[2]
    src = g
    for r in range(k):
        chain(dve.tensor_reduce(top[:, min(r, 1), :], src, AX_X, ALU.max))
        chain(dve.tensor_tensor(hit, src, bcast(top[:, min(r, 1), :], e), ALU.is_equal))
        chain(dve.tensor_tensor(hit, hit, bcast_mid(rank, groups), ALU.mult))
        chain(dve.tensor_reduce(top[:, 2, :], hit, AX_X, ALU.max))
        chain(dve.tensor_tensor(hit, hit, bcast(top[:, 2, :], e), ALU.is_equal))
        if r < k - 1:
            chain(dve.scalar_tensor_tensor(work, hit, MASKED, src, ALU.mult, ALU.add))
            src = work
        if r == 0:
            chain(dve.tensor_copy(sel, hit))
        else:
            chain(dve.tensor_tensor(sel, sel, hit, ALU.add))


def top_links(k):
    return 7 * k - 1


def keep_tile(dve, chain, s, tile):
    one = bass.ds(tile, 1)
    chain(dve.bn_stats(s.bn[:], s.xs[:]))
    chain.count(dve.tensor_scalar(s.x[:, one, :], s.xs[:].unsqueeze(1), 1.0, None, ALU.mult))
    chain(dve.bn_aggr(s.mvs[:], s.bn[:]))
    return dve.tensor_scalar(s.mv[:, one, :], s.mvs[:].unsqueeze(1), 1.0, None, ALU.mult)


def tile_stats(dve, chain, s, tile):
    chain(dve.bn_stats(s.bn[:], s.x[:, tile, :]))
    chain(dve.bn_aggr(s.mv[:, tile, :], s.bn[:]))


class Store:
    pass


def setup_stage(nc, a, s):
    with ExitStack() as ctx:
        sb = lambda name, shape, dt=F32: ctx.enter_context(nc.sbuf_tensor(name, shape, dt))
        sem = lambda name: ctx.enter_context(nc.semaphore(name))
        raw0 = [sb(f"raw0_{n}", [P, C, D]) for n in "qkvo"]
        raw1 = [sb(f"raw1_{n}", [P, C, D]) for n in "qkvo"]
        rawq, rawk = sb("rawq", [P, 8, D]), sb("rawk", [P, 8, D])
        rawv = sb("rawv", [P, 4, D])
        rawg = sb("rawg", [P, 2, D])
        rawo = sb("rawo", [P, C, E0, DH])
        rows = sb("bias_rows", [8, P])
        rowsu = sb("bup_rows", [E1 * 8, P])
        rawwg = sb("rawwg", [P, C, E1])
        gates = sb("gates_raw", [P, 4])
        ps = ctx.enter_context(nc.psum_tensor("setup_psum", [P, 4, 512], F32))
        x_loaded = [sem(f"x_loaded{i}") for i in range(4)]
        w_loaded = [sem(f"w_loaded{i}") for i in range(11)]
        small_loaded = sem("small_loaded")
        ones_set, ident_made, transposed, hi_made, bank_done = (
            sem("ones_set"), sem("ident_made"), sem("setup_transposed"), sem("setup_hi"), sem("setup_done"))
        dve_step, act_step, pool_step, tanh_done = (
            sem("setup_dve_step"), sem("setup_act_step"), sem("setup_pool_step"), sem("tanh_done"))
        block = ctx.enter_context(nc.Block())

        groups = []
        for n in range(4):
            groups.append(([raw1[n][:, o, c * P:(c + 1) * P] for c in range(C) for o in range(C)],
                           [s.w1[n][:, hl] for hl in range(2)], 0))
        for raw, dst, load in ((rawq, s.fq, 1), (rawk, s.fk, 2)):
            for c in range(C):
                for og in range(2):
                    groups.append(([raw[:, og * 4 + o, c * P:(c + 1) * P] for o in range(4)],
                                   [dst[:, hl, c, og * 512:(og + 1) * 512] for hl in range(2)], load))
        for c in range(C):
            groups.append(([rawv[:, o, c * P:(c + 1) * P] for o in range(4)],
                           [s.fv[:, hl, c, :] for hl in range(2)], 3))
        groups.append(([rawg[:, o, c * P:(c + 1) * P] for c in range(C) for o in range(2)],
                       [s.fg[:, hl] for hl in range(2)], 4))
        for half in range(2):
            groups.append(([rawo[:, fc, 2 * ec:2 * ec + 2, :].rearrange("p e d -> p (e d)")
                            for ec in (2 * half, 2 * half + 1) for fc in range(C)],
                           [s.fo[:, hl, 2 * half:2 * half + 2, :] for hl in range(2)], 5))
        flat = lambda ap: ap.rearrange("p a b -> p (a b)") if len(ap.shape) == 3 else ap

        @block.sync
        def _(sp):
            x = a["x"].rearrange("b (t p) d -> p (b t) d", p=P)
            n = TILES // 4
            for i in range(4):
                sp.dma_start(s.x[:, n * i:n * i + n, :], x[:, n * i:n * i + n, :]).then_inc(x_loaded[i], 16)
            for n, k in enumerate(("Wq", "Wk", "Wv", "Wo")):
                sp.dma_start(raw0[n][:], a["L0_xattn_" + k].rearrange("(c p) o -> p c o", p=P)).then_inc(w_loaded[6], 16)
            sp.dma_start(rawwg[:], a["L1_ffn_Wg"].rearrange("(c p) o -> p c o", p=P)).then_inc(w_loaded[7], 16)
            sp.wait_ge(w_loaded[6], 64)

        @block.scalar
        def _(act):
            for n, k in enumerate(("W_q", "W_k", "W_v", "W_o")):
                act.dma_start(raw1[n][:], a["L1_xattn_" + k].rearrange("(o p) i -> p o i", p=P)).then_inc(w_loaded[0], 16)
            act.dma_start(rawq[:], a["L0_ffn_Wq"].rearrange("(g h) d c -> (h d) g c", h=2)).then_inc(w_loaded[1], 16)
            act.dma_start(rawk[:], a["L0_ffn_Wk"].rearrange("(g h) d c -> (h d) g c", h=2)).then_inc(w_loaded[2], 16)
            act.dma_start(rawv[:], a["L0_ffn_Wv"].rearrange("(g h) d c -> (h d) g c", h=2)).then_inc(w_loaded[3], 16)
            act.dma_start(rawg[:, 0, :], a["L0_ffn_Ws"].rearrange("h e c -> (h e) c")).then_inc(w_loaded[4], 16)
            act.dma_start(rawg[:, 1, :], a["L0_ffn_Wd"].rearrange("h e c -> (h e) c")).then_inc(w_loaded[4], 16)
            act.dma_start(rawo[:, 0], a["L0_ffn_Wo"][:, 0:P, :].rearrange("e p d -> p e d")).then_inc(w_loaded[5], 16)
            act.dma_start(rawo[:, 1], a["L0_ffn_Wo"][:, P:2 * P, :].rearrange("e p d -> p e d")).then_inc(w_loaded[5], 16)
            act.wait_ge(small_loaded, 16 * SMALL_LOADS)
            act.activation(s.tg[:], gates[:], ACT.Tanh).then_inc(tanh_done, 1)
            act.wait_ge(w_loaded[6], 64)
            for n in range(4):
                act.activation(s.w0[n][:, 0], raw0[n][:], ACT.Copy, scale=SPLIT).then_inc(act_step, 1)
            act.wait_ge(w_loaded[7], 16)
            act.activation(s.wg[:, 0], rawwg[:], ACT.Copy, scale=SPLIT).then_inc(act_step, 1)
            for g, (_, dst, _) in enumerate(groups):
                act.wait_ge(transposed, g + 1)
                act.activation(flat(dst[0]), ps[:, g % 2, :], ACT.Copy, scale=SPLIT).then_inc(hi_made, 1)

        @block.gpsimd
        def _(pool):
            b2 = lambda k: a[k].rearrange("(m p) -> m p", p=P)
            for n, k in enumerate(("L0_xattn_bq", "L0_xattn_bk", "L1_xattn_b_q", "L1_xattn_b_k")):
                pool.dma_start(rows[2 * n:2 * n + 2, :], b2(k)).then_inc(small_loaded, 16)
            row = lambda k: a[k].rearrange("(o n) -> o n", o=1)
            for n, k in enumerate(("L0_xattn_bv", "L1_xattn_b_v")):
                pool.dma_start(s.bv[:, n, :], row(k).partition_broadcast(P)).then_inc(small_loaded, 16)
            for n, k in enumerate(("L0_xattn_bo", "L1_xattn_b_o")):
                pool.dma_start(s.bo[:, n, :], row(k).partition_broadcast(P)).then_inc(small_loaded, 16)
            pool.dma_start(gates[:, 0:2], row("g_xattn").partition_broadcast(P)).then_inc(small_loaded, 16)
            pool.dma_start(gates[:, 2:4], row("g_ffn").partition_broadcast(P)).then_inc(small_loaded, 16)
            pool.dma_start(rowsu[:], a["L1_ffn_bup"].rearrange("e (m p) -> (e m) p", p=P)).then_inc(small_loaded, 16)
            pool.dma_start(s.bdown[:], a["L1_ffn_bdown"]).then_inc(small_loaded, 16)
            pool.dma_start(s.causal[:], a["mask_SxS2_fk0"].rearrange("(t p) k -> p t k", p=P)).then_inc(small_loaded, 16)
            chain = Chain(pool, pool_step)
            chain(pool.memset(s.ident[:], 0.0))
            pool.affine_select(out=s.ident[:], in_=s.ident[:], compare_op=ALU.not_equal, fill=1.0, base=0,
                               pattern=[[-1, P]], channel_multiplier=1).then_inc(ident_made, 1)
            chain(pool.memset(s.head_of[:], 1.0))
            chain(pool.affine_select(out=s.head_of[:], in_=s.head_of[:], compare_op=ALU.is_ge, fill=0.0, base=0,
                                     pattern=[[-DK, 8]], channel_multiplier=1))
            chain(pool.affine_select(out=s.head_of[:], in_=s.head_of[:], compare_op=ALU.is_ge, fill=0.0, base=DK - 1,
                                     pattern=[[DK, 8]], channel_multiplier=-1))

        @block.tensor
        def _(pe):
            pe.wait_ge(ident_made, 1)
            for g, (src, _, load) in enumerate(groups):
                pe.wait_ge(w_loaded[load], 16 * (4, 1, 1, 1, 2, 2)[load])
                if g >= 2:
                    pe.wait_ge(bank_done, g - 1)
                for j in range(4):
                    last = pe.transpose(ps[:, g % 2, j * P:(j + 1) * P], src[j], s.ident[:])
                last.then_inc(transposed, 1)
            pe.wait_ge(small_loaded, 16 * SMALL_LOADS)
            pe.transpose(ps[:, 2, 0:8], rows[:], s.ident[0:8, 0:8])
            pe.transpose(ps[:, 2, 8:8 + E1 * 8], rowsu[:], s.ident[0:E1 * 8, 0:E1 * 8]).then_inc(transposed, 1)

        @block.vector
        def _(dve):
            chain = Chain(dve, dve_step)
            for e in range(E1):
                dve.memset(s.rank[:, e:e + 1], float(E1 - e))
            dve.memset(s.zrow[:], 0.0)
            for i in range(TILES):
                if i % 4 == 0:
                    dve.wait_ge(x_loaded[i // 4], 16)
                tile_stats(dve, chain, s, i)
            for n in range(4):
                dve.wait_ge(act_step, n + 1)
                dve.scalar_tensor_tensor(s.w0[n][:, 1], raw0[n][:], SPLIT, s.w0[n][:, 0], ALU.mult, ALU.subtract)
            dve.wait_ge(act_step, 5)
            dve.scalar_tensor_tensor(s.wg[:, 1], rawwg[:], SPLIT, s.wg[:, 0], ALU.mult, ALU.subtract)
            for g, (_, dst, _) in enumerate(groups):
                dve.wait_ge(hi_made, g + 1)
                dve.scalar_tensor_tensor(flat(dst[1]), ps[:, g % 2, :], SPLIT, flat(dst[0]),
                                         ALU.mult, ALU.subtract).then_inc(bank_done, 1)
            dve.wait_ge(transposed, len(groups) + 1)
            dve.tensor_scalar(s.bqk[:], ps[:, 2, 0:8], SPLIT, None, ALU.mult)
            dve.tensor_copy(s.bup[:], ps[:, 2, 8:8 + E1 * 8].rearrange("p (e m) -> p e m", e=E1))
            dve.wait_ge(tanh_done, 1)
            dve.tensor_scalar(s.tgu[:], s.tg[:], UNSPLIT, None, ALU.mult)
            for n in range(2):
                dve.tensor_scalar(s.bv[:, n, :], s.bv[:, n, :], SPLIT, None, ALU.mult)
                dve.tensor_scalar(s.bo[:, n, :], s.bo[:, n, :], s.tg[:, n:n + 1], None, ALU.mult)
            rsqrt_all(dve, chain, s)


SMALL_LOADS = 13


def run_slots(eng, slot, drains):
    slot(0, 0, 0)
    slot(1, 0, 1)
    with eng.Fori(1, B // 2 - 1) as i:
        slot(2 * i, i, 0)
        slot(2 * i + 1, i, 1)
    slot(B - 2, B // 2 - 1, 0)
    slot(B - 1, B // 2 - 1, 1)
    for k in range(drains):
        slot(B + k, B // 2 + k // 2, k % 2)


def within(b, lo, hi=B):
    return not isinstance(b, int) or lo <= b < hi


def has_next(b):
    return within(b, 0, B - 1)


XN_T, CTX_T, Q_T, K_T, V_ = range(5)
XA_FRONT = 5
XA_FRONT_CREDIT = 1
XA_ACT = (XN_T, CTX_T, Q_T, K_T)
XA_UNITS = 8
HG = 4
BACK = 2 * TPB


def xattn_stage(nc, a, s, layer):
    t = f"x{layer}_"
    w = (s.w0, s.w1)[layer]
    with ExitStack() as ctx:
        sb = lambda name, shape, dt=F32: ctx.enter_context(nc.sbuf_tensor(t + name, shape, dt))
        sem = lambda name: ctx.enter_context(nc.semaphore(t + name))
        two = lambda name, shape, dt=F32: [sb(f"{name}{i}", shape, dt) for i in range(2)]
        c_in = two("ctx", [SK, D])
        m_in = two("mask", [P, SK], U8)
        xn = two("xn", [P, TPB, D])
        xt = two("xt", [P, 2, C, SQ], F16)
        ct = two("ct", [P, 2, C, SK], F16)
        qf, kf = two("qf", [P, C, SQ]), two("kf", [P, C, SK])
        qt = two("qt", [P, 2, C, SQ], F16)
        ks = two("ks", [P, 2, C, SK], F16)
        km = two("km", [P, 2, C, 8, SK], F16)
        vf = two("vf", [SK, D])
        va = two("va", [SK, 2, H, DK + 1], F16)
        mf = two("mf", [P, SK])
        add = two("add", [P, TPB, SK])
        keep = two("keep", [P, SK])
        live = two("live", [P, 1])
        sc = two("sc", [P, HG, SK])
        mx = two("mx", [P, HG])
        pr = two("pr", [P, HG, SK])
        pt = two("pt", [SK, 2, HG, P], F16)
        rs = sb("rs", [P, TPB, H])
        cn = sb("cn", [P, TPB, D])
        cnt = sb("cnt", [P, TPB, 2, C, P], F16)
        ps = ctx.enter_context(nc.psum_tensor(t + "ps", [P, 8, 512], F32))
        front, back = ps[:, 0, :], ps[:, 1, :]
        S = lambda u: ps[:, 2 + u % 2, 0:HG * SK].rearrange("p (h k) -> p h k", h=HG)
        PT = lambda u: ps[0:SK, 4 + u % 2, :].rearrange("p (h q) -> p h q", h=HG)
        O = lambda ti: ps[:, 6 + ti, 0:H * (DK + 1)].rearrange("p (h d) -> p h d", h=H)

        loaded = [sem("loaded0"), sem("loaded1")]
        load_free = sem("load_free")
        xn_ready = sem("xn_ready")
        front_ready = sem("front_ready")
        act_front = sem("act_front")
        front_done = sem("front_done")
        km_ready = sem("km_ready")
        s_ready = sem("s_ready")
        s_max = sem("s_max")
        shifted = sem("shifted")
        p_ready = sem("p_ready")
        pt_ready = sem("pt_ready")
        pt_hi = sem("pt_hi")
        pt_done = sem("pt_done")
        pv_done = sem("pv_done")
        o_done = sem("o_done")
        back_ready = sem("back_ready")
        act_back = sem("act_back")
        back_done = sem("back_done")
        ones_set = sem("ones_set")
        front_step, core_step, back_step = sem("front_step"), sem("core_step"), sem("back_step")
        block = ctx.enter_context(nc.Block())

        def earlier(b, par, u, lag, do):
            if u >= lag and within(b, 0):
                do(b, par, u - lag)
            elif u < lag and within(b, 1, B + 1):
                do(b - 1, 1 - par, u - lag + XA_UNITS)

        @block.sync
        def _(sp):
            masks = (a["mask_Bx1xS2_bk0"].rearrange("b o k -> b (o k)"), a["mask_BxS2_bf0"])[layer]
            with sp.Fori(0, B // 2) as i:
                for par in range(2):
                    b = 2 * i + par
                    sp.wait_ge(load_free, b + 1)
                    sp.dma_start(c_in[par][:], a["ctx_1024"][bass.ds(b, 1)].rearrange("o k d -> (o k) d")).then_inc(loaded[par], 16)
                    sp.dma_start(m_in[par][:], masks[bass.ds(b, 1), :].partition_broadcast(P)).then_inc(loaded[par], 16)

        @block.gpsimd
        def _(pool):
            chain = Chain(pool, ones_set)
            for par in range(2):
                chain(pool.memset(va[par][:, 0, :, DK:DK + 1], 1.0))
                chain(pool.memset(va[par][:, 1, :, DK:DK + 1], 0.0))
            with pool.Fori(0, B) as b:
                for u in range(XA_UNITS):
                    n = XA_UNITS * b + u
                    pool.wait_ge(s_max, 2 + n + 1)
                    pool.tensor_tensor(sc[u % 2][:], sc[u % 2][:], bcast(mx[u % 2][:], SK),
                                       ALU.subtract).then_inc(shifted, 1)

        @block.scalar
        def _(act):
            act.sem_inc(p_ready, 2)

            def evacuate(b, par, j):
                act.wait_ge(front_ready, XA_FRONT * b + j + 1)
                if j == XN_T:
                    if within(b, 1):
                        act.wait_ge(pv_done, 2 + XA_UNITS * (b - 1))
                    ins = act.activation(xt[par][:, 0].rearrange("p c q -> p (c q)"), front, ACT.Copy, scale=SPLIT)
                elif j == CTX_T:
                    ins = act.activation(ct[par][:, 0].rearrange("p c k -> p (c k)"), front[:, 0:C * SK], ACT.Copy, scale=SPLIT)
                else:
                    dst, n, col = (qf[par], SQ, 4 * layer) if j == Q_T else (kf[par], SK, 4 * layer + 2)
                    for m in range(C):
                        ins = act.activation(dst[:, m, :], front[:, m * n:(m + 1) * n], ACT.Identity,
                                             bias=s.bqk[:, col + m:col + m + 1], scale=1.0 / SPLIT)
                ins.then_inc(act_front, 1)

            def exps(b, u):
                n = XA_UNITS * b + u
                act.wait_ge(shifted, n + 1)
                act.wait_ge(pt_ready, n + 1)
                act.activation(pr[u % 2][:], sc[u % 2][:], ACT.Exp).then_inc(p_ready, 1)

            def pt_part(b, par, u):
                act.wait_ge(pt_ready, 2 + XA_UNITS * b + u + 1)
                act.wait_ge(pv_done, XA_UNITS * b + u + 1)
                act.activation(pt[u % 2][:, 0], PT(u), ACT.Copy, scale=SPLIT).then_inc(pt_hi, 1)

            def back_hi(b, ti):
                act.wait_ge(back_ready, BACK * b + 2 * ti + 1)
                act.wait_ge(back_done, BACK * b + 2 * ti + 2)
                act.activation(cnt[:, ti, 0], back[:, 0:D].rearrange("p (c q) -> p c q", c=C),
                               ACT.Copy).then_inc(act_back, 1)

            for j in XA_ACT:
                evacuate(0, 0, j)

            def slot(b, half, par):
                for u in range(XA_UNITS):
                    earlier(b, par, u, 1, pt_part)
                    if has_next(b) and u - 1 in XA_ACT:
                        evacuate(b + 1, 1 - par, u - 1)
                    if u == 3 and within(b, 1, B + 1):
                        back_hi(b - 1, 1)
                    if u == 7 and within(b, 0):
                        back_hi(b, 0)
                    if within(b, 0):
                        exps(b, u)

            run_slots(act, slot, 1)

        @block.tensor
        def _(pe):
            pe.sem_inc(pt_ready, 2)
            pe.sem_inc(pv_done, 2)
            pair = lambda ap, c, lo, n: tuple(ap[:, hl, c, lo:lo + n] for hl in range(2))

            def project(b, half, par, j):
                pe.wait_ge(front_done, XA_FRONT * b + j + 1)
                if j == XN_T:
                    pe.wait_ge(xn_ready, b + 1)
                    for c in range(C):
                        for ti in range(TPB):
                            last = pe.transpose(front[:, c * SQ + ti * P:c * SQ + (ti + 1) * P],
                                                xn[par][:, ti, c * P:(c + 1) * P], s.ident[:])
                elif j == CTX_T:
                    pe.wait_ge(loaded[par], 32 * (half + 1))
                    for c in range(C):
                        last = pe.transpose(front[:, c * SK:(c + 1) * SK], c_in[par][:, c * P:(c + 1) * P],
                                            s.ident[0:SK, 0:SK])
                elif j == V_:
                    last = matmul3(pe, front[0:SK, 0:D], [(pair(ct[par], c, 0, SK), pair(w[2], c, 0, D)) for c in range(C)])
                else:
                    wj, src, n = (w[0], xt[par], SQ) if j == Q_T else (w[1], ct[par], SK)
                    for m in range(C):
                        last = matmul3(pe, front[:, m * n:(m + 1) * n],
                                       [(pair(wj, c, m * P, P), pair(src, c, 0, n)) for c in range(C)])
                last.then_inc(front_ready, 1)

            def score(b, par, u):
                if u == 0:
                    pe.wait_ge(km_ready, b + 1)
                pe.wait_ge(s_max, XA_UNITS * b + u + 1)
                ti, m, h0 = u // 4, (u % 4) // 2, HG * (u % 2)
                matmul3(pe, S(u), [(pair(qt[par], m, ti * P, P),
                                    tuple(km[par][:, hl, m, h0:h0 + HG, :] for hl in range(2)))]).then_inc(s_ready, 1)

            def transposes(b, u):
                n = XA_UNITS * b + u
                pe.wait_ge(p_ready, 2 + n + 1)
                pe.wait_ge(pt_done, n + 1)
                for h in range(HG):
                    last = pe.transpose(PT(u)[:, h, :], pr[u % 2][:, h, :], s.ident[:])
                last.then_inc(pt_ready, 1)

            def times_v(b, par, u):
                ti = u // 4
                if u % 4 == 0:
                    pe.wait_ge(o_done, TPB * b + ti + 1)
                pe.wait_ge(pt_done, 2 + XA_UNITS * b + u + 1)
                for h in range(HG):
                    head = HG * (u % 4) + h
                    last = matmul3(pe, O(ti)[:, head, :],
                                   [(tuple(pt[u % 2][:, hl, h, :] for hl in range(2)),
                                     tuple(va[par][:, hl, head, :] for hl in range(2)))])
                last.then_inc(pv_done, 1)

            def back_transposes(b, ti):
                pe.wait_ge(back_done, BACK + BACK * b + 2 * ti)
                pe.wait_ge(o_done, 2 + TPB * b + ti + 1)
                for c in range(C):
                    last = pe.transpose(back[:, c * P:(c + 1) * P], cn[:, ti, c * P:(c + 1) * P], s.ident[:])
                last.then_inc(back_ready, 1)

            def back_product(b, ti):
                pe.wait_ge(back_done, BACK + BACK * b + 2 * ti + 1)
                matmul3(pe, back[:, 0:D],
                        [(tuple(cnt[:, ti, hl, c, :] for hl in range(2)), tuple(w[3][:, hl, c, :] for hl in range(2)))
                         for c in range(C)]).then_inc(back_ready, 1)

            for j in range(XA_FRONT):
                project(0, 0, 0, j)
            pe.wait_ge(ones_set, 4)
            score(0, 0, 0)
            score(0, 0, 1)

            def slot(b, half, par):
                for u in range(XA_UNITS):
                    if within(b, 0) and u + 2 < XA_UNITS:
                        score(b, par, u + 2)
                    elif has_next(b) and u + 2 >= XA_UNITS:
                        score(b + 1, 1 - par, u + 2 - XA_UNITS)
                    earlier(b, par, u, LAG, times_v)
                    if within(b, 0):
                        transposes(b, u)
                    if has_next(b) and u < XA_FRONT:
                        project(b + 1, half + par, 1 - par, u)
                    if within(b, 1, B + 1):
                        if u == 2:
                            back_transposes(b - 1, 1)
                        if u == 3:
                            back_product(b - 1, 1)
                    if within(b, 0):
                        if u == 6:
                            back_transposes(b, 0)
                        if u == 7:
                            back_product(b, 0)

            run_slots(pe, slot, 1)

        @block.vector
        def _(dve):
            dve.sem_inc(front_done, XA_FRONT_CREDIT)
            dve.sem_inc(load_free, 2)
            dve.sem_inc(s_max, 2)
            dve.sem_inc(pt_done, 2)
            dve.sem_inc(o_done, 2)
            dve.sem_inc(back_done, BACK)
            for par in range(2):
                dve.memset(live[par][:], 1.0)

            def normalised_x(b, par):
                for ti in range(TPB):
                    tile = bass.ds(TPB * b + ti, 1)
                    ins = dve.tensor_scalar(xn[par][:, ti, :], s.x[:, tile, :], s.mv[:, tile, 0], s.rstd[:, tile],
                                            ALU.subtract, ALU.mult)
                ins.then_inc(xn_ready, 1)

            def masks(half, par, chain):
                dve.wait_ge(loaded[par], 32 * (half + 1))
                chain(dve.tensor_copy(mf[par][:], m_in[par][:]))
                if layer == 0:
                    chain(dve.tensor_reduce(live[par][:], mf[par][:], AX_X, ALU.min))
                    chain(dve.tensor_scalar(live[par][:], live[par][:], -1.0, 1.0, ALU.mult, ALU.add))
                    for ti in range(TPB):
                        chain(dve.tensor_scalar(add[par][:, ti, :], mf[par][:], MASKED, None, ALU.mult))
                else:
                    chain(dve.tensor_scalar(keep[par][:], mf[par][:], -1.0, 1.0, ALU.mult, ALU.add))
                    for ti in range(TPB):
                        chain(dve.scalar_tensor_tensor(add[par][:, ti, :], mf[par][:], NEG, s.causal[:, ti, :],
                                                       ALU.mult, ALU.add))

            def evacuate(b, par, j, chain):
                if j in XA_ACT:
                    dve.wait_ge(act_front, len(XA_ACT) * b + XA_ACT.index(j) + 1)
                if j == XN_T:
                    dve.scalar_tensor_tensor(xt[par][:, 1].rearrange("p c q -> p (c q)"), front, SPLIT,
                                             xt[par][:, 0].rearrange("p c q -> p (c q)"),
                                             ALU.mult, ALU.subtract).then_inc(front_done, 1)
                elif j == CTX_T:
                    dve.scalar_tensor_tensor(ct[par][:, 1].rearrange("p c k -> p (c k)"), front[:, 0:C * SK], SPLIT,
                                             ct[par][:, 0].rearrange("p c k -> p (c k)"),
                                             ALU.mult, ALU.subtract).then_inc(front_done, 1)
                    dve.sem_inc(load_free, 1)
                elif j == Q_T:
                    chain(dve.tensor_copy(qt[par][:, 0], qf[par][:]))
                    dve.tensor_tensor(qt[par][:, 1], qf[par][:], qt[par][:, 0], ALU.subtract).then_inc(front_done, 1)
                elif j == K_T:
                    if layer == 1:
                        chain(dve.tensor_tensor(kf[par][:], kf[par][:], bcast_mid(keep[par][:], C), ALU.mult))
                    chain(dve.tensor_copy(ks[par][:, 0], kf[par][:]))
                    dve.tensor_tensor(ks[par][:, 1], kf[par][:], ks[par][:, 0], ALU.subtract).then_inc(front_done, 1)
                    dve.wait_ge(front_done, XA_FRONT_CREDIT + XA_FRONT * b + K_T + 1)
                    for h in range(8):
                        ins = dve.tensor_scalar(km[par][:].rearrange("p l m h k -> p (l m) h k")[:, :, h, :],
                                                ks[par][:].rearrange("p l m k -> p (l m) k"),
                                                s.head_of[:, h:h + 1], None, ALU.mult)
                    ins.then_inc(km_ready, 1)
                else:
                    dve.wait_ge(front_ready, XA_FRONT * b + V_ + 1)
                    chain(dve.scalar_tensor_tensor(vf[par][:], front[0:SK, 0:D], 1.0 / SPLIT, s.bv[0:SK, layer, :],
                                                   ALU.mult, ALU.add))
                    v = vf[par][:].rearrange("k (h d) -> k h d", h=H)
                    chain(dve.tensor_copy(va[par][:, 0, :, 0:DK], v))
                    dve.tensor_tensor(va[par][:, 1, :, 0:DK], v, va[par][:, 0, :, 0:DK], ALU.subtract).then_inc(front_done, 1)

            def soft(b, par, u, chain):
                n = XA_UNITS * b + u
                dve.wait_ge(s_ready, n + 1)
                dve.wait_ge(p_ready, n + 1)
                chain(dve.scalar_tensor_tensor(sc[u % 2][:], S(u), UNSPLIT / DK ** 0.5,
                                               bcast_mid(add[par][:, u // 4, :], HG), ALU.mult, ALU.add))
                dve.tensor_reduce(mx[u % 2][:], sc[u % 2][:], AX_X, ALU.max).then_inc(s_max, 1)

            def pt_part(b, par, u):
                n = XA_UNITS * b + u
                dve.wait_ge(pt_hi, n + 1)
                dve.scalar_tensor_tensor(pt[u % 2][:, 1], PT(u), SPLIT, pt[u % 2][:, 0],
                                         ALU.mult, ALU.subtract).then_inc(pt_done, 1)

            def normalise(b, par, ti, chain):
                dve.wait_ge(pv_done, 2 + XA_UNITS * b + 4 * ti + 4)
                chain(dve.reciprocal(rs[:, ti, :], O(ti)[:, :, DK]))
                if layer == 0:
                    chain(dve.tensor_scalar(rs[:, ti, :], rs[:, ti, :], live[par][:], None, ALU.mult))
                dve.tensor_tensor(cn[:, ti, :].rearrange("p (h d) -> p h d", h=H), O(ti)[:, :, 0:DK],
                                  bcast(rs[:, ti, :], DK), ALU.mult).then_inc(o_done, 1)

            def back_lo(b, ti):
                dve.wait_ge(act_back, TPB * b + ti + 1)
                dve.tensor_tensor(cnt[:, ti, 1], back[:, 0:D].rearrange("p (c q) -> p c q", c=C), cnt[:, ti, 0],
                                  ALU.subtract).then_inc(back_done, 1)

            def update(b, ti, chain):
                j = BACK * b + 2 * ti + 1
                dve.wait_ge(back_ready, j + 1)
                dve.scalar_tensor_tensor(s.xs[:].unsqueeze(1), back[:, 0:D].unsqueeze(1), s.tgu[:, layer:layer + 1],
                                         s.x[:, bass.ds(TPB * b + ti, 1), :], ALU.mult, ALU.add).then_inc(back_done, 1)
                dve.wait_ge(back_done, BACK + j + 1)
                chain(dve.tensor_tensor(s.xs[:], s.xs[:], s.bo[:, layer, :], ALU.add))
                chain(keep_tile(dve, chain, s, TPB * b + ti))

            chain = Chain(dve, front_step)
            normalised_x(0, 0)
            masks(0, 0, chain)
            for j in range(XA_FRONT):
                evacuate(0, 0, j, chain)

            def slot(b, half, par):
                front_chain = Chain(dve, front_step, XA_FRONT_LINKS[layer], b + 1)
                core_chain = Chain(dve, core_step, XA_UNITS, b)
                last_chain = Chain(dve, back_step, 2 * XA_BACK_LINKS[layer], b - 1)
                for u in range(XA_UNITS):
                    if within(b, 0):
                        soft(b, par, u, core_chain)
                    if u == 0 and has_next(b):
                        normalised_x(b + 1, 1 - par)
                        masks(half + par, 1 - par, front_chain)
                    earlier(b, par, u, LAG, pt_part)
                    if within(b, 1, B + 1):
                        if u == 0:
                            last_chain.n = XA_NORM_LINKS[layer]
                            update(b - 1, 0, last_chain)
                        if u == 2:
                            normalise(b - 1, 1 - par, 1, last_chain)
                        if u == 3:
                            back_lo(b - 1, 1)
                        if u == 4:
                            update(b - 1, 1, last_chain)
                            last_chain.close()
                    if within(b, 0):
                        if u == 6:
                            normalise(b, par, 0, Chain(dve, back_step, 2 * XA_BACK_LINKS[layer], b))
                        if u == 7:
                            back_lo(b, 0)
                    if has_next(b) and 1 <= u <= XA_FRONT:
                        evacuate(b + 1, 1 - par, u - 1, front_chain)
                if has_next(b):
                    front_chain.close()

            run_slots(dve, slot, 1)
            rsqrt_all(dve, Chain(dve, s.stage_step[layer]), s)


XA_FRONT_LINKS = (9, 9)
XA_BACK_LINKS = (7, 6)
XA_NORM_LINKS = (2, 1)
LAG = 2


F_XN, F_GATES, F_V, F_Q, F_K = 0, 1, 2, 4, 8
FF_FRONT = 12
FF_FRONT_CREDIT = 1
FF_ACT = (F_XN, *range(F_Q, FF_FRONT))
PARTS = TPB * E0
Z_STEPS = {h: range(2 * (h - 2), 2 * (h - 2) + 2) for h in range(2, 6)}
V_STEPS = {h: range(2 * (h - 6), 2 * (h - 6) + 2) for h in range(6, 11)}
V_STEPS |= {11: range(10, 13), 12: range(13, 16)}
Z_STEPS |= {13: range(8, 11), 14: range(11, 14), 15: range(14, 16)}
GATES = 2 * H


def ffn_stage(nc, a, s):
    t = "f_"
    with ExitStack() as ctx:
        sb = lambda name, shape, dt=F32: ctx.enter_context(nc.sbuf_tensor(t + name, shape, dt))
        sem = lambda name: ctx.enter_context(nc.semaphore(t + name))
        two = lambda name, shape, dt=F32: [sb(f"{name}{i}", shape, dt) for i in range(2)]
        xn = two("xn", [P, TPB, D])
        xt = two("xt", [P, 2, C, SQ], F16)
        qt = two("qt", [P, 2, H // 2, SQ], F16)
        kz = [sb(f"kz{i}", [P, 2, H, SQ], F16) for i in range(2)]
        g = sb("g", [P, TPB * GATES, E0])
        work, hit = sb("work", [P, TPB * GATES, E0]), sb("hit", [P, TPB * GATES, E0])
        sel = two("sel", [P, TPB, 2, H, E0])
        top = sb("top", [P, 3, TPB * GATES])
        mix = sb("mix", [P, TPB, H, E0])
        pv = sb("pv", [P, TPB, E0, DH])
        vtmp, ztmp = two("vtmp", [P, H, DH]), two("ztmp", [P, H, DH])
        vf = sb("vf", [P, H, DH])
        vh = two("vh", [P, 2, TPB, H, DH + 1], F16)
        mx, nb = two("mx", [P, TPB]), two("nb", [P, TPB])
        pr = two("pr", [P, TPB, SQ])
        pt = two("pt", [P, 2, TPB, TPB, P], F16)
        rs = two("rs", [P, 2 * TPB])
        at = two("at", [P, TPB, H, DH])
        selz = sb("selz", [P, TPB, H, E0])
        z = sb("z", [P, TPB, E0, DH])
        zt = sb("zt", [P, TPB, 2, E0 // 2, P], F16)
        ps = ctx.enter_context(nc.psum_tensor(t + "ps", [P, 8, 512], F32))
        front, back = ps[:, 0, :], ps[:, 1, :]
        S = lambda h: ps[:, 2 + h % 2, :].rearrange("p (t k) -> p t k", t=TPB)
        PT = lambda h: ps[:, 4 + h % 2, :]
        O = lambda h: ps[:, 6 + (h // 2) % 2, 0:4 * (DH + 1)].rearrange("p (h t d) -> p h t d", h=2, t=TPB)

        xn_ready = sem("xn_ready")
        front_ready = sem("front_ready")
        act_front = sem("act_front")
        front_done = sem("front_done")
        gates_ready = sem("gates_ready")
        gates_exp = sem("gates_exp")
        selz_ready = sem("selz_ready")
        vpart_ready, zpart_ready = sem("vpart_ready"), sem("zpart_ready")
        vpart_used, zpart_used = sem("vpart_used"), sem("zpart_used")
        v_sum = sem("v_sum")
        v_hi = sem("v_hi")
        v_done = sem("v_done")
        at_ready = sem("at_ready")
        z_ready = sem("z_ready")
        s_ready = sem("s_ready")
        s_max = sem("s_max")
        p_ready = sem("p_ready")
        pt_ready = sem("pt_ready")
        pt_hi = sem("pt_hi")
        pt_done = sem("pt_done")
        pv_done = sem("pv_done")
        o_done = sem("o_done")
        back_ready = sem("back_ready")
        act_back = sem("act_back")
        back_done = sem("back_done")
        zeroed = sem("zeroed")
        front_step, core_step, norm_step, back_step = (
            sem("front_step"), sem("core_step"), sem("norm_step"), sem("back_step"))
        block = ctx.enter_context(nc.Block())

        def earlier(b, par, h, lag, do):
            if h >= lag and within(b, 0):
                do(b, par, h - lag)
            elif h < lag and within(b, 1, B + 1):
                do(b - 1, 1 - par, h - lag + H)

        @block.gpsimd
        def _(pool):
            chain = Chain(pool, zeroed)
            for par in range(2):
                chain(pool.memset(vh[par][:, 0, :, :, DH:DH + 1], 1.0))
                chain(pool.memset(vh[par][:, 1, :, :, DH:DH + 1], 0.0))
                chain(pool.memset(kz[par][:].rearrange("p l h k -> p (l h k)").bitcast(F32), 0.0))

            def v_part(b, n):
                pool.wait_ge(vpart_used, PARTS * b + n + 1)
                ti, e = n // E0, n % E0
                pool.tensor_tensor(vtmp[n % 2][:], bcast_mid(pv[:, ti, e, :], H), bcast(mix[:, ti, :, e], DH),
                                   ALU.mult).then_inc(vpart_ready, 1)

            def z_part(b, par, n):
                pool.wait_ge(zpart_used, PARTS * b + n + 1)
                ti, e = n // E0, n % E0
                pool.tensor_tensor(ztmp[n % 2][:], at[par][:, ti], bcast(selz[:, ti, :, e], DH),
                                   ALU.mult).then_inc(zpart_ready, 1)

            def projected(b):
                pool.wait_ge(gates_ready, 2 * b + 2)
                pool.wait_ge(front_done, FF_FRONT_CREDIT + FF_FRONT * b + F_V + TPB)

            projected(0)
            for n in range(PARTS):
                v_part(0, n)

            def slot(b, half, par):
                for h in range(H):
                    if within(b, 1, B + 1):
                        if h == min(Z_STEPS):
                            pool.wait_ge(selz_ready, b)
                            pool.wait_ge(at_ready, b)
                        for n in Z_STEPS.get(h, ()):
                            z_part(b - 1, 1 - par, n)
                    if has_next(b):
                        if h == min(V_STEPS):
                            projected(b + 1)
                        for n in V_STEPS.get(h, ()):
                            v_part(b + 1, n)

            run_slots(pool, slot, 1)

        @block.scalar
        def _(act):
            act.sem_inc(p_ready, 2)

            def pt_part(b, par, h):
                act.wait_ge(pt_ready, 2 + H * b + h + 1)
                act.wait_ge(pv_done, H * b + h + 1)
                act.activation(pt[h % 2][:, 0].rearrange("p c t q -> p (c t q)"), PT(h), ACT.Copy,
                               scale=SPLIT).then_inc(pt_hi, 1)

            def evacuate(b, par, j):
                act.wait_ge(front_ready, FF_FRONT * b + j + 1)
                if j == F_XN:
                    if within(b, 1):
                        act.wait_ge(pv_done, 2 + H * (b - 1))
                    ins = act.activation(xt[par][:, 0].rearrange("p c q -> p (c q)"), front, ACT.Copy, scale=SPLIT)
                elif j < F_K:
                    r = j - F_Q
                    ins = act.activation(qt[par][:, 0, 2 * r:2 * r + 2, :].rearrange("p m q -> p (m q)"), front,
                                         ACT.Copy, scale=1.0 / SPLIT)
                else:
                    r = j - F_K
                    for odd in range(2):
                        rows = slice(DH * odd, DH * odd + DH)
                        ins = act.activation(kz[par][rows, 0, 4 * r + odd:4 * r + 4:2, :],
                                             front[rows, :].rearrange("p (m k) -> p m k", m=2), ACT.Copy, scale=1.0 / SPLIT)
                ins.then_inc(act_front, 1)

            def gates(b):
                act.wait_ge(gates_ready, 2 * b + 1)
                act.activation(work[:], g[:], ACT.Exp, scale=-1.0).then_inc(gates_exp, 1)

            def v_part(b, par, ti):
                act.wait_ge(v_sum, TPB * b + ti + 1)
                act.activation(vh[par][:, 0, ti, :, 0:DH], vf[:], ACT.Copy).then_inc(v_hi, 1)

            def exps(b, h):
                n = H * b + h
                act.wait_ge(s_max, n + 1)
                act.wait_ge(pt_ready, n + 1)
                for ti in range(TPB):
                    ins = act.activation(pr[h % 2][:, ti, :], S(h)[:, ti, :], ACT.Exp, bias=nb[h % 2][:, ti:ti + 1],
                                         scale=UNSPLIT / DH ** 0.5)
                ins.then_inc(p_ready, 1)

            def back_hi(b, ti):
                act.wait_ge(back_ready, BACK * b + 2 * ti + 1)
                act.wait_ge(back_done, BACK * b + 2 * ti + 2)
                act.activation(zt[:, ti, 0].rearrange("p c q -> p (c q)"), back, ACT.Copy).then_inc(act_back, 1)

            act.wait_ge(zeroed, 6)
            evacuate(0, 0, F_XN)
            gates(0)
            for j in range(F_Q, FF_FRONT):
                evacuate(0, 0, j)
            for ti in range(TPB):
                v_part(0, 0, ti)

            def slot(b, half, par):
                for h in range(H):
                    earlier(b, par, h, 1, pt_part)
                    if has_next(b):
                        if h - 1 in FF_ACT:
                            evacuate(b + 1, 1 - par, h - 1)
                        if h == GATES_STEP + 1:
                            gates(b + 1)
                        for ti in range(TPB):
                            if h == V_SUMMED[ti] + 1:
                                v_part(b + 1, 1 - par, ti)
                    if h == 1 and within(b, 2, B + 2):
                        back_hi(b - 2, 1)
                    if h == 7 and within(b, 1, B + 1):
                        back_hi(b - 1, 0)
                    if within(b, 0):
                        exps(b, h)

            run_slots(act, slot, 2)

        @block.tensor
        def _(pe):
            pe.sem_inc(pt_ready, 2)
            pe.sem_inc(pv_done, 2)

            pair = lambda ap, c, lo, n: tuple(ap[:, hl, c, lo:lo + n] for hl in range(2))

            def score(b, par, h):
                if h == 0:
                    pe.wait_ge(front_done, FF_FRONT_CREDIT + FF_FRONT * (b + 1))
                pe.wait_ge(p_ready, H * b + h + 1)
                for ti in range(TPB):
                    last = matmul3(pe, S(h)[:, ti, :],
                                   [(pair(qt[par], h // 2, ti * P, P), pair(kz[par], h, 0, SQ))])
                last.then_inc(s_ready, 1)

            def transposes(b, h):
                n = H * b + h
                pe.wait_ge(p_ready, 2 + n + 1)
                pe.wait_ge(pt_done, n + 1)
                for c in range(TPB):
                    for ti in range(TPB):
                        at_ = (c * TPB + ti) * P
                        last = pe.transpose(PT(h)[:, at_:at_ + P], pr[h % 2][:, ti, c * P:(c + 1) * P], s.ident[:])
                last.then_inc(pt_ready, 1)

            def times_v(b, par, h):
                if h == 0:
                    pe.wait_ge(v_done, TPB * (b + 1))
                if h % 2 == 0:
                    pe.wait_ge(o_done, H // 2 * b + h // 2 + 1)
                pe.wait_ge(pt_done, 2 + H * b + h + 1)
                for ti in range(TPB):
                    last = matmul3(pe, O(h)[:, h % 2, ti, :],
                                   [(tuple(pt[h % 2][:, hl, c, ti, :] for hl in range(2)),
                                     tuple(vh[par][:, hl, c, h, :] for hl in range(2))) for c in range(TPB)])
                last.then_inc(pv_done, 1)

            def project(b, par, j):
                pe.wait_ge(front_done, FF_FRONT * b + j + 1)
                if j == F_XN:
                    pe.wait_ge(xn_ready, b + 1)
                    for c in range(C):
                        for ti in range(TPB):
                            last = pe.transpose(front[:, c * SQ + ti * P:c * SQ + (ti + 1) * P],
                                                xn[par][:, ti, c * P:(c + 1) * P], s.ident[:])
                elif j == F_GATES:
                    for ti in range(TPB):
                        last = matmul3(pe, front[:, ti * 256:(ti + 1) * 256],
                                       [(pair(xt[par], c, ti * P, P), pair(s.fg, c, 0, 2 * H * E0)) for c in range(C)])
                elif j < F_Q:
                    ti = j - F_V
                    last = matmul3(pe, front, [(pair(xt[par], c, ti * P, P), pair(s.fv, c, 0, E0 * DH)) for c in range(C)])
                else:
                    w, r = (s.fq, j - F_Q) if j < F_K else (s.fk, j - F_K)
                    for m in range(2):
                        last = matmul3(pe, front[:, m * SQ:(m + 1) * SQ],
                                       [(pair(w, c, (2 * r + m) * P, P), pair(xt[par], c, 0, SQ)) for c in range(C)])
                last.then_inc(front_ready, 1)

            def back_transposes(b, ti):
                pe.wait_ge(back_done, BACK + BACK * b + 2 * ti)
                pe.wait_ge(z_ready, TPB * b + ti + 1)
                for ec in range(E0 // 2):
                    last = pe.transpose(back[:, ec * P:(ec + 1) * P],
                                        z[:, ti, 2 * ec:2 * ec + 2, :].rearrange("p e d -> p (e d)"), s.ident[:])
                last.then_inc(back_ready, 1)

            def back_product(b, ti):
                pe.wait_ge(back_done, BACK + BACK * b + 2 * ti + 1)
                matmul3(pe, back[:, 0:D],
                        [(tuple(zt[:, ti, hl, ec, :] for hl in range(2)), tuple(s.fo[:, hl, ec, :] for hl in range(2)))
                         for ec in range(E0 // 2)]).then_inc(back_ready, 1)

            for j in range(FF_FRONT):
                project(0, 0, j)
            score(0, 0, 0)
            score(0, 0, 1)

            def slot(b, half, par):
                for h in range(H):
                    earlier(b, par, h, LAG, times_v)
                    if within(b, 0):
                        transposes(b, h)
                    if within(b, 0) and h + 2 < H:
                        score(b, par, h + 2)
                    elif has_next(b) and h + 2 >= H:
                        score(b + 1, 1 - par, h + 2 - H)
                    if has_next(b) and h < FF_FRONT:
                        project(b + 1, 1 - par, h)
                    if within(b, 2, B + 2):
                        if h == 0:
                            back_transposes(b - 2, 1)
                        if h == 1:
                            back_product(b - 2, 1)
                    if within(b, 1, B + 1):
                        if h == 6:
                            back_transposes(b - 1, 0)
                        if h == 7:
                            back_product(b - 1, 0)

            run_slots(pe, slot, 2)

        @block.vector
        def _(dve):
            dve.sem_inc(front_done, FF_FRONT_CREDIT)
            dve.sem_inc(vpart_used, 2)
            dve.sem_inc(zpart_used, 2)
            dve.sem_inc(pt_done, 2)
            dve.sem_inc(o_done, 2)
            dve.sem_inc(back_done, BACK)

            def gate_choice(b, par, chain):
                dve.wait_ge(front_ready, FF_FRONT * b + F_GATES + 1)
                dve.tensor_scalar(g[:].rearrange("p a e -> p (a e)"), front, UNSPLIT, None, ALU.mult).then_inc(front_done, 1)
                dve.wait_ge(front_done, FF_FRONT_CREDIT + FF_FRONT * b + F_GATES + 1)
                choose_top(dve, chain, g[:], s.rank[:, E1 - E0:E1], TOP0, work[:], hit[:], top[:],
                           sel[par][:].rearrange("p t v h e -> p (t v h) e"))
                dve.sem_inc(gates_ready, 1)

            def gate_weights(b, par, chain):
                dve.wait_ge(gates_exp, b + 1)
                chain(dve.tensor_scalar(work[:], work[:], 1.0, None, ALU.add))
                chain(dve.reciprocal(hit[:], work[:]))
                dve.scalar_tensor_tensor(mix[:], hit[:].rearrange("p (t v h) e -> p t v h e", t=TPB, v=2)[:, :, 0],
                                         SPLIT, sel[par][:, :, 0], ALU.mult, ALU.mult).then_inc(gates_ready, 1)

            def evacuate(b, par, j):
                if j in FF_ACT:
                    dve.wait_ge(act_front, len(FF_ACT) * b + FF_ACT.index(j) + 1)
                if j == F_XN:
                    ins = dve.scalar_tensor_tensor(xt[par][:, 1].rearrange("p c q -> p (c q)"), front, SPLIT,
                                                   xt[par][:, 0].rearrange("p c q -> p (c q)"), ALU.mult, ALU.subtract)
                elif j < F_Q:
                    dve.wait_ge(front_ready, FF_FRONT * b + j + 1)
                    ins = dve.tensor_scalar(pv[:, j - F_V].rearrange("p e d -> p (e d)"), front, UNSPLIT, None, ALU.mult)
                elif j < F_K:
                    m = slice(2 * (j - F_Q), 2 * (j - F_Q) + 2)
                    ins = dve.scalar_tensor_tensor(qt[par][:, 1, m, :].rearrange("p m q -> p (m q)"), front, 1.0 / SPLIT,
                                                   qt[par][:, 0, m, :].rearrange("p m q -> p (m q)"), ALU.mult, ALU.subtract)
                else:
                    for odd in range(2):
                        rows = slice(DH * odd, DH * odd + DH)
                        hs = slice(4 * (j - F_K) + odd, 4 * (j - F_K) + 4, 2)
                        ins = dve.scalar_tensor_tensor(kz[par][rows, 1, hs, :],
                                                       front[rows, :].rearrange("p (m k) -> p m k", m=2),
                                                       1.0 / SPLIT, kz[par][rows, 0, hs, :], ALU.mult, ALU.subtract)
                ins.then_inc(front_done, 1)

            def normalised_x(b, par):
                for ti in range(TPB):
                    tile = bass.ds(TPB * b + ti, 1)
                    ins = dve.tensor_scalar(xn[par][:, ti, :], s.x[:, tile, :], s.mv[:, tile, 0], s.rstd[:, tile],
                                            ALU.subtract, ALU.mult)
                ins.then_inc(xn_ready, 1)

            def v_part(b, n):
                ti, e = n // E0, n % E0
                if n == E0:
                    dve.wait_ge(v_hi, TPB * b + 1)
                    dve.wait_ge(v_done, TPB * b + 1)
                dve.wait_ge(vpart_ready, PARTS * b + n + 1)
                if e == 0:
                    dve.tensor_copy(vf[:], vtmp[n % 2][:]).then_inc(vpart_used, 1)
                else:
                    dve.tensor_tensor(vf[:], vf[:], vtmp[n % 2][:], ALU.add).then_inc(vpart_used, 1)
                dve.wait_ge(vpart_used, 2 + PARTS * b + n + 1)
                if e == E0 - 1:
                    dve.sem_inc(v_sum, 1)

            def v_lo(b, par, ti):
                dve.wait_ge(v_hi, TPB * b + ti + 1)
                dve.tensor_tensor(vh[par][:, 1, ti, :, 0:DH], vf[:], vh[par][:, 0, ti, :, 0:DH],
                                  ALU.subtract).then_inc(v_done, 1)

            def z_part(b, n):
                ti, e = n // E0, n % E0
                dve.wait_ge(zpart_ready, PARTS * b + n + 1)
                dve.tensor_reduce(z[:, ti, e, :], ztmp[n % 2][:].rearrange("p h d -> p d h"), AX_X,
                                  ALU.add).then_inc(zpart_used, 1)
                if e == E0 - 1:
                    dve.wait_ge(zpart_used, 2 + PARTS * b + n + 1)
                    dve.sem_inc(z_ready, 1)

            def maxima(b, h, chain):
                dve.wait_ge(s_ready, H * b + h + 1)
                dve.wait_ge(p_ready, H * b + h + 1)
                chain(dve.tensor_reduce(mx[h % 2][:], S(h), AX_X, ALU.max))
                dve.tensor_scalar(nb[h % 2][:], mx[h % 2][:], -UNSPLIT / DH ** 0.5, None, ALU.mult).then_inc(s_max, 1)

            def pt_part(b, par, h):
                dve.wait_ge(pt_hi, H * b + h + 1)
                dve.scalar_tensor_tensor(pt[h % 2][:, 1].rearrange("p c t q -> p (c t q)"), PT(h), SPLIT,
                                         pt[h % 2][:, 0].rearrange("p c t q -> p (c t q)"),
                                         ALU.mult, ALU.subtract).then_inc(pt_done, 1)

            def normalise(b, par, hp):
                chain = Chain(dve, norm_step, 1, H // 2 * b + hp)
                h = 2 * hp
                dve.wait_ge(pv_done, 2 + H * b + h + 2)
                r = rs[hp % 2][:].rearrange("p (h t) -> p h t", h=2)
                chain(dve.reciprocal(r, O(h)[:, :, :, DH]))
                for ti in range(TPB):
                    ins = dve.tensor_tensor(at[par][:, ti, h:h + 2, :], O(h)[:, :, ti, 0:DH], bcast(r[:, :, ti], DH), ALU.mult)
                ins.then_inc(o_done, 1)

            def back_lo(b, ti):
                dve.wait_ge(act_back, TPB * b + ti + 1)
                dve.tensor_tensor(zt[:, ti, 1].rearrange("p c q -> p (c q)"), back,
                                  zt[:, ti, 0].rearrange("p c q -> p (c q)"), ALU.subtract).then_inc(back_done, 1)

            def update(b, ti):
                chain = Chain(dve, back_step, UPDATE_LINKS, TPB * b + ti)
                j = BACK * b + 2 * ti + 1
                dve.wait_ge(back_ready, j + 1)
                dve.scalar_tensor_tensor(s.xs[:].unsqueeze(1), back[:, 0:D].unsqueeze(1), s.tgu[:, 2:3],
                                         s.x[:, bass.ds(TPB * b + ti, 1), :], ALU.mult, ALU.add).then_inc(back_done, 1)
                dve.wait_ge(back_done, BACK + j + 1)
                chain(keep_tile(dve, chain, s, TPB * b + ti))
                chain.close()

            chain = Chain(dve, front_step)
            normalised_x(0, 0)
            evacuate(0, 0, F_XN)
            gate_choice(0, 0, chain)
            gate_weights(0, 0, chain)
            for j in range(F_V, FF_FRONT):
                evacuate(0, 0, j)
            for ti in range(TPB):
                for n in range(E0 * ti, E0 * ti + E0):
                    v_part(0, n)
                v_lo(0, 0, ti)

            def slot(b, half, par):
                front_chain = Chain(dve, front_step, FF_FRONT_LINKS, b + 1)
                core_chain = Chain(dve, core_step, H, b)
                for h in range(H):
                    if within(b, 0):
                        maxima(b, h, core_chain)
                    if h == 0 and has_next(b):
                        normalised_x(b + 1, 1 - par)
                    if h == 0 and within(b, 1, B + 1):
                        dve.tensor_copy(selz[:], sel[1 - par][:, :, 1]).then_inc(selz_ready, 1)
                    earlier(b, par, h, LAG, pt_part)
                    if h % 2 == 0:
                        if h >= 4 and within(b, 0):
                            normalise(b, par, (h - 4) // 2)
                        elif h < 4 and within(b, 1, B + 1):
                            normalise(b - 1, 1 - par, (h - 4) // 2 + H // 2)
                            if h == 2:
                                dve.wait_ge(o_done, 2 + H // 2 * b)
                                dve.sem_inc(at_ready, 1)
                    if within(b, 2, B + 2):
                        if h == 1:
                            back_lo(b - 2, 1)
                        if h == 2:
                            update(b - 2, 1)
                    if within(b, 1, B + 1):
                        for n in Z_STEPS.get(h, ()):
                            z_part(b - 1, n)
                        if h == 7:
                            back_lo(b - 1, 0)
                        if h == 8:
                            update(b - 1, 0)
                    if has_next(b):
                        for ti in range(TPB):
                            if h == V_SUMMED[ti] + 1:
                                v_lo(b + 1, 1 - par, ti)
                        for n in V_STEPS.get(h, ()):
                            v_part(b + 1, n)
                        if h - 1 == F_GATES:
                            gate_choice(b + 1, 1 - par, front_chain)
                        elif 0 <= h - 1 < FF_FRONT:
                            evacuate(b + 1, 1 - par, h - 1)
                        if h == GATES_STEP + 1:
                            gate_weights(b + 1, 1 - par, front_chain)
                            front_chain.close()

            run_slots(dve, slot, 2)
            rsqrt_all(dve, Chain(dve, s.stage_step[2]), s)


GATES_STEP = F_GATES + 1
V_SUMMED = [max(h for h in V_STEPS if E0 * ti + E0 - 1 in V_STEPS[h]) for ti in range(TPB)]
FF_FRONT_LINKS = 15
UPDATE_LINKS = 4


TN = 512
CHUNKS = TILES * P // TN
TPC = TN // P
M = HID // P
RING = 4


def moe_stage(nc, a, s, out):
    t = "m_"
    with ExitStack() as ctx:
        sb = lambda name, shape, dt=F32: ctx.enter_context(nc.sbuf_tensor(t + name, shape, dt))
        sem = lambda name: ctx.enter_context(nc.semaphore(t + name))
        two = lambda name, shape, dt=F32: [sb(f"{name}{i}", shape, dt) for i in range(2)]
        uraw, draw = two("uraw", [P, C, HID]), two("draw", [P, M, D])
        us, dsp = two("us", [P, 2, C, HID], F16), two("ds", [P, 2, M, D], F16)
        xt = sb("xt", [P, 2, C, TILES * P], F16)
        hs = two("hs", [P, 2, M, TN], F16)
        cwe = two("cwe", [P, TILES])
        bue = two("bue", [P, M])
        ps = ctx.enter_context(nc.psum_tensor(t + "ps", [P, 8, 512], F32))
        cwu = sb("cwu", [P, TILES, E1])
        w_loaded = [sem(f"w_loaded{i}") for i in range(2)]
        w_split = sem("w_split")
        w_hi = sem("w_hi")
        w_free = sem("w_free")
        u_ready = sem("u_ready")
        h_gelu = sem("h_gelu")
        h_done = sem("h_done")
        h_hi = sem("h_hi")
        y_ready = sem("y_ready")
        y_done = sem("y_done")
        stored = sem("stored")
        xn_ready, tr_ready, tr_hi, tr_done = sem("xn_ready"), sem("tr_ready"), sem("tr_hi"), sem("tr_done")
        g_ready, cw_exp, cwt_ready, cwt_done, b_ready, b_done = (
            sem("g_ready"), sem("cw_exp"), sem("cwt_ready"), sem("cwt_done"), sem("b_ready"), sem("b_done"))
        dve_step = sem("dve_step")
        cw_ready, shifted = sem("cw_ready"), sem("shifted")

        def load(sp, e, par):
            sp.wait_ge(w_split, e + 1)
            sp.dma_start(uraw[par][:], a["L1_ffn_Wup"][bass.ds(e, 1)].rearrange("o (c p) h -> (o p) c h", p=P)).then_inc(w_loaded[par], 16)
            sp.dma_start(draw[par][:], a["L1_ffn_Wdown"][bass.ds(e, 1)].rearrange("o (m p) d -> (o p) m d", p=P)).then_inc(w_loaded[par], 16)

        prep = ExitStack()
        with prep:
            psb = lambda name, shape, dt=F32: prep.enter_context(nc.sbuf_tensor(t + name, shape, dt))
            xn = [psb(f"xn{i}", [P, TPB, D]) for i in range(2)]
            g, work, hit = (psb(n, [P, TILES, E1]) for n in ("g", "work", "hit"))
            sel, cw = psb("sel", [P, TILES, E1]), psb("cw", [P, TILES, E1])
            top = psb("top", [P, 3, TILES])
            cwt = psb("cwt", [E1, TILES * P])
            tr = lambda k: ps[:, k % 2, :]
            G = ps[:, 2, 0:TILES * E1].rearrange("p (t e) -> p t e", t=TILES)
            block = prep.enter_context(nc.Block())

            @block.sync
            def _(sp):
                sp.wait_ge(w_split, 2)
                for e in range(2):
                    load(sp, e, e)

            @block.scalar
            def _(act):
                for k in range(B):
                    act.wait_ge(tr_ready, k + 1)
                    act.activation(xt[:, 0, :, k * SQ:(k + 1) * SQ], tr(k).rearrange("p (c q) -> p c q", c=C),
                                   ACT.Copy, scale=SPLIT).then_inc(tr_hi, 1)
                act.wait_ge(shifted, 1)
                act.activation(work[:], work[:], ACT.Exp).then_inc(cw_exp, 1)
                for q in range(CHUNKS):
                    act.wait_ge(cwt_ready, q + 1)
                    act.activation(cwt[:, q * TN:(q + 1) * TN], ps[0:E1, 4 + q, :], ACT.Copy).then_inc(cwt_done, 1)

            @block.tensor
            def _(pe):
                def gate(k):
                    pe.wait_ge(tr_done, k + 1)
                    for ti in range(TPB):
                        tile = TPB * k + ti
                        last = matmul3(pe, G[:, tile, :],
                                       [(tuple(xt[:, hl, c, tile * P:(tile + 1) * P] for hl in range(2)),
                                         tuple(s.wg[:, hl, c, :] for hl in range(2))) for c in range(C)])
                    return last

                for k in range(B):
                    pe.wait_ge(xn_ready, k + 1)
                    if k >= 2:
                        pe.wait_ge(tr_done, k - 1)
                    for c in range(C):
                        for ti in range(TPB):
                            last = pe.transpose(tr(k)[:, c * SQ + ti * P:c * SQ + (ti + 1) * P],
                                                xn[k % 2][:, ti, c * P:(c + 1) * P], s.ident[:])
                    last.then_inc(tr_ready, 1)
                    if k >= 1:
                        gate(k - 1)
                gate(B - 1).then_inc(g_ready, 1)
                pe.wait_ge(cw_ready, 1)
                for q in range(CHUNKS):
                    for ti in range(TPC):
                        last = pe.transpose(ps[0:E1, 4 + q, ti * P:(ti + 1) * P], cw[:, TPC * q + ti, :], s.ident[:])
                    last.then_inc(cwt_ready, 1)
                for tile in range(TILES):
                    if tile % TPC == 0:
                        pe.wait_ge(cwt_done, tile // TPC + 1)
                    if tile >= 2:
                        pe.wait_ge(b_done, tile - 1)
                    pe.matmul(ps[:, 2 + tile % 2, 0:D], cwt[:, tile * P:(tile + 1) * P], s.bdown[:],
                              start=True, stop=True).then_inc(b_ready, 1)

            def lo_part(dve, k):
                dve.wait_ge(tr_hi, k + 1)
                dve.scalar_tensor_tensor(xt[:, 1, :, k * SQ:(k + 1) * SQ], tr(k).rearrange("p (c q) -> p c q", c=C),
                                         SPLIT, xt[:, 0, :, k * SQ:(k + 1) * SQ], ALU.mult, ALU.subtract).then_inc(tr_done, 1)

            @block.vector
            def _(dve):
                dve.sem_inc(w_split, 2)
                chain = Chain(dve, dve_step)
                for k in range(B):
                    if k >= 2:
                        dve.wait_ge(tr_ready, k - 1)
                    for ti in range(TPB):
                        tile = TPB * k + ti
                        ins = dve.tensor_scalar(xn[k % 2][:, ti, :], s.x[:, tile, :], s.mv[:, tile, 0:1],
                                                s.rstd[:, tile:tile + 1], ALU.subtract, ALU.mult)
                    ins.then_inc(xn_ready, 1)
                    if k >= 1:
                        lo_part(dve, k - 1)
                lo_part(dve, B - 1)
                dve.wait_ge(g_ready, 1)
                chain(dve.tensor_scalar(g[:], G, UNSPLIT, None, ALU.mult))
                choose_top(dve, chain, g[:], s.rank[:], TOP1, work[:], hit[:], top[:], sel[:])
                dve.tensor_tensor(work[:], g[:], bcast(top[:, 0, :], E1), ALU.subtract).then_inc(shifted, 1)
                dve.wait_ge(cw_exp, 1)
                chain(dve.tensor_tensor(cw[:], work[:], sel[:], ALU.mult))
                chain(dve.tensor_reduce(top[:, 1, :], cw[:], AX_X, ALU.add))
                chain(dve.reciprocal(top[:, 2, :], top[:, 1, :]))
                chain(dve.tensor_scalar(top[:, 2, :], top[:, 2, :], s.tg[:, 3:4], None, ALU.mult))
                dve.tensor_tensor(cw[:], cw[:], bcast(top[:, 2, :], E1), ALU.mult).then_inc(cw_ready, 1)
                dve.wait_ge(cw_ready, 1)
                chain(dve.tensor_scalar(cwu[:], cw[:], UNSPLIT, None, ALU.mult))
                for tile in range(TILES):
                    dve.wait_ge(b_ready, tile + 1)
                    dve.tensor_tensor(s.x[:, tile, :], s.x[:, tile, :], ps[:, 2 + tile % 2, 0:D], ALU.add).then_inc(b_done, 1)
                dve.wait_ge(b_done, TILES)

        hf = [sb(f"hf{i}", [P, TN]) for i in range(RING)]
        block = ctx.enter_context(nc.Block())
        U = lambda m: ps[:, m % RING, :]
        Y = lambda ti: ps[:, RING + ti % RING, 0:D]

        @block.sync
        def _(sp):
            with sp.Fori(1, E1 // 2) as i:
                for par in range(2):
                    load(sp, 2 * i + par, par)
            for c in range(CHUNKS):
                sp.wait_ge(y_done, RING + ((E1 - 1) * CHUNKS + c + 1) * TPC)
                sp.dma_start(out.rearrange("b (t p) d -> p (b t) d", p=P)[:, TPC * c:TPC * (c + 1), :],
                             s.x[:, TPC * c:TPC * (c + 1), :]).then_inc(stored, 16)
            sp.wait_ge(stored, 16 * CHUNKS)

        @block.scalar
        def _(act):
            act.sem_inc(h_gelu, RING)

            def split(e, par, turn):
                act.wait_ge(w_loaded[par], 32 * (turn + 1))
                act.wait_ge(w_free, e + 1)
                act.activation(us[par][:, 0], uraw[par][:], ACT.Copy, scale=SPLIT)
                act.activation(dsp[par][:, 0], draw[par][:], ACT.Copy, scale=SPLIT).then_inc(w_hi, 1)

            def expert(e, par, turn, last=False):
                for c in range(CHUNKS):
                    for m in range(M):
                        n = (e * CHUNKS + c) * M + m
                        act.wait_ge(u_ready, n + 1)
                        act.wait_ge(h_done, n + 1)
                        act.activation(hf[m % RING][:], U(m), ACT.Gelu, bias=bue[par][:, m:m + 1],
                                       scale=UNSPLIT).then_inc(h_gelu, 1)
                    if c == 1 and not last:
                        split(e + 1, 1 - par, turn + par)

            split(0, 0, 0)
            act.wait_ge(w_split, 2 + 1)
            with act.Fori(0, E1 // 2 - 1) as i:
                for par in range(2):
                    expert(2 * i + par, par, i)
            expert(E1 - 2, 0, E1 // 2 - 1)
            expert(E1 - 1, 1, E1 // 2 - 1, last=True)

        @block.tensor
        def _(pe):
            def up(e, par, c):
                for m in range(M):
                    n = (e * CHUNKS + c) * M + m
                    pe.wait_ge(h_gelu, n + 1)
                    matmul3(pe, U(m),
                            [(tuple(us[par][:, hl, k, m * P:(m + 1) * P] for hl in range(2)),
                              tuple(xt[:, hl, k, c * TN:(c + 1) * TN] for hl in range(2))) for k in range(C)]).then_inc(u_ready, 1)

            def down(e, par, c):
                pe.wait_ge(h_done, RING + (e * CHUNKS + c + 1) * M)
                for ti in range(TPC):
                    n = (e * CHUNKS + c) * TPC + ti
                    pe.wait_ge(y_done, n + 1)
                    matmul3(pe, Y(ti),
                            [(tuple(hs[c % 2][:, hl, m, ti * P:(ti + 1) * P] for hl in range(2)),
                              tuple(dsp[par][:, hl, m, :] for hl in range(2))) for m in range(M)]).then_inc(y_ready, 1)

            def expert(e, par, last=False):
                for c in range(CHUNKS):
                    if c + 1 < CHUNKS:
                        up(e, par, c + 1)
                    elif not last:
                        pe.wait_ge(w_split, 2 + e + 2)
                        up(e + 1, 1 - par, 0)
                    down(e, par, c)

            pe.wait_ge(w_split, 2 + 1)
            up(0, 0, 0)
            with pe.Fori(0, E1 // 2 - 1) as i:
                for par in range(2):
                    expert(2 * i + par, par)
            expert(E1 - 2, 0)
            expert(E1 - 1, 1, last=True)

        @block.vector
        def _(dve):
            dve.sem_inc(w_free, 2)
            dve.sem_inc(h_done, RING)
            dve.sem_inc(y_done, RING)

            def split(e, par):
                dve.wait_ge(w_hi, e + 1)
                one = slice(e, e + 1) if isinstance(e, int) else bass.ds(e, 1)
                dve.tensor_copy(cwe[par][:].unsqueeze(2), cwu[:, :, one])
                dve.tensor_copy(bue[par][:].unsqueeze(1), s.bup[:, one, :])
                dve.scalar_tensor_tensor(us[par][:, 1], uraw[par][:], SPLIT, us[par][:, 0], ALU.mult, ALU.subtract)
                dve.scalar_tensor_tensor(dsp[par][:, 1], draw[par][:], SPLIT, dsp[par][:, 0],
                                         ALU.mult, ALU.subtract).then_inc(w_split, 1)
                dve.wait_ge(w_split, 2 + e + 1)

            def hidden(e, c, m):
                n = (e * CHUNKS + c) * M + m
                dve.wait_ge(h_gelu, RING + n + 1)
                dve.tensor_scalar(hs[c % 2][:, 0, m, :], hf[m % RING][:], SPLIT, None, ALU.mult).then_inc(h_hi, 1)
                dve.wait_ge(h_hi, n + 1)
                dve.scalar_tensor_tensor(hs[c % 2][:, 1, m, :], hf[m % RING][:], SPLIT, hs[c % 2][:, 0, m, :],
                                         ALU.mult, ALU.subtract).then_inc(h_done, 1)

            def add(e, par, c):
                for ti in range(TPC):
                    n = (e * CHUNKS + c) * TPC + ti
                    tile = TPC * c + ti
                    dve.wait_ge(y_ready, n + 1)
                    dve.wait_ge(y_done, n + 1)
                    ins = dve.scalar_tensor_tensor(s.x[:, tile, :], Y(ti), cwe[par][:, tile:tile + 1], s.x[:, tile, :],
                                                   ALU.mult, ALU.add)
                    ins.then_inc(y_done, 1)

            def expert(e, par, last=False):
                for c in range(CHUNKS):
                    if c + 1 < CHUNKS:
                        for m in range(M):
                            hidden(e, c + 1, m)
                    elif not last:
                        for m in range(M):
                            hidden(e + 1, 0, m)
                    add(e, par, c)
                    if c == 1 and not last:
                        split(e + 1, 1 - par)
                dve.wait_ge(y_done, RING + (e + 1) * TILES)
                dve.sem_inc(w_free, 1)

            split(0, 0)
            for m in range(M):
                hidden(0, 0, m)
            with dve.Fori(0, E1 // 2 - 1) as i:
                for par in range(2):
                    expert(2 * i + par, par)
            expert(E1 - 2, 0)
            expert(E1 - 1, 1, last=True)

OUTPUTS = {"out": ((B, SQ, D), F32)}


def build(nc, a, out):
    s = Store()
    with ExitStack() as ctx:
        sb = lambda name, shape, dt=F32: ctx.enter_context(nc.sbuf_tensor(name, shape, dt))
        s.x = sb("x", [P, TILES, D])
        s.w0 = [sb(f"w0_{n}", [P, 2, C, D], F16) for n in "qkvo"]
        s.w1 = [sb(f"w1_{n}", [P, 2, C, D], F16) for n in "qkvo"]
        s.fq, s.fk = sb("fq", [P, 2, C, H * DH], F16), sb("fk", [P, 2, C, H * DH], F16)
        s.fv = sb("fv", [P, 2, C, E0 * DH], F16)
        s.fg = sb("fg", [P, 2, C, 2 * H * E0], F16)
        s.fo = sb("fo", [P, 2, E0 // 2, D], F16)
        s.wg = sb("wg", [P, 2, C, E1], F16)
        s.ident = sb("ident", [P, P])
        s.head_of = sb("head_of", [P, 8])
        s.stage_step = [ctx.enter_context(nc.semaphore(f"stage_step{i}")) for i in range(3)]
        s.rank = sb("rank", [P, E1])
        s.zrow = sb("zrow", [P, 1])
        s.bqk = sb("bqk", [P, 8])
        s.bup = sb("bup", [P, E1, HID // P])
        s.bv, s.bo = sb("bv", [P, 2, D]), sb("bo", [P, 2, D])
        s.bdown = sb("bdown", [E1, D])
        s.causal = sb("causal", [P, TPB, SK])
        s.tg, s.tgu = sb("tg", [P, 4]), sb("tgu", [P, 4])
        s.mv, s.mvs, s.bn = sb("mv", [P, TILES, 2]), sb("mvs", [P, 2]), sb("bn", [P, 6])
        s.xs = sb("xs", [P, D])
        s.var, s.nt, s.rstd = sb("var", [P, TILES]), sb("nt", [P, TILES]), sb("rstd", [P, TILES])
        setup_stage(nc, a, s)
        for stage in STAGES:
            if stage in (0, 1):
                xattn_stage(nc, a, s, stage)
            elif stage == "ffn":
                ffn_stage(nc, a, s)
            elif stage == "moe":
                moe_stage(nc, a, s, out)
            else:
                store_stage(nc, a, s, out)


def store_stage(nc, a, s, out):
    with ExitStack() as ctx:
        done = ctx.enter_context(nc.semaphore("out_stored"))
        block = ctx.enter_context(nc.Block())

        @block.sync
        def _(sp):
            sp.dma_start(out.rearrange("b (t p) d -> p (b t) d", p=P), s.x[:]).then_inc(done, 16)
            sp.wait_ge(done, 16)


STAGES = (0, "ffn", 1, "moe")

_INS = ['x', 'ctx_1024', 'mask_Bx1xS2_bk0', 'mask_SxS2_fk0', 'mask_BxS2_bf0', 'g_xattn', 'g_ffn',
        'L0_xattn_Wq', 'L0_xattn_bq', 'L0_xattn_Wk', 'L0_xattn_bk', 'L0_xattn_Wv', 'L0_xattn_bv',
        'L0_xattn_Wo', 'L0_xattn_bo', 'L0_ffn_Wq', 'L0_ffn_Wk', 'L0_ffn_Wv', 'L0_ffn_Ws', 'L0_ffn_Wd',
        'L0_ffn_Wo', 'L1_xattn_W_q', 'L1_xattn_b_q', 'L1_xattn_W_k', 'L1_xattn_b_k', 'L1_xattn_W_v',
        'L1_xattn_b_v', 'L1_xattn_W_o', 'L1_xattn_b_o', 'L1_ffn_Wg', 'L1_ffn_Wup', 'L1_ffn_bup',
        'L1_ffn_Wdown', 'L1_ffn_bdown']


def kernel(**inputs):
    import numpy as _np
    import concourse.bacc as _bacc
    from concourse import mybir as _mybir
    from concourse.bass_utils import run_bass_kernel_spmd as _run

    nc = _bacc.Bacc("TRN2", target_bir_lowering=False, num_devices=1)
    arrays, drams = {}, {}
    for name in _INS:
        v = _np.ascontiguousarray(inputs[name])
        arrays[f"in_{name}"] = v
        drams[name] = nc.dram_tensor(f"in_{name}", v.shape, _mybir.dt.from_np(v.dtype), kind="ExternalInput").ap()
    out = nc.dram_tensor("out_0", (B, SQ, D), F32, kind="ExternalOutput").ap()
    build(nc, drams, out)
    r = _run(nc, [arrays], core_ids=[0])
    return r.results[0]["out_0"]
```

```python
from contextlib import ExitStack

import numpy as np

import concourse.bass as bass
from concourse import mybir
from concourse.alu_op_type import AluOpType as ALU

ACT = mybir.ActivationFunctionType
AX_X = mybir.AxisListType.X
F32 = mybir.dt.float32
F16 = mybir.dt.float16
I32 = mybir.dt.int32
U8 = mybir.dt.uint8

P = 128
SPLIT = 64.0
UNSPLIT = 1.0 / SPLIT ** 2
NEG = -1.0e9
MASKED = -1.0e30
EPS = 1e-5
RSQRT_SEED = float(0x5F3759DF)
NEWTON_STEPS = 3

B, SQ, D = 8, 256, 256
SK = 120
H = 16
DK = D // H
DH = 64
E0 = 8
E1, TOP1, HID = 12, 3, 1024
TILES = B * SQ // P
TPB = SQ // P
C = D // P


class Chain:

    def __init__(self, eng, sem, per=0, turn=0):
        self.eng, self.sem, self.base, self.per, self.n = eng, sem, turn * per, per, 0

    def count(self, instruction):
        self.n += 1
        instruction.then_inc(self.sem, 1)

    def __call__(self, instruction):
        self.count(instruction)
        self.eng.wait_ge(self.sem, self.base + self.n)

    def close(self):
        assert self.n == self.per, (self.n, self.per)


def bcast(ap, n):
    return ap.unsqueeze(2).to_broadcast([ap.shape[0], ap.shape[1], n])


def bcast_mid(ap, n):
    return ap.unsqueeze(1).to_broadcast([ap.shape[0], n, ap.shape[1]])


def matmul3(pe, out, terms):
    last = None
    for n, (lhs, rhs) in enumerate(terms):
        pe.matmul(out, lhs[0], rhs[0], start=(n == 0), stop=False)
        pe.matmul(out, lhs[0], rhs[1], start=False, stop=False)
        last = pe.matmul(out, lhs[1], rhs[0], start=False, stop=(n == len(terms) - 1))
    return last


def rsqrt_all(dve, chain, s):
    chain(dve.tensor_scalar(s.var[:], s.mv[:, :, 1], EPS, None, ALU.add))
    chain(dve.tensor_scalar(s.nt[:].bitcast(I32), s.var[:].bitcast(I32), 1, None, ALU.logical_shift_right))
    chain(dve.tensor_scalar(s.rstd[:].bitcast(I32), s.nt[:].bitcast(I32), -1.0, RSQRT_SEED, ALU.mult, ALU.add))
    for _ in range(NEWTON_STEPS):
        chain(dve.tensor_tensor(s.nt[:], s.rstd[:], s.rstd[:], ALU.mult))
        chain(dve.scalar_tensor_tensor(s.nt[:], s.nt[:], -0.5, s.var[:], ALU.mult, ALU.mult))
        chain(dve.scalar_tensor_tensor(s.rstd[:], s.nt[:], 1.5, s.rstd[:], ALU.add, ALU.mult))


def keep_tile(dve, chain, s, tile):
    one = bass.ds(tile, 1)
    chain(dve.bn_stats(s.bn[:], s.xs[:]))
    chain.count(dve.tensor_scalar(s.x[:, one, :], s.xs[:].unsqueeze(1), 1.0, None, ALU.mult))
    chain(dve.bn_aggr(s.mvs[:], s.bn[:]))
    return dve.tensor_scalar(s.mv[:, one, :], s.mvs[:].unsqueeze(1), 1.0, None, ALU.mult)


def tile_stats(dve, chain, s, tile):
    chain(dve.bn_stats(s.bn[:], s.x[:, tile, :]))
    chain(dve.bn_aggr(s.mv[:, tile, :], s.bn[:]))


class Store:
    pass


SMALL_LOADS = 13
SETUP_BANKS = 4
STRAIGHT_AFTER = 11


def setup_stage(nc, a, s):
    with ExitStack() as ctx:
        sb = lambda name, shape, dt=F32: ctx.enter_context(nc.sbuf_tensor(name, shape, dt))
        sem = lambda name: ctx.enter_context(nc.semaphore(name))
        raw0 = [sb(f"raw0_{n}", [P, C, D]) for n in "qkvo"]
        raw1 = [sb(f"raw1_{n}", [P, C, D]) for n in "qkvo"]
        rawq, rawk = sb("rawq", [P, 8, D]), sb("rawk", [P, 8, D])
        rawv = sb("rawv", [P, 4, D])
        rawg = sb("rawg", [P, 2, D])
        rawo = sb("rawo", [P, C, E0, DH])
        rows = sb("bias_rows", [8, P])
        rowsu = sb("bup_rows", [E1 * 8, P])
        rawwg = sb("rawwg", [P, C, E1])
        gates = sb("gates_raw", [P, 4])
        ps = ctx.enter_context(nc.psum_tensor("setup_psum", [P, SETUP_BANKS + 1, 512], F32))
        x_loaded = [sem(f"x_loaded{i}") for i in range(2)]
        w_loaded = [sem(f"w_loaded{i}") for i in range(8)]
        small_loaded = sem("small_loaded")
        ident_made, transposed, hi_made, bank_done = (
            sem("ident_made"), sem("setup_transposed"), sem("setup_hi"), sem("setup_done"))
        dve_step, act_step, pool_step, tanh_done = (
            sem("setup_dve_step"), sem("setup_act_step"), sem("setup_pool_step"), sem("tanh_done"))
        block = ctx.enter_context(nc.Block())

        groups = []
        for n in range(4):
            groups.append(([raw1[n][:, o, c * P:(c + 1) * P] for c in range(C) for o in range(C)],
                           [s.w1[n][:, hl] for hl in range(2)], 0))
        for raw, dst, load in ((rawq, s.fq, 1), (rawk, s.fk, 2)):
            for c in range(C):
                for og in range(2):
                    groups.append(([raw[:, og * 4 + o, c * P:(c + 1) * P] for o in range(4)],
                                   [dst[:, hl, c, og * 512:(og + 1) * 512] for hl in range(2)], load))
        for c in range(C):
            groups.append(([rawv[:, o, c * P:(c + 1) * P] for o in range(4)],
                           [s.fv[:, hl, c, :] for hl in range(2)], 3))
        groups.append(([rawg[:, o, c * P:(c + 1) * P] for c in range(C) for o in range(2)],
                       [s.fg[:, hl] for hl in range(2)], 4))
        for half in range(2):
            groups.append(([rawo[:, fc, 2 * ec:2 * ec + 2, :].rearrange("p e d -> p (e d)")
                            for ec in (2 * half, 2 * half + 1) for fc in range(C)],
                           [s.fo[:, hl, 2 * half:2 * half + 2, :] for hl in range(2)], 5))
        flat = lambda ap: ap.rearrange("p a b -> p (a b)") if len(ap.shape) == 3 else ap

        @block.sync
        def _(sp):
            x = a["x"].rearrange("b (t p) d -> p (b t) d", p=P)
            n = TILES // 2
            for i in range(2):
                sp.dma_start(s.x[:, n * i:n * i + n, :], x[:, n * i:n * i + n, :]).then_inc(x_loaded[i], 16)
            for n, k in enumerate(("Wq", "Wk", "Wv", "Wo")):
                sp.dma_start(raw0[n][:], a["L0_xattn_" + k].rearrange("(c p) o -> p c o", p=P)).then_inc(w_loaded[6], 16)
            sp.dma_start(rawwg[:], a["L1_ffn_Wg"].rearrange("(c p) o -> p c o", p=P)).then_inc(w_loaded[7], 16)
            sp.wait_ge(w_loaded[6], 64)

        @block.scalar
        def _(act):
            for n, k in enumerate(("W_q", "W_k", "W_v", "W_o")):
                act.dma_start(raw1[n][:], a["L1_xattn_" + k].rearrange("(o p) i -> p o i", p=P)).then_inc(w_loaded[0], 16)
            act.dma_start(rawq[:], a["L0_ffn_Wq"].rearrange("(g h) d c -> (h d) g c", h=2)).then_inc(w_loaded[1], 16)
            act.dma_start(rawk[:], a["L0_ffn_Wk"].rearrange("(g h) d c -> (h d) g c", h=2)).then_inc(w_loaded[2], 16)
            act.dma_start(rawv[:], a["L0_ffn_Wv"].rearrange("(g h) d c -> (h d) g c", h=2)).then_inc(w_loaded[3], 16)
            act.dma_start(rawg[:, 0, :], a["L0_ffn_Ws"].rearrange("h e c -> (h e) c")).then_inc(w_loaded[4], 16)
            act.dma_start(rawg[:, 1, :], a["L0_ffn_Wd"].rearrange("h e c -> (h e) c")).then_inc(w_loaded[4], 16)
            act.dma_start(rawo[:, 0], a["L0_ffn_Wo"][:, 0:P, :].rearrange("e p d -> p e d")).then_inc(w_loaded[5], 16)
            act.dma_start(rawo[:, 1], a["L0_ffn_Wo"][:, P:2 * P, :].rearrange("e p d -> p e d")).then_inc(w_loaded[5], 16)
            for g, (_, dst, _) in enumerate(groups):
                act.wait_ge(transposed, g + 1)
                act.activation(flat(dst[0]), ps[:, g % SETUP_BANKS, :], ACT.Copy, scale=SPLIT).then_inc(hi_made, 1)
                if g == STRAIGHT_AFTER:
                    act.wait_ge(w_loaded[6], 64)
                    for n in range(4):
                        act.activation(s.w0[n][:, 0], raw0[n][:], ACT.Copy, scale=SPLIT).then_inc(act_step, 1)
                    act.wait_ge(w_loaded[7], 16)
                    act.activation(s.wg[:, 0], rawwg[:], ACT.Copy, scale=SPLIT).then_inc(act_step, 1)
            act.wait_ge(small_loaded, 16 * SMALL_LOADS)
            act.activation(s.tg[:], gates[:], ACT.Tanh).then_inc(tanh_done, 1)

        @block.gpsimd
        def _(pool):
            chain = Chain(pool, pool_step)
            chain(pool.memset(s.ident[:], 0.0))
            pool.affine_select(out=s.ident[:], in_=s.ident[:], compare_op=ALU.not_equal, fill=1.0, base=0,
                               pattern=[[-1, P]], channel_multiplier=1).then_inc(ident_made, 1)
            chain(pool.memset(s.head_of[:], 1.0))
            chain(pool.affine_select(out=s.head_of[:], in_=s.head_of[:], compare_op=ALU.is_ge, fill=0.0, base=0,
                                     pattern=[[-DK, 8]], channel_multiplier=1))
            chain(pool.affine_select(out=s.head_of[:], in_=s.head_of[:], compare_op=ALU.is_ge, fill=0.0, base=DK - 1,
                                     pattern=[[DK, 8]], channel_multiplier=-1))
            b2 = lambda k: a[k].rearrange("(m p) -> m p", p=P)
            for n, k in enumerate(("L0_xattn_bq", "L0_xattn_bk", "L1_xattn_b_q", "L1_xattn_b_k")):
                pool.dma_start(rows[2 * n:2 * n + 2, :], b2(k)).then_inc(small_loaded, 16)
            row = lambda k: a[k].rearrange("(o n) -> o n", o=1)
            for n, k in enumerate(("L0_xattn_bv", "L1_xattn_b_v")):
                pool.dma_start(s.bv[:, n, :], row(k).partition_broadcast(P)).then_inc(small_loaded, 16)
            for n, k in enumerate(("L0_xattn_bo", "L1_xattn_b_o")):
                pool.dma_start(s.bo[:, n, :], row(k).partition_broadcast(P)).then_inc(small_loaded, 16)
            pool.dma_start(gates[:, 0:2], row("g_xattn").partition_broadcast(P)).then_inc(small_loaded, 16)
            pool.dma_start(gates[:, 2:4], row("g_ffn").partition_broadcast(P)).then_inc(small_loaded, 16)
            pool.dma_start(rowsu[:], a["L1_ffn_bup"].rearrange("e (m p) -> (e m) p", p=P)).then_inc(small_loaded, 16)
            pool.dma_start(s.bdown[:], a["L1_ffn_bdown"]).then_inc(small_loaded, 16)
            pool.dma_start(s.causal[:], a["mask_SxS2_fk0"].rearrange("(t p) k -> p t k", p=P)).then_inc(small_loaded, 16)

        @block.tensor
        def _(pe):
            pe.wait_ge(ident_made, 1)
            for g, (src, _, load) in enumerate(groups):
                pe.wait_ge(w_loaded[load], 16 * (4, 1, 1, 1, 2, 2)[load])
                if g >= SETUP_BANKS:
                    pe.wait_ge(bank_done, g - SETUP_BANKS + 1)
                for j in range(4):
                    last = pe.transpose(ps[:, g % SETUP_BANKS, j * P:(j + 1) * P], src[j], s.ident[:])
                last.then_inc(transposed, 1)
            pe.wait_ge(small_loaded, 16 * SMALL_LOADS)
            pe.transpose(ps[:, SETUP_BANKS, 0:8], rows[:], s.ident[0:8, 0:8])
            pe.transpose(ps[:, SETUP_BANKS, 8:8 + E1 * 8], rowsu[:], s.ident[0:E1 * 8, 0:E1 * 8]).then_inc(transposed, 1)

        @block.vector
        def _(dve):
            chain = Chain(dve, dve_step)
            for e in range(E1):
                dve.memset(s.rank[:, e:e + 1], float(E1 - e))
            for g, (_, dst, _) in enumerate(groups):
                if g < TILES:
                    if g % (TILES // 2) == 0:
                        dve.wait_ge(x_loaded[g // (TILES // 2)], 16)
                    tile_stats(dve, chain, s, g)
                dve.wait_ge(hi_made, g + 1)
                dve.scalar_tensor_tensor(flat(dst[1]), ps[:, g % SETUP_BANKS, :], SPLIT, flat(dst[0]),
                                         ALU.mult, ALU.subtract).then_inc(bank_done, 1)
                if g == STRAIGHT_AFTER + 1:
                    for n in range(4):
                        dve.wait_ge(act_step, n + 1)
                        dve.scalar_tensor_tensor(s.w0[n][:, 1], raw0[n][:], SPLIT, s.w0[n][:, 0], ALU.mult, ALU.subtract)
                    dve.wait_ge(act_step, 5)
                    dve.scalar_tensor_tensor(s.wg[:, 1], rawwg[:], SPLIT, s.wg[:, 0], ALU.mult, ALU.subtract)
            dve.wait_ge(transposed, len(groups) + 1)
            dve.tensor_scalar(s.bqk[:], ps[:, SETUP_BANKS, 0:8], SPLIT, None, ALU.mult)
            dve.tensor_copy(s.bup[:], ps[:, SETUP_BANKS, 8:8 + E1 * 8].rearrange("p (e m) -> p e m", e=E1))
            dve.wait_ge(tanh_done, 1)
            dve.tensor_scalar(s.tgu[:], s.tg[:], UNSPLIT, None, ALU.mult)
            for n in range(2):
                dve.tensor_scalar(s.bv[:, n, :], s.bv[:, n, :], SPLIT, None, ALU.mult)
                dve.tensor_scalar(s.bo[:, n, :], s.bo[:, n, :], s.tg[:, n:n + 1], None, ALU.mult)
            rsqrt_all(dve, chain, s)


def run_slots(eng, slot, drains):
    slot(0, 0, 0)
    slot(1, 0, 1)
    with eng.Fori(1, B // 2 - 1) as i:
        slot(2 * i, i, 0)
        slot(2 * i + 1, i, 1)
    slot(B - 2, B // 2 - 1, 0)
    slot(B - 1, B // 2 - 1, 1)
    for k in range(drains):
        slot(B + k, B // 2 + k // 2, k % 2)


def within(b, lo, hi=B):
    return not isinstance(b, int) or lo <= b < hi


def has_next(b):
    return within(b, 0, B - 1)


XN_T, CTX_T, Q_T, K_T, V_ = range(5)
XA_FRONT = 5
XA_FRONT_CREDIT = 1
XA_ACT = (XN_T, CTX_T, Q_T, K_T)
XA_LAG = 3
XA_UNITS = 8
HG = 4
BACK = 2 * TPB


def xattn_stage(nc, a, s, layer):
    t = f"x{layer}_"
    w = (s.w0, s.w1)[layer]
    with ExitStack() as ctx:
        sb = lambda name, shape, dt=F32: ctx.enter_context(nc.sbuf_tensor(t + name, shape, dt))
        sem = lambda name: ctx.enter_context(nc.semaphore(t + name))
        two = lambda name, shape, dt=F32: [sb(f"{name}{i}", shape, dt) for i in range(2)]
        c_in = two("ctx", [SK, D])
        m_in = two("mask", [P, SK], U8)
        xn = two("xn", [P, TPB, D])
        xt = two("xt", [P, 2, C, SQ], F16)
        ct = two("ct", [P, 2, C, SK], F16)
        qf, kf = two("qf", [P, C, SQ]), two("kf", [P, C, SK])
        qt = two("qt", [P, 2, C, SQ], F16)
        ks = two("ks", [P, 2, C, SK], F16)
        km = two("km", [P, 2, C, 8, SK], F16)
        vf = two("vf", [SK, D])
        va = two("va", [SK, 2, H, DK + 1], F16)
        mf = two("mf", [P, SK])
        add = two("add", [P, TPB, SK])
        keep = two("keep", [P, SK])
        live = two("live", [P, 1])
        sc = two("sc", [P, HG, SK])
        mx = two("mx", [P, HG])
        pr = two("pr", [P, HG, SK])
        pt = two("pt", [SK, 2, HG, P], F16)
        rs = sb("rs", [P, TPB, H])
        cn = sb("cn", [P, TPB, D])
        cnt = sb("cnt", [P, TPB, 2, C, P], F16)
        zeros = sb("zeros", [P, D])
        ps = ctx.enter_context(nc.psum_tensor(t + "ps", [P, 8, 512], F32))
        front, back = ps[:, 0, :], ps[:, 1, :]
        S = lambda u: ps[:, 2 + u % 2, 0:HG * SK].rearrange("p (h k) -> p h k", h=HG)
        PT = lambda u: ps[0:SK, 4 + u % 2, :].rearrange("p (h q) -> p h q", h=HG)
        O = lambda ti: ps[:, 6 + ti, 0:H * (DK + 1)].rearrange("p (h d) -> p h d", h=H)

        loaded = [sem("loaded0"), sem("loaded1")]
        load_free = sem("load_free")
        xn_ready = sem("xn_ready")
        front_ready = sem("front_ready")
        act_front = sem("act_front")
        front_done = sem("front_done")
        km_ready = sem("km_ready")
        s_ready = sem("s_ready")
        s_max = sem("s_max")
        shifted = sem("shifted")
        p_ready = sem("p_ready")
        pt_ready = sem("pt_ready")
        pt_hi = sem("pt_hi")
        pt_done = sem("pt_done")
        pv_done = sem("pv_done")
        o_done = sem("o_done")
        back_ready = sem("back_ready")
        act_back = sem("act_back")
        back_done = sem("back_done")
        ones_set = sem("ones_set")
        rows_zeroed = sem("rows_zeroed")
        front_step, core_step, back_step = sem("front_step"), sem("core_step"), sem("back_step")
        block = ctx.enter_context(nc.Block())

        def earlier(b, par, u, lag, do):
            if u >= lag and within(b, 0):
                do(b, par, u - lag)
            elif u < lag and within(b, 1, B + 1):
                do(b - 1, 1 - par, u - lag + XA_UNITS)

        @block.sync
        def _(sp):
            masks = (a["mask_Bx1xS2_bk0"].rearrange("b o k -> b (o k)"), a["mask_BxS2_bf0"])[layer]
            with sp.Fori(0, B // 2) as i:
                for par in range(2):
                    b = 2 * i + par
                    sp.wait_ge(load_free, b + 1)
                    sp.dma_start(c_in[par][:], a["ctx_1024"][bass.ds(b, 1)].rearrange("o k d -> (o k) d")).then_inc(loaded[par], 16)
                    sp.dma_start(m_in[par][:], masks[bass.ds(b, 1), :].partition_broadcast(P)).then_inc(loaded[par], 16)
            if layer == 1:
                sp.wait_ge(ones_set, 5)
                sp.dma_start(s.rows_in.rearrange("(n p) d -> p n d", p=P), bcast_mid(zeros[:], NB * TPB)).then_inc(rows_zeroed, 16)
                sp.wait_ge(rows_zeroed, 16)

        @block.gpsimd
        def _(pool):
            chain = Chain(pool, ones_set)
            for par in range(2):
                chain(pool.memset(va[par][:, 0, :, DK:DK + 1], 1.0))
                chain(pool.memset(va[par][:, 1, :, DK:DK + 1], 0.0))
            chain(pool.memset(zeros[:], 0.0))
            with pool.Fori(0, B) as b:
                for u in range(XA_UNITS):
                    n = XA_UNITS * b + u
                    pool.wait_ge(s_max, 2 + n + 1)
                    pool.tensor_tensor(sc[u % 2][:], sc[u % 2][:], bcast(mx[u % 2][:], SK),
                                       ALU.subtract).then_inc(shifted, 1)

        @block.scalar
        def _(act):
            act.sem_inc(p_ready, 2)

            def evacuate(b, par, j):
                act.wait_ge(front_ready, XA_FRONT * b + j + 1)
                if j == XN_T:
                    ins = act.activation(xt[par][:, 0].rearrange("p c q -> p (c q)"), front, ACT.Copy, scale=SPLIT)
                elif j == CTX_T:
                    ins = act.activation(ct[par][:, 0].rearrange("p c k -> p (c k)"), front[:, 0:C * SK], ACT.Copy, scale=SPLIT)
                else:
                    dst, n, col = (qf[par], SQ, 4 * layer) if j == Q_T else (kf[par], SK, 4 * layer + 2)
                    outs = (dst, qt[par][:, 0]) if j == Q_T else (dst,)
                    for to in outs:
                        for m in range(C):
                            ins = act.activation(to[:, m, :], front[:, m * n:(m + 1) * n], ACT.Identity,
                                                 bias=s.bqk[:, col + m:col + m + 1], scale=1.0 / SPLIT)
                ins.then_inc(act_front, 1)

            def spread_keys(b, par, part):
                if part == 0:
                    act.wait_ge(front_done, XA_FRONT_CREDIT + XA_FRONT * b + K_T + 1)
                for h in range(HG * part, HG * part + HG):
                    ins = act.activation(km[par][:].rearrange("p l m h k -> p (l m) h k")[:, :, h, :],
                                         ks[par][:].rearrange("p l m k -> p (l m) k"), ACT.Copy, scale=s.head_of[:, h:h + 1])
                ins.then_inc(km_ready, 1)

            def exps(b, u):
                n = XA_UNITS * b + u
                act.wait_ge(shifted, n + 1)
                act.wait_ge(pt_ready, n + 1)
                act.activation(pr[u % 2][:], sc[u % 2][:], ACT.Exp).then_inc(p_ready, 1)

            def pt_part(b, par, u):
                act.wait_ge(pt_ready, 2 + XA_UNITS * b + u + 1)
                act.wait_ge(pv_done, XA_UNITS * b + u + 1)
                act.activation(pt[u % 2][:, 0], PT(u), ACT.Copy, scale=SPLIT).then_inc(pt_hi, 1)

            def back_hi(b, ti):
                act.wait_ge(back_ready, BACK * b + 2 * ti + 1)
                act.wait_ge(back_done, BACK * b + 2 * ti + 2)
                act.activation(cnt[:, ti, 0], back[:, 0:D].rearrange("p (c q) -> p c q", c=C),
                               ACT.Copy).then_inc(act_back, 1)

            for j in XA_ACT:
                evacuate(0, 0, j)
            for part in range(2):
                spread_keys(0, 0, part)

            def slot(b, half, par):
                for u in range(XA_UNITS):
                    earlier(b, par, u, XA_LAG - 1, pt_part)
                    if has_next(b) and u - 1 in XA_ACT:
                        evacuate(b + 1, 1 - par, u - 1)
                    if within(b, 1, B + 1):
                        if u == 0:
                            back_hi(b - 1, 0)
                        if u == 4:
                            back_hi(b - 1, 1)
                    if within(b, 0):
                        exps(b, u)
                    if has_next(b) and u in (5, 6):
                        spread_keys(b + 1, 1 - par, u - 5)

            run_slots(act, slot, 1)

        @block.tensor
        def _(pe):
            pe.sem_inc(pt_ready, 2)
            pe.sem_inc(pv_done, 2)
            pair = lambda ap, c, lo, n: tuple(ap[:, hl, c, lo:lo + n] for hl in range(2))

            def project(b, half, par, j):
                pe.wait_ge(front_done, XA_FRONT * b + j + 1)
                if j == XN_T:
                    pe.wait_ge(xn_ready, b + 1)
                    for c in range(C):
                        for ti in range(TPB):
                            last = pe.transpose(front[:, c * SQ + ti * P:c * SQ + (ti + 1) * P],
                                                xn[par][:, ti, c * P:(c + 1) * P], s.ident[:])
                elif j == CTX_T:
                    pe.wait_ge(loaded[par], 32 * (half + 1))
                    for c in range(C):
                        last = pe.transpose(front[:, c * SK:(c + 1) * SK], c_in[par][:, c * P:(c + 1) * P],
                                            s.ident[0:SK, 0:SK])
                elif j == V_:
                    last = matmul3(pe, front[0:SK, 0:D], [(pair(ct[par], c, 0, SK), pair(w[2], c, 0, D)) for c in range(C)])
                else:
                    wj, src, n = (w[0], xt[par], SQ) if j == Q_T else (w[1], ct[par], SK)
                    for m in range(C):
                        last = matmul3(pe, front[:, m * n:(m + 1) * n],
                                       [(pair(wj, c, m * P, P), pair(src, c, 0, n)) for c in range(C)])
                last.then_inc(front_ready, 1)

            def score(b, par, u):
                if u < 2:
                    pe.wait_ge(km_ready, 2 * b + u + 1)
                pe.wait_ge(s_max, XA_UNITS * b + u + 1)
                ti, m, h0 = u // 4, (u % 4) // 2, HG * (u % 2)
                matmul3(pe, S(u), [(pair(qt[par], m, ti * P, P),
                                    tuple(km[par][:, hl, m, h0:h0 + HG, :] for hl in range(2)))]).then_inc(s_ready, 1)

            def transposes(b, par, u):
                n = XA_UNITS * b + u
                pe.wait_ge(p_ready, 2 + n + 1)
                pe.wait_ge(pt_done, n + 1)
                for h in range(HG):
                    last = pe.transpose(PT(u)[:, h, :], pr[u % 2][:, h, :], s.ident[:])
                last.then_inc(pt_ready, 1)

            def times_v(b, par, u):
                ti = u // 4
                if u % 4 == 0:
                    pe.wait_ge(o_done, TPB * b + ti + 1)
                pe.wait_ge(pt_done, 2 + XA_UNITS * b + u + 1)
                for h in range(HG):
                    head = HG * (u % 4) + h
                    last = matmul3(pe, O(ti)[:, head, :],
                                   [(tuple(pt[u % 2][:, hl, h, :] for hl in range(2)),
                                     tuple(va[par][:, hl, head, :] for hl in range(2)))])
                last.then_inc(pv_done, 1)

            def back_transposes(b, ti):
                pe.wait_ge(back_done, BACK + BACK * b + 2 * ti)
                pe.wait_ge(o_done, 2 + TPB * b + ti + 1)
                for c in range(C):
                    last = pe.transpose(back[:, c * P:(c + 1) * P], cn[:, ti, c * P:(c + 1) * P], s.ident[:])
                last.then_inc(back_ready, 1)

            def back_product(b, ti):
                pe.wait_ge(back_done, BACK + BACK * b + 2 * ti + 1)
                matmul3(pe, back[:, 0:D],
                        [(tuple(cnt[:, ti, hl, c, :] for hl in range(2)), tuple(w[3][:, hl, c, :] for hl in range(2)))
                         for c in range(C)]).then_inc(back_ready, 1)

            for j in range(XA_FRONT):
                project(0, 0, 0, j)
            pe.wait_ge(ones_set, 4)
            score(0, 0, 0)
            score(0, 0, 1)

            def slot(b, half, par):
                for u in range(XA_UNITS):
                    earlier(b, par, u, 1, transposes)
                    if within(b, 0) and u + 2 < XA_UNITS:
                        score(b, par, u + 2)
                    elif has_next(b) and u + 2 >= XA_UNITS:
                        score(b + 1, 1 - par, u + 2 - XA_UNITS)
                    earlier(b, par, u, XA_LAG, times_v)
                    if has_next(b) and u < XA_FRONT:
                        project(b + 1, half + par, 1 - par, u)
                    if within(b, 1, B + 1):
                        if u == 0:
                            back_product(b - 1, 0)
                        if u == 3:
                            back_transposes(b - 1, 1)
                        if u == 4:
                            back_product(b - 1, 1)
                    if u == 7 and within(b, 0):
                        back_transposes(b, 0)

            run_slots(pe, slot, 1)

        @block.vector
        def _(dve):
            dve.sem_inc(front_done, XA_FRONT_CREDIT)
            dve.sem_inc(load_free, 2)
            dve.sem_inc(s_max, 2)
            dve.sem_inc(pt_done, 2)
            dve.sem_inc(o_done, 2)
            dve.sem_inc(back_done, BACK)
            for par in range(2):
                dve.memset(live[par][:], 1.0)

            def normalised_x(b, par):
                for ti in range(TPB):
                    tile = bass.ds(TPB * b + ti, 1)
                    ins = dve.tensor_scalar(xn[par][:, ti, :], s.x[:, tile, :], s.mv[:, tile, 0], s.rstd[:, tile],
                                            ALU.subtract, ALU.mult)
                ins.then_inc(xn_ready, 1)

            def masks(half, par, chain):
                dve.wait_ge(loaded[par], 32 * (half + 1))
                chain(dve.tensor_copy(mf[par][:], m_in[par][:]))
                if layer == 0:
                    for ti in range(TPB):
                        chain(dve.tensor_scalar(add[par][:, ti, :], mf[par][:], MASKED, None, ALU.mult))
                else:
                    chain(dve.tensor_scalar(keep[par][:], mf[par][:], -1.0, 1.0, ALU.mult, ALU.add))
                    for ti in range(TPB):
                        chain(dve.scalar_tensor_tensor(add[par][:, ti, :], mf[par][:], NEG, s.causal[:, ti, :],
                                                       ALU.mult, ALU.add))

            def find_live(par, chain):
                if layer == 0:
                    chain(dve.tensor_reduce(live[par][:], mf[par][:], AX_X, ALU.min))
                    chain(dve.tensor_scalar(live[par][:], live[par][:], -1.0, 1.0, ALU.mult, ALU.add))

            def evacuate(b, par, j, chain):
                if j in XA_ACT:
                    dve.wait_ge(act_front, len(XA_ACT) * b + XA_ACT.index(j) + 1)
                if j == XN_T:
                    dve.scalar_tensor_tensor(xt[par][:, 1].rearrange("p c q -> p (c q)"), front, SPLIT,
                                             xt[par][:, 0].rearrange("p c q -> p (c q)"),
                                             ALU.mult, ALU.subtract).then_inc(front_done, 1)
                elif j == CTX_T:
                    dve.scalar_tensor_tensor(ct[par][:, 1].rearrange("p c k -> p (c k)"), front[:, 0:C * SK], SPLIT,
                                             ct[par][:, 0].rearrange("p c k -> p (c k)"),
                                             ALU.mult, ALU.subtract).then_inc(front_done, 1)
                    dve.sem_inc(load_free, 1)
                elif j == Q_T:
                    dve.tensor_tensor(qt[par][:, 1], qf[par][:], qt[par][:, 0], ALU.subtract).then_inc(front_done, 1)
                elif j == K_T:
                    if layer == 1:
                        chain(dve.tensor_tensor(kf[par][:], kf[par][:], bcast_mid(keep[par][:], C), ALU.mult))
                    chain(dve.tensor_copy(ks[par][:, 0], kf[par][:]))
                    dve.tensor_tensor(ks[par][:, 1], kf[par][:], ks[par][:, 0], ALU.subtract).then_inc(front_done, 1)
                else:
                    dve.wait_ge(front_ready, XA_FRONT * b + V_ + 1)
                    chain(dve.scalar_tensor_tensor(vf[par][:], front[0:SK, 0:D], 1.0 / SPLIT, s.bv[0:SK, layer, :],
                                                   ALU.mult, ALU.add))
                    v = vf[par][:].rearrange("k (h d) -> k h d", h=H)
                    chain(dve.tensor_copy(va[par][:, 0, :, 0:DK], v))
                    dve.tensor_tensor(va[par][:, 1, :, 0:DK], v, va[par][:, 0, :, 0:DK], ALU.subtract).then_inc(front_done, 1)

            def soft(b, par, u, chain):
                n = XA_UNITS * b + u
                dve.wait_ge(s_ready, n + 1)
                dve.wait_ge(p_ready, n + 1)
                chain(dve.scalar_tensor_tensor(sc[u % 2][:], S(u), UNSPLIT / DK ** 0.5,
                                               bcast_mid(add[par][:, u // 4, :], HG), ALU.mult, ALU.add))
                dve.tensor_reduce(mx[u % 2][:], sc[u % 2][:], AX_X, ALU.max).then_inc(s_max, 1)

            def pt_part(b, par, u):
                n = XA_UNITS * b + u
                dve.wait_ge(pt_hi, n + 1)
                dve.scalar_tensor_tensor(pt[u % 2][:, 1], PT(u), SPLIT, pt[u % 2][:, 0],
                                         ALU.mult, ALU.subtract).then_inc(pt_done, 1)

            def normalise(b, par, ti, chain):
                dve.wait_ge(pv_done, 2 + XA_UNITS * b + 4 * ti + 4)
                chain(dve.reciprocal(rs[:, ti, :], O(ti)[:, :, DK]))
                if layer == 0:
                    chain(dve.tensor_scalar(rs[:, ti, :], rs[:, ti, :], live[par][:], None, ALU.mult))
                dve.tensor_tensor(cn[:, ti, :].rearrange("p (h d) -> p h d", h=H), O(ti)[:, :, 0:DK],
                                  bcast(rs[:, ti, :], DK), ALU.mult).then_inc(o_done, 1)

            def back_lo(b, ti):
                dve.wait_ge(act_back, TPB * b + ti + 1)
                dve.tensor_tensor(cnt[:, ti, 1], back[:, 0:D].rearrange("p (c q) -> p c q", c=C), cnt[:, ti, 0],
                                  ALU.subtract).then_inc(back_done, 1)

            def update(b, ti, chain):
                j = BACK * b + 2 * ti + 1
                dve.wait_ge(back_ready, j + 1)
                dve.scalar_tensor_tensor(s.xs[:].unsqueeze(1), back[:, 0:D].unsqueeze(1), s.tgu[:, layer:layer + 1],
                                         s.x[:, bass.ds(TPB * b + ti, 1), :], ALU.mult, ALU.add).then_inc(back_done, 1)
                dve.wait_ge(back_done, BACK + j + 1)
                chain(dve.tensor_tensor(s.xs[:], s.xs[:], s.bo[:, layer, :], ALU.add))
                chain(keep_tile(dve, chain, s, TPB * b + ti))

            chain = Chain(dve, front_step)
            normalised_x(0, 0)
            masks(0, 0, chain)
            find_live(0, chain)
            for j in range(XA_FRONT):
                evacuate(0, 0, j, chain)

            def slot(b, half, par):
                front_chain = Chain(dve, front_step, XA_FRONT_LINKS[layer], b + 1)
                core_chain = Chain(dve, core_step, XA_UNITS, b)
                last_chain = Chain(dve, back_step, 2 * XA_BACK_LINKS[layer], b - 1)
                for u in range(XA_UNITS):
                    if within(b, 0):
                        soft(b, par, u, core_chain)
                    if u == 0 and has_next(b):
                        normalised_x(b + 1, 1 - par)
                        masks(half + par, 1 - par, front_chain)
                    earlier(b, par, u, XA_LAG - 1, pt_part)
                    if has_next(b) and 1 <= u <= XA_FRONT:
                        evacuate(b + 1, 1 - par, u - 1, front_chain)
                    if within(b, 1, B + 1):
                        if u == 0:
                            back_lo(b - 1, 0)
                        if u == 1:
                            last_chain.n = XA_NORM_LINKS[layer]
                            update(b - 1, 0, last_chain)
                        if u == 3:
                            normalise(b - 1, 1 - par, 1, last_chain)
                        if u == 4:
                            back_lo(b - 1, 1)
                        if u == 5:
                            update(b - 1, 1, last_chain)
                            last_chain.close()
                    if u == 7 and within(b, 0):
                        normalise(b, par, 0, Chain(dve, back_step, 2 * XA_BACK_LINKS[layer], b))
                if has_next(b):
                    find_live(1 - par, front_chain)
                    front_chain.close()

            run_slots(dve, slot, 1)
            rsqrt_all(dve, Chain(dve, s.stage_step[layer]), s)


XA_FRONT_LINKS = (8, 8)
XA_BACK_LINKS = (7, 6)
XA_NORM_LINKS = (2, 1)


F_XN, F_GATES, F_V, F_Q, F_K = 0, 1, 2, 4, 8
FF_FRONT = 12
FF_LAG = 3
FF_FRONT_CREDIT = 1
PARTS = TPB * E0
RING_PARTS = 4
Z_STEPS = {h: range(2 * (h - 4), 2 * (h - 4) + 2) for h in range(4, 8)}
V_STEPS = {h: range(3 * (h - 8), 3 * (h - 8) + 3) for h in range(8, 12)} | {12: range(12, 16)}
Z_STEPS |= {13: range(8, 11), 14: range(11, 14), 15: range(14, 16)}
FIRST_V_STEPS = {0: range(8, 12), 1: range(12, 16)}
GATES = 2 * H


def v_number(slot, n):
    if isinstance(slot, int) and slot <= 0:
        return PARTS * (slot + 1) + n
    return 2 * PARTS * slot + E0 + n


def z_number(slot, n):
    if isinstance(slot, int) and slot >= B - 1:
        return 2 * PARTS * (B - 1) + PARTS * (slot - B + 1) + n
    return 2 * PARTS * slot + n + (PARTS if n >= E0 else 0)


def ffn_stage(nc, a, s):
    t = "f_"
    with ExitStack() as ctx:
        sb = lambda name, shape, dt=F32: ctx.enter_context(nc.sbuf_tensor(t + name, shape, dt))
        sem = lambda name: ctx.enter_context(nc.semaphore(t + name))
        two = lambda name, shape, dt=F32: [sb(f"{name}{i}", shape, dt) for i in range(2)]
        xn = two("xn", [P, TPB, D])
        xt = two("xt", [P, 2, C, SQ], F16)
        qt = two("qt", [P, 2, H // 2, SQ], F16)
        kz = [sb(f"kz{i}", [P, 2, H, SQ], F16) for i in range(2)]
        g = sb("g", [P, TPB * GATES, E0])
        work, hit = sb("work", [P, TPB * GATES, E0]), sb("hit", [P, TPB * GATES, E0])
        sel = two("sel", [P, TPB, 2, H, E0])
        top = sb("top", [P, 3, TPB * GATES])
        mix = sb("mix", [P, TPB, H, E0])
        pv = sb("pv", [P, TPB, E0, DH])
        parts = [sb(f"part{i}", [P, H, DH]) for i in range(RING_PARTS)]
        vf = sb("vf", [P, H, DH])
        vh = two("vh", [P, 2, TPB, H, DH + 1], F16)
        mx, nb = two("mx", [P, TPB]), two("nb", [P, TPB])
        pr = two("pr", [P, TPB, SQ])
        pt = two("pt", [P, 2, TPB, TPB, P], F16)
        rs = two("rs", [P, 2 * TPB])
        at = two("at", [P, TPB, H, DH])
        selz = sb("selz", [P, TPB, H, E0])
        z = sb("z", [P, TPB, E0, DH])
        zt = sb("zt", [P, TPB, 2, E0 // 2, P], F16)
        ps = ctx.enter_context(nc.psum_tensor(t + "ps", [P, 8, 512], F32))
        front, back = ps[:, 0, :], ps[:, 1, :]
        S = lambda h: ps[:, 2 + h % 2, :].rearrange("p (t k) -> p t k", t=TPB)
        PT = lambda h: ps[:, 4 + h % 2, :]
        O = lambda h: ps[:, 6 + (h // 2) % 2, 0:4 * (DH + 1)].rearrange("p (h t d) -> p h t d", h=2, t=TPB)

        xn_ready = sem("xn_ready")
        front_ready = sem("front_ready")
        act_front = sem("act_front")
        front_done = sem("front_done")
        gates_ready = sem("gates_ready")
        selz_ready = sem("selz_ready")
        part_ready = sem("part_ready")
        part_used = sem("part_used")
        v_sum = sem("v_sum")
        v_hi = sem("v_hi")
        v_done = sem("v_done")
        at_ready = sem("at_ready")
        z_ready = sem("z_ready")
        s_ready = sem("s_ready")
        s_max = sem("s_max")
        p_ready = sem("p_ready")
        pt_ready = sem("pt_ready")
        pt_hi = sem("pt_hi")
        pt_done = sem("pt_done")
        pv_done = sem("pv_done")
        o_done = sem("o_done")
        back_ready = sem("back_ready")
        act_back = sem("act_back")
        back_done = sem("back_done")
        zeroed = sem("zeroed")
        front_step, core_step, norm_step, back_step = (
            sem("front_step"), sem("core_step"), sem("norm_step"), sem("back_step"))
        block = ctx.enter_context(nc.Block())

        def earlier(b, par, h, lag, do):
            if h >= lag and within(b, 0):
                do(b, par, h - lag)
            elif h < lag and within(b, 1, B + 1):
                do(b - 1, 1 - par, h - lag + H)

        @block.gpsimd
        def _(pool):
            chain = Chain(pool, zeroed)
            for par in range(2):
                chain(pool.memset(vh[par][:, 0, :, :, DH:DH + 1], 1.0))
                chain(pool.memset(vh[par][:, 1, :, :, DH:DH + 1], 0.0))
                chain(pool.memset(kz[par][:].rearrange("p l h k -> p (l h k)").bitcast(F32), 0.0))

            def v_part(slot, n):
                number = v_number(slot, n)
                pool.wait_ge(part_used, number + 1)
                ti, e = n // E0, n % E0
                pool.tensor_tensor(parts[n % RING_PARTS][:], bcast_mid(pv[:, ti, e, :], H), bcast(mix[:, ti, :, e], DH),
                                   ALU.mult).then_inc(part_ready, 1)

            def z_part(slot, par, n):
                number = z_number(slot, n)
                pool.wait_ge(part_used, number + 1)
                ti, e = n // E0, n % E0
                part = parts[n % RING_PARTS]
                pool.tensor_tensor(part[:], at[par][:, ti], bcast(selz[:, ti, :, e], DH), ALU.mult).then_inc(part_ready, 1)

            def projected(b):
                pool.wait_ge(gates_ready, b + 1)
                pool.wait_ge(front_done, FF_FRONT_CREDIT + FF_FRONT * b + F_V + TPB)

            projected(0)
            for n in range(PARTS):
                v_part(-1, n)

            def slot(b, half, par):
                if within(b, 1, B + 1):
                    pool.wait_ge(selz_ready, b)
                    pool.wait_ge(at_ready, b)
                    for n in range(E0):
                        z_part(b, 1 - par, n)
                if has_next(b):
                    projected(b + 1)
                    for n in range(PARTS):
                        v_part(b, n)
                if within(b, 1, B + 1):
                    for n in range(E0, PARTS):
                        z_part(b, 1 - par, n)

            run_slots(pool, slot, 1)

        @block.scalar
        def _(act):
            act.sem_inc(p_ready, 2)

            def pt_part(b, par, h):
                act.wait_ge(pt_ready, 2 + H * b + h + 1)
                act.wait_ge(pv_done, H * b + h + 1)
                act.activation(pt[h % 2][:, 0].rearrange("p c t q -> p (c t q)"), PT(h), ACT.Copy,
                               scale=SPLIT).then_inc(pt_hi, 1)

            def evacuate(b, par, j):
                act.wait_ge(front_ready, FF_FRONT * b + j + 1)
                if j == F_XN:
                    ins = act.activation(xt[par][:, 0].rearrange("p c q -> p (c q)"), front, ACT.Copy, scale=SPLIT)
                elif j == F_GATES:
                    act.activation(g[:].rearrange("p a e -> p (a e)"), front, ACT.Copy, scale=UNSPLIT)
                    ins = act.activation(mix[:], front.rearrange("p (t v h e) -> p t v h e", t=TPB, v=2, h=H)[:, :, 0],
                                         ACT.Exp, scale=-UNSPLIT)
                elif j < F_Q:
                    ins = act.activation(pv[:, j - F_V].rearrange("p e d -> p (e d)"), front, ACT.Copy, scale=UNSPLIT)
                elif j < F_K:
                    r = j - F_Q
                    ins = act.activation(qt[par][:, 0, 2 * r:2 * r + 2, :].rearrange("p m q -> p (m q)"), front,
                                         ACT.Copy, scale=1.0 / SPLIT)
                else:
                    r = j - F_K
                    for odd in range(2):
                        rows = slice(DH * odd, DH * odd + DH)
                        ins = act.activation(kz[par][rows, 0, 4 * r + odd:4 * r + 4:2, :],
                                             front[rows, :].rearrange("p (m k) -> p m k", m=2), ACT.Copy, scale=1.0 / SPLIT)
                ins.then_inc(act_front, 1)

            def v_part(b, par, ti):
                act.wait_ge(v_sum, TPB * b + ti + 1)
                act.activation(vh[par][:, 0, ti, :, 0:DH], vf[:], ACT.Copy).then_inc(v_hi, 1)

            def exps(b, h):
                n = H * b + h
                act.wait_ge(s_max, n + 1)
                act.wait_ge(pt_ready, n + 1)
                for ti in range(TPB):
                    ins = act.activation(pr[h % 2][:, ti, :], S(h)[:, ti, :], ACT.Exp, bias=nb[h % 2][:, ti:ti + 1],
                                         scale=UNSPLIT / DH ** 0.5)
                ins.then_inc(p_ready, 1)

            def back_hi(b, ti):
                act.wait_ge(back_ready, BACK * b + 2 * ti + 1)
                act.wait_ge(back_done, BACK * b + 2 * ti + 2)
                act.activation(zt[:, ti, 0].rearrange("p c q -> p (c q)"), back, ACT.Copy).then_inc(act_back, 1)

            for j in range(FF_FRONT):
                if j == F_K:
                    act.wait_ge(zeroed, 6)
                evacuate(0, 0, j)
            v_part(0, 0, 0)

            def slot(b, half, par):
                for h in range(H):
                    if h == FF_LAG and not within(b, 1, B + 2):
                        v_part(0, 0, 1)
                    earlier(b, par, h, FF_LAG - 1, pt_part)
                    if has_next(b):
                        if 0 <= h - 1 < FF_FRONT:
                            evacuate(b + 1, 1 - par, h - 1)
                        for ti in range(TPB):
                            if h == V_SUMMED[ti] + 1:
                                v_part(b + 1, 1 - par, ti)
                    if h == 1 and within(b, 2, B + 2):
                        back_hi(b - 2, 1)
                    if h == 9 and within(b, 1, B + 1):
                        back_hi(b - 1, 0)
                    if within(b, 0):
                        exps(b, h)

            run_slots(act, slot, 2)

        @block.tensor
        def _(pe):
            pe.sem_inc(pt_ready, 2)
            pe.sem_inc(pv_done, 2)

            pair = lambda ap, c, lo, n: tuple(ap[:, hl, c, lo:lo + n] for hl in range(2))

            def score(b, par, h):
                if h == 0:
                    pe.wait_ge(front_done, FF_FRONT_CREDIT + FF_FRONT * (b + 1))
                pe.wait_ge(p_ready, H * b + h + 1)
                for ti in range(TPB):
                    last = matmul3(pe, S(h)[:, ti, :],
                                   [(pair(qt[par], h // 2, ti * P, P), pair(kz[par], h, 0, SQ))])
                last.then_inc(s_ready, 1)

            def transposes(b, par, h):
                n = H * b + h
                pe.wait_ge(p_ready, 2 + n + 1)
                pe.wait_ge(pt_done, n + 1)
                for c in range(TPB):
                    for ti in range(TPB):
                        at_ = (c * TPB + ti) * P
                        last = pe.transpose(PT(h)[:, at_:at_ + P], pr[h % 2][:, ti, c * P:(c + 1) * P], s.ident[:])
                last.then_inc(pt_ready, 1)

            def times_v(b, par, h):
                if h == 0:
                    pe.wait_ge(v_done, TPB * (b + 1))
                if h % 2 == 0:
                    pe.wait_ge(o_done, H // 2 * b + h // 2 + 1)
                pe.wait_ge(pt_done, 2 + H * b + h + 1)
                for ti in range(TPB):
                    last = matmul3(pe, O(h)[:, h % 2, ti, :],
                                   [(tuple(pt[h % 2][:, hl, c, ti, :] for hl in range(2)),
                                     tuple(vh[par][:, hl, c, h, :] for hl in range(2))) for c in range(TPB)])
                last.then_inc(pv_done, 1)

            def project(b, par, j):
                pe.wait_ge(front_done, FF_FRONT * b + j + 1)
                if j == F_XN:
                    pe.wait_ge(xn_ready, b + 1)
                    for c in range(C):
                        for ti in range(TPB):
                            last = pe.transpose(front[:, c * SQ + ti * P:c * SQ + (ti + 1) * P],
                                                xn[par][:, ti, c * P:(c + 1) * P], s.ident[:])
                elif j == F_GATES:
                    for ti in range(TPB):
                        last = matmul3(pe, front[:, ti * 256:(ti + 1) * 256],
                                       [(pair(xt[par], c, ti * P, P), pair(s.fg, c, 0, 2 * H * E0)) for c in range(C)])
                elif j < F_Q:
                    ti = j - F_V
                    last = matmul3(pe, front, [(pair(xt[par], c, ti * P, P), pair(s.fv, c, 0, E0 * DH)) for c in range(C)])
                else:
                    w, r = (s.fq, j - F_Q) if j < F_K else (s.fk, j - F_K)
                    for m in range(2):
                        last = matmul3(pe, front[:, m * SQ:(m + 1) * SQ],
                                       [(pair(w, c, (2 * r + m) * P, P), pair(xt[par], c, 0, SQ)) for c in range(C)])
                last.then_inc(front_ready, 1)

            def back_transposes(b, ti):
                pe.wait_ge(back_done, BACK + BACK * b + 2 * ti)
                pe.wait_ge(z_ready, TPB * b + ti + 1)
                for ec in range(E0 // 2):
                    last = pe.transpose(back[:, ec * P:(ec + 1) * P],
                                        z[:, ti, 2 * ec:2 * ec + 2, :].rearrange("p e d -> p (e d)"), s.ident[:])
                last.then_inc(back_ready, 1)

            def back_product(b, ti):
                pe.wait_ge(back_done, BACK + BACK * b + 2 * ti + 1)
                matmul3(pe, back[:, 0:D],
                        [(tuple(zt[:, ti, hl, ec, :] for hl in range(2)), tuple(s.fo[:, hl, ec, :] for hl in range(2)))
                         for ec in range(E0 // 2)]).then_inc(back_ready, 1)

            for j in range(FF_FRONT):
                project(0, 0, j)
            score(0, 0, 0)
            score(0, 0, 1)

            def slot(b, half, par):
                for h in range(H):
                    earlier(b, par, h, 1, transposes)
                    earlier(b, par, h, FF_LAG, times_v)
                    if has_next(b) and h < FF_FRONT:
                        project(b + 1, 1 - par, h)
                    if within(b, 0) and h + 2 < H:
                        score(b, par, h + 2)
                    elif has_next(b) and h + 2 >= H:
                        score(b + 1, 1 - par, h + 2 - H)
                    if within(b, 2, B + 2):
                        if h == 0:
                            back_transposes(b - 2, 1)
                        if h == 1:
                            back_product(b - 2, 1)
                    if within(b, 1, B + 1):
                        if h == 8:
                            back_transposes(b - 1, 0)
                        if h == 9:
                            back_product(b - 1, 0)

            run_slots(pe, slot, 2)

        @block.vector
        def _(dve):
            dve.sem_inc(front_done, FF_FRONT_CREDIT)
            dve.sem_inc(part_used, RING_PARTS)
            dve.sem_inc(pt_done, 2)
            dve.sem_inc(o_done, 2)
            dve.sem_inc(back_done, BACK)

            def gate_choice(par, part, chain):
                chosen = sel[par][:].rearrange("p t v h e -> p (t v h) e")
                src = g if part < 2 else work
                if part % 2 == 0:
                    chain(dve.tensor_reduce(top[:, 0, :], src[:], AX_X, ALU.max))
                    chain(dve.tensor_tensor(hit[:], src[:], bcast(top[:, 0, :], E0), ALU.is_equal))
                    chain(dve.tensor_tensor(hit[:], hit[:], bcast_mid(s.rank[:, E1 - E0:E1], TPB * GATES), ALU.mult))
                elif part == 1:
                    chain(dve.tensor_reduce(top[:, 1, :], hit[:], AX_X, ALU.max))
                    chain(dve.tensor_tensor(chosen, hit[:], bcast(top[:, 1, :], E0), ALU.is_equal))
                    chain(dve.scalar_tensor_tensor(work[:], chosen, MASKED, g[:], ALU.mult, ALU.add))
                else:
                    chain(dve.tensor_reduce(top[:, 1, :], hit[:], AX_X, ALU.max))
                    chain(dve.tensor_tensor(hit[:], hit[:], bcast(top[:, 1, :], E0), ALU.is_equal))
                    chain(dve.tensor_tensor(chosen, chosen, hit[:], ALU.add))

            def sigmoids(chain):
                chain(dve.tensor_scalar(mix[:], mix[:], 1.0, None, ALU.add))
                chain(dve.reciprocal(mix[:], mix[:]))

            def gate_weights(par):
                dve.scalar_tensor_tensor(mix[:], mix[:], SPLIT, sel[par][:, :, 0], ALU.mult, ALU.mult).then_inc(gates_ready, 1)

            def evacuate(b, par, j):
                dve.wait_ge(act_front, FF_FRONT * b + j + 1)
                if F_XN < j < F_Q:
                    dve.sem_inc(front_done, 1)
                    return
                if j == F_XN:
                    ins = dve.scalar_tensor_tensor(xt[par][:, 1].rearrange("p c q -> p (c q)"), front, SPLIT,
                                                   xt[par][:, 0].rearrange("p c q -> p (c q)"), ALU.mult, ALU.subtract)
                elif j < F_K:
                    m = slice(2 * (j - F_Q), 2 * (j - F_Q) + 2)
                    ins = dve.scalar_tensor_tensor(qt[par][:, 1, m, :].rearrange("p m q -> p (m q)"), front, 1.0 / SPLIT,
                                                   qt[par][:, 0, m, :].rearrange("p m q -> p (m q)"), ALU.mult, ALU.subtract)
                else:
                    for odd in range(2):
                        rows = slice(DH * odd, DH * odd + DH)
                        hs = slice(4 * (j - F_K) + odd, 4 * (j - F_K) + 4, 2)
                        ins = dve.scalar_tensor_tensor(kz[par][rows, 1, hs, :],
                                                       front[rows, :].rearrange("p (m k) -> p m k", m=2),
                                                       1.0 / SPLIT, kz[par][rows, 0, hs, :], ALU.mult, ALU.subtract)
                ins.then_inc(front_done, 1)

            def normalised_x(b, par):
                for ti in range(TPB):
                    tile = bass.ds(TPB * b + ti, 1)
                    ins = dve.tensor_scalar(xn[par][:, ti, :], s.x[:, tile, :], s.mv[:, tile, 0], s.rstd[:, tile],
                                            ALU.subtract, ALU.mult)
                ins.then_inc(xn_ready, 1)

            def v_part(slot, n):
                ti, e, number = n // E0, n % E0, v_number(slot, n)
                if e == 0:
                    return
                if n == E0 + 1:
                    dve.wait_ge(v_hi, TPB * (slot + 1) + 1)
                    dve.wait_ge(v_done, TPB * (slot + 1) + 1)
                dve.wait_ge(part_ready, number + 1)
                part = parts[n % RING_PARTS]
                if e == 1:
                    dve.tensor_tensor(vf[:], parts[0][:], part[:], ALU.add).then_inc(part_used, 2)
                else:
                    dve.tensor_tensor(vf[:], vf[:], part[:], ALU.add).then_inc(part_used, 1)
                dve.wait_ge(part_used, RING_PARTS + number + 1)
                if e == E0 - 1:
                    dve.sem_inc(v_sum, 1)

            def v_lo(b, par, ti):
                dve.wait_ge(v_hi, TPB * b + ti + 1)
                dve.tensor_tensor(vh[par][:, 1, ti, :, 0:DH], vf[:], vh[par][:, 0, ti, :, 0:DH],
                                  ALU.subtract).then_inc(v_done, 1)

            def z_part(slot, n):
                ti, e, number = n // E0, n % E0, z_number(slot, n)
                dve.wait_ge(part_ready, number + 1)
                dve.tensor_reduce(z[:, ti, e, :], parts[n % RING_PARTS][:].rearrange("p h d -> p d h"), AX_X,
                                  ALU.add).then_inc(part_used, 1)
                if e == E0 - 1:
                    dve.wait_ge(part_used, RING_PARTS + number + 1)
                    dve.sem_inc(z_ready, 1)

            def maxima(b, h, chain):
                dve.wait_ge(s_ready, H * b + h + 1)
                dve.wait_ge(p_ready, H * b + h + 1)
                chain(dve.tensor_reduce(mx[h % 2][:], S(h), AX_X, ALU.max))
                dve.tensor_scalar(nb[h % 2][:], mx[h % 2][:], -UNSPLIT / DH ** 0.5, None, ALU.mult).then_inc(s_max, 1)

            def pt_part(b, par, h):
                dve.wait_ge(pt_hi, H * b + h + 1)
                dve.scalar_tensor_tensor(pt[h % 2][:, 1].rearrange("p c t q -> p (c t q)"), PT(h), SPLIT,
                                         pt[h % 2][:, 0].rearrange("p c t q -> p (c t q)"),
                                         ALU.mult, ALU.subtract).then_inc(pt_done, 1)

            def normalise(b, par, hp):
                chain = Chain(dve, norm_step, 1, H // 2 * b + hp)
                h = 2 * hp
                dve.wait_ge(pv_done, 2 + H * b + h + 2)
                r = rs[hp % 2][:].rearrange("p (h t) -> p h t", h=2)
                chain(dve.reciprocal(r, O(h)[:, :, :, DH]))
                for ti in range(TPB):
                    ins = dve.tensor_tensor(at[par][:, ti, h:h + 2, :], O(h)[:, :, ti, 0:DH], bcast(r[:, :, ti], DH), ALU.mult)
                ins.then_inc(o_done, 1)

            def back_lo(b, ti):
                dve.wait_ge(act_back, TPB * b + ti + 1)
                dve.tensor_tensor(zt[:, ti, 1].rearrange("p c q -> p (c q)"), back,
                                  zt[:, ti, 0].rearrange("p c q -> p (c q)"), ALU.subtract).then_inc(back_done, 1)

            def update(b, ti):
                chain = Chain(dve, back_step, UPDATE_LINKS, TPB * b + ti)
                j = BACK * b + 2 * ti + 1
                dve.wait_ge(back_ready, j + 1)
                dve.scalar_tensor_tensor(s.xs[:].unsqueeze(1), back[:, 0:D].unsqueeze(1), s.tgu[:, 2:3],
                                         s.x[:, bass.ds(TPB * b + ti, 1), :], ALU.mult, ALU.add).then_inc(back_done, 1)
                dve.wait_ge(back_done, BACK + j + 1)
                chain(keep_tile(dve, chain, s, TPB * b + ti))
                chain.close()

            chain = Chain(dve, front_step)
            normalised_x(0, 0)
            for j in range(F_Q):
                evacuate(0, 0, j)
            sigmoids(chain)
            for j in range(F_Q, F_K):
                gate_choice(0, j - F_Q, chain)
                evacuate(0, 0, j)
            gate_weights(0)
            for j in range(F_K, FF_FRONT):
                evacuate(0, 0, j)
                for n in range(2 * (j - F_K), 2 * (j - F_K) + 2):
                    v_part(-1, n)
            v_lo(0, 0, 0)

            def slot(b, half, par):
                front_chain = Chain(dve, front_step, FF_FRONT_LINKS, b + 1)
                core_chain = Chain(dve, core_step, H, b)
                for h in range(H):
                    if within(b, 0):
                        maxima(b, h, core_chain)
                    if not within(b, 1, B + 2):
                        for n in FIRST_V_STEPS.get(h, ()):
                            v_part(-1, n)
                        if h == FF_LAG:
                            v_lo(0, 0, 1)
                    if h == 0 and has_next(b):
                        normalised_x(b + 1, 1 - par)
                    if h == 0 and within(b, 1, B + 1):
                        dve.tensor_copy(selz[:], sel[1 - par][:, :, 1]).then_inc(selz_ready, 1)
                    earlier(b, par, h, FF_LAG - 1, pt_part)
                    if h % 2 == 1:
                        if h >= 5 and within(b, 0):
                            normalise(b, par, (h - 5) // 2)
                        elif h < 5 and within(b, 1, B + 1):
                            normalise(b - 1, 1 - par, (h - 5) // 2 + H // 2)
                            if h == 3:
                                dve.wait_ge(o_done, 2 + H // 2 * b)
                                dve.sem_inc(at_ready, 1)
                    if has_next(b) and 0 <= h - 1 < FF_FRONT:
                        evacuate(b + 1, 1 - par, h - 1)
                    if within(b, 2, B + 2):
                        if h == 1:
                            back_lo(b - 2, 1)
                        if h == 2:
                            update(b - 2, 1)
                    if within(b, 1, B + 1):
                        for n in Z_STEPS.get(h, ()):
                            z_part(b, n)
                        if h == 9:
                            back_lo(b - 1, 0)
                        if h == 10:
                            update(b - 1, 0)
                    if has_next(b):
                        for ti in range(TPB):
                            if h == V_SUMMED[ti] + 1:
                                v_lo(b + 1, 1 - par, ti)
                        for n in V_STEPS.get(h, ()):
                            v_part(b, n)
                        if h == GATES_STEP:
                            sigmoids(front_chain)
                        if GATES_STEP <= h < GATES_STEP + 4:
                            gate_choice(1 - par, h - GATES_STEP, front_chain)
                        if h == GATES_STEP + 3:
                            gate_weights(1 - par)
                            front_chain.close()

            run_slots(dve, slot, 2)
            rsqrt_all(dve, Chain(dve, s.stage_step[2]), s)


GATES_STEP = F_GATES + 1
V_SUMMED = [max(h for h in V_STEPS if E0 * ti + E0 - 1 in V_STEPS[h]) for ti in range(TPB)]
FF_FRONT_LINKS = 14
UPDATE_LINKS = 4


M = HID // P
BT = TPB * P
NB = (TOP1 * TILES * P + E1 * (BT - 1)) // BT
CHOICES = TOP1 * TILES
UP_PAIRS = M // 2
GATHER_GROUP = 4
LAST_TURN = (NB - 4) // 2

ROUTE_SEMS = ("xn_ready", "tr_ready", "tr_hi", "tr_done", "gate_done", "cw_exp", "cwt_ready",
              "cwt_done", "b_ready", "b_done", "dve_step", "cw_ready", "shifted", "masks_made",
              "sel_ready", "counted", "slots_ready", "experts_ready", "sent")
EXPERT_SEMS = ("up_hi", "up_split", "down_hi", "down_split", "turned", "xt_hi", "xt_split", "u_ready",
               "h_gelu", "h_hi", "h_done", "y_ready", "y_done")
LOAD_SEMS = tuple(f"{n}{i}" for n in ("u_loaded", "d_loaded", "x_loaded", "y_stored") for i in range(2))
COMBINE_SEMS = ("added", "stored", *(f"fetched{n}" for n in range(CHOICES // GATHER_GROUP)))


def run_blocks(eng, slot):
    for j in range(3):
        slot(j, j % 2, j // 2)
    with eng.Fori(1, LAST_TURN) as i:
        slot(2 * i + 1, 1, i)
        slot(2 * i + 2, 0, i + 1)
    for j in range(2 * LAST_TURN + 1, NB):
        slot(j, j % 2, j // 2)


def moe_stage(nc, a, s, out):
    t = "m_"
    rows_in, rows_out = s.rows_in, nc.dram_tensor("expert_out", (NB * BT, D), F32).ap()
    with ExitStack() as ctx:
        sb = lambda name, shape, dt=F32: ctx.enter_context(nc.sbuf_tensor(t + name, shape, dt))
        sems = {name: ctx.enter_context(nc.semaphore(t + name))
                for name in (*ROUTE_SEMS, *EXPERT_SEMS, *LOAD_SEMS, *COMBINE_SEMS)}
        sem = lambda name: sems[name]
        slot_of = sb("slot_of", [P, CHOICES], I32)
        weight_of = sb("weight_of", [P, CHOICES])
        expert_of = sb("expert_of", [1, NB], I32)
        with ExitStack() as work:
            buf = lambda name, shape, dt=F32: work.enter_context(nc.sbuf_tensor(t + name, shape, dt))
            two = lambda name, shape, dt=F32: [buf(f"{name}{i}", shape, dt) for i in range(2)]
            uraw, draw = two("uraw", [P, C, HID]), two("draw", [P, M, D])
            us, dsp = two("us", [P, 2, C, HID], F16), two("ds", [P, 2, M, D], F16)
            xg = two("xg", [P, TPB, D])
            xt = two("xt", [P, 2, C, BT], F16)
            ps = work.enter_context(nc.psum_tensor(t + "ps", [P, 8, 512], F32))
            bue = two("bue", [P, M])
            weights = ExpertWeights(a, s, sem, uraw, draw, us, dsp, bue, expert_of)
            route(nc, s, t, sem, ps, xt, rows_in, slot_of, weight_of, expert_of, weights)
            run_experts(nc, s, t, sem, work, ps, xg, xt, rows_in, rows_out, weights)
        combine(nc, s, t, sem, sb, rows_out, slot_of, weight_of, out)


class ExpertWeights:

    def __init__(self, a, s, sem, uraw, draw, us, dsp, bue, expert_of):
        self.a, self.s, self.expert_of = a, s, expert_of
        self.uraw, self.draw, self.us, self.dsp, self.bue = uraw, draw, us, dsp, bue
        self.u_loaded = [sem(f"u_loaded{i}") for i in range(2)]
        self.d_loaded = [sem(f"d_loaded{i}") for i in range(2)]
        self.up_hi, self.up_split = sem("up_hi"), sem("up_split")
        self.down_hi, self.down_split = sem("down_hi"), sem("down_split")
        self.u_ready, self.y_ready = sem("u_ready"), sem("y_ready")

    def load_up(self, sp, j, par, turn=0, first=False):
        e = sp.value_load(self.expert_of[0:1, bass.ds(j, 1)], min_val=0, max_val=E1 - 1)
        if not first:
            sp.wait_ge(self.up_split, j + 1)
        sp.dma_start(self.uraw[par][:],
                     self.a["L1_ffn_Wup"][bass.ds(e, 1)].rearrange("o (c p) h -> (o p) c h", p=P)).then_inc(self.u_loaded[par], 16)

    def load_down(self, sp, j, par, turn=0, first=False):
        e = sp.value_load(self.expert_of[0:1, bass.ds(j, 1)], min_val=0, max_val=E1 - 1)
        if not first:
            sp.wait_ge(self.down_split, j + 1)
        sp.dma_start(self.draw[par][:],
                     self.a["L1_ffn_Wdown"][bass.ds(e, 1)].rearrange("o (m p) d -> (o p) m d", p=P)).then_inc(self.d_loaded[par], 16)

    def split_up_hi(self, act, j, par, turn, first=False):
        act.wait_ge(self.u_loaded[par], 16 * (turn + 1))
        if not first:
            act.wait_ge(self.u_ready, UP_PAIRS * (j + 1))
        act.activation(self.us[par][:, 0], self.uraw[par][:], ACT.Copy, scale=SPLIT).then_inc(self.up_hi, 1)

    def split_down_hi(self, act, j, par, turn, first=False):
        act.wait_ge(self.d_loaded[par], 16 * (turn + 1))
        if not first:
            act.wait_ge(self.y_ready, TPB * (j + 1))
        act.activation(self.dsp[par][:, 0], self.draw[par][:], ACT.Copy, scale=SPLIT).then_inc(self.down_hi, 1)

    def split_up_lo(self, dve, j, par, turn=0):
        e = dve.value_load(self.expert_of[0:1, bass.ds(j, 1)], min_val=0, max_val=E1 - 1)
        dve.tensor_copy(self.bue[par][:].unsqueeze(1), self.s.bup[:, bass.ds(e, 1), :])
        dve.wait_ge(self.up_hi, j + 1)
        dve.scalar_tensor_tensor(self.us[par][:, 1], self.uraw[par][:], SPLIT, self.us[par][:, 0],
                                 ALU.mult, ALU.subtract).then_inc(self.up_split, 1)

    def split_down_lo(self, dve, j, par, turn=0):
        dve.wait_ge(self.down_hi, j + 1)
        dve.scalar_tensor_tensor(self.dsp[par][:, 1], self.draw[par][:], SPLIT, self.dsp[par][:, 0],
                                 ALU.mult, ALU.subtract).then_inc(self.down_split, 1)


def route(nc, s, t, sem, ps, xt, rows_in, slot_of, weight_of, expert_of, weights):
    xn_ready, tr_ready, tr_hi, tr_done = sem("xn_ready"), sem("tr_ready"), sem("tr_hi"), sem("tr_done")
    gate_done = sem("gate_done")
    cw_exp, cwt_ready, cwt_done, b_ready, b_done = (
        sem("cw_exp"), sem("cwt_ready"), sem("cwt_done"), sem("b_ready"), sem("b_done"))
    dve_step = sem("dve_step")
    cw_ready, shifted = sem("cw_ready"), sem("shifted")
    masks_made = sem("masks_made")
    sel_ready = sem("sel_ready")
    counted = sem("counted")
    slots_ready = sem("slots_ready")
    experts_ready = sem("experts_ready")
    sent = sem("sent")
    with ExitStack() as prep:
        sb = lambda name, shape, dt=F32: prep.enter_context(nc.sbuf_tensor(t + name, shape, dt))
        xn = sb("xn", [P, TILES, D])
        g, work, hit = (sb(n, [P, TILES, E1]) for n in ("g", "work", "hit"))
        chosen = sb("chosen", [P, TOP1, TILES, E1])
        picked = sb("picked", [P, TOP1, TILES, E1])
        sel, cw = sb("sel", [P, TILES, E1]), sb("cw", [P, TILES, E1])
        sel16 = sb("sel16", [P, TILES, E1], F16)
        before, ones = sb("before", [P, P], F16), sb("ones", [P, P], F16)
        place = sb("place", [P, TILES, E1])
        top = sb("top", [P, 3, TILES])
        filled, blocks, ends = sb("filled", [P, E1], I32), sb("blocks", [P, E1]), sb("ends", [P, E1])
        start = sb("start", [P, E1])
        slot_f = sb("slot_f", [P, CHOICES])
        nth, nth_f = sb("nth", [1, NB], I32), sb("nth_f", [1, NB])
        past, expert_f = sb("past", [1, NB, E1]), sb("expert_f", [1, NB])
        cwt = sb("cwt", [E1, TILES * P])
        tr = lambda k: ps[:, k % 2, :]
        G = ps[:, 2, 0:TILES * E1].rearrange("p (t e) -> p t e", t=TILES)
        RANK = ps[:, 3, 0:TILES * E1].rearrange("p (t e) -> p t e", t=TILES)
        TOTAL = ps[:, 4, 0:E1]
        block = prep.enter_context(nc.Block())

        @block.gpsimd
        def _(pool):
            chain = Chain(pool, masks_made)
            pool.memset(ones[:], 1.0)
            chain(pool.memset(before[:], 1.0))
            pool.iota(nth[:], [[1, NB]], base=0, channel_multiplier=0)
            pool.affine_select(out=before[:], in_=before[:], compare_op=ALU.is_ge, fill=0.0, base=-1,
                               pattern=[[1, P]], channel_multiplier=-1).then_inc(masks_made, 1)
            pool.wait_ge(slots_ready, 1)
            for n in range(CHOICES):
                pool.indirect_dma_start(rows_in[:, :], bass.IndirectOffsetOnAxis(slot_of[:, n:n + 1], 0),
                                        xn[:, n % TILES, :], None).then_inc(sent, 16)
            pool.wait_ge(sent, 16 * CHOICES)

        @block.sync
        def _(sp):
            sp.wait_ge(experts_ready, 1)
            for j in range(2):
                weights.load_up(sp, j, j, first=True)
            for j in range(2):
                weights.load_down(sp, j, j, first=True)

        @block.scalar
        def _(act):
            for k in range(B):
                act.wait_ge(tr_ready, k + 1)
                if k >= 2:
                    act.wait_ge(gate_done, k - 1)
                act.activation(xt[k % 2][:, 0], tr(k).rearrange("p (c q) -> p c q", c=C),
                               ACT.Copy, scale=SPLIT).then_inc(tr_hi, 1)
            act.wait_ge(shifted, 1)
            act.activation(work[:], work[:], ACT.Exp).then_inc(cw_exp, 1)
            for q in range(TILES // 4):
                act.wait_ge(cwt_ready, q + 1)
                act.activation(cwt[:, q * 512:(q + 1) * 512], ps[0:E1, 4 + q, :], ACT.Copy).then_inc(cwt_done, 1)
            weights.split_up_hi(act, 0, 0, 0, first=True)
            weights.split_up_hi(act, 1, 1, 0, first=True)
            weights.split_down_hi(act, 0, 0, 0, first=True)

        @block.tensor
        def _(pe):
            def gate(k):
                pe.wait_ge(tr_done, k + 1)
                for ti in range(TPB):
                    last = matmul3(pe, G[:, TPB * k + ti, :],
                                   [(tuple(xt[k % 2][:, hl, c, ti * P:(ti + 1) * P] for hl in range(2)),
                                     tuple(s.wg[:, hl, c, :] for hl in range(2))) for c in range(C)])
                last.then_inc(gate_done, 1)

            for k in range(B):
                pe.wait_ge(xn_ready, k + 1)
                if k >= 2:
                    pe.wait_ge(tr_done, k - 1)
                for c in range(C):
                    for ti in range(TPB):
                        last = pe.transpose(tr(k)[:, c * SQ + ti * P:c * SQ + (ti + 1) * P],
                                            xn[:, TPB * k + ti, c * P:(c + 1) * P], s.ident[:])
                last.then_inc(tr_ready, 1)
                if k >= 1:
                    gate(k - 1)
            gate(B - 1)
            pe.wait_ge(masks_made, 2)
            pe.wait_ge(sel_ready, 1)
            pe.matmul(RANK, before[:], sel16[:], start=True, stop=False)
            for tile in range(TILES - 1):
                pe.matmul(RANK[:, tile + 1:, :], ones[:], bcast_mid(sel16[:, tile, :], TILES - 1 - tile),
                          start=False, stop=(tile == TILES - 2))
            for tile in range(TILES):
                last = pe.matmul(TOTAL, ones[:], sel16[:, tile, :], start=(tile == 0), stop=(tile == TILES - 1))
            last.then_inc(counted, 1)
            pe.wait_ge(cw_ready, 1)
            for q in range(TILES // 4):
                for ti in range(4):
                    last = pe.transpose(ps[0:E1, 4 + q, ti * P:(ti + 1) * P], cw[:, 4 * q + ti, :], s.ident[:])
                last.then_inc(cwt_ready, 1)
            for tile in range(TILES):
                if tile % 4 == 0:
                    pe.wait_ge(cwt_done, tile // 4 + 1)
                if tile >= 2:
                    pe.wait_ge(b_done, tile - 1)
                pe.matmul(ps[:, 2 + tile % 2, 0:D], cwt[:, tile * P:(tile + 1) * P], s.bdown[:],
                          start=True, stop=True).then_inc(b_ready, 1)

        def lo_part(dve, k):
            dve.wait_ge(tr_hi, k + 1)
            dve.scalar_tensor_tensor(xt[k % 2][:, 1], tr(k).rearrange("p (c q) -> p c q", c=C),
                                     SPLIT, xt[k % 2][:, 0], ALU.mult, ALU.subtract).then_inc(tr_done, 1)

        @block.vector
        def _(dve):
            chain = Chain(dve, dve_step)
            dve.sem_inc(weights.up_split, 2)
            dve.sem_inc(weights.down_split, 2)
            for k in range(B):
                for ti in range(TPB):
                    tile = TPB * k + ti
                    ins = dve.tensor_scalar(xn[:, tile, :], s.x[:, tile, :], s.mv[:, tile, 0:1],
                                            s.rstd[:, tile:tile + 1], ALU.subtract, ALU.mult)
                ins.then_inc(xn_ready, 1)
                if k >= 1:
                    lo_part(dve, k - 1)
            lo_part(dve, B - 1)
            dve.wait_ge(gate_done, B)
            chain(dve.tensor_scalar(g[:], G, UNSPLIT, None, ALU.mult))
            src = g[:]
            for r in range(TOP1):
                most = top[:, min(r, 1), :]
                chain(dve.tensor_reduce(most, src, AX_X, ALU.max))
                chain(dve.tensor_tensor(hit[:], src, bcast(most, E1), ALU.is_equal))
                chain(dve.tensor_tensor(hit[:], hit[:], bcast_mid(s.rank[:], TILES), ALU.mult))
                chain(dve.tensor_reduce(top[:, 2, :], hit[:], AX_X, ALU.max))
                chain(dve.tensor_tensor(chosen[:, r], hit[:], bcast(top[:, 2, :], E1), ALU.is_equal))
                if r < TOP1 - 1:
                    chain(dve.scalar_tensor_tensor(work[:], chosen[:, r], MASKED, src, ALU.mult, ALU.add))
                    src = work[:]
            chain(dve.tensor_tensor(sel[:], chosen[:, 0], chosen[:, 1], ALU.add))
            chain(dve.tensor_tensor(sel[:], sel[:], chosen[:, 2], ALU.add))
            dve.tensor_copy(sel16[:], sel[:]).then_inc(sel_ready, 1)
            dve.tensor_tensor(work[:], g[:], bcast(top[:, 0, :], E1), ALU.subtract).then_inc(shifted, 1)
            dve.wait_ge(masks_made, 2)
            dve.tensor_copy(nth_f[:], nth[:])
            dve.wait_ge(counted, 1)
            chain(dve.tensor_scalar(filled[:], TOTAL, float(BT - 1), None, ALU.add))
            chain(dve.tensor_scalar(filled[:], filled[:], BT.bit_length() - 1, None, ALU.logical_shift_right))
            chain(dve.tensor_copy(blocks[:], filled[:]))
            chain(dve.tensor_copy(ends[:, 0:1], blocks[:, 0:1]))
            for e in range(1, E1):
                chain(dve.tensor_tensor(ends[:, e:e + 1], ends[:, e - 1:e], blocks[:, e:e + 1], ALU.add))
            chain(dve.tensor_tensor(start[:], ends[:], blocks[:], ALU.subtract))
            chain(dve.scalar_tensor_tensor(place[:], bcast_mid(start[:], TILES), float(BT), RANK, ALU.mult, ALU.add))
            for r in range(TOP1):
                chain(dve.tensor_tensor(picked[:, r], chosen[:, r], place[:], ALU.mult))
            chain(dve.tensor_reduce(slot_f[:], picked[:].rearrange("p r t e -> p (r t) e"), AX_X, ALU.add))
            dve.tensor_copy(slot_of[:], slot_f[:]).then_inc(slots_ready, 1)
            chain(dve.tensor_tensor(past[:], bcast(nth_f[:], E1), bcast_mid(ends[0:1, :], NB), ALU.is_ge))
            chain(dve.tensor_reduce(expert_f[:], past[:], AX_X, ALU.add))
            dve.tensor_scalar(expert_of[:], expert_f[:], float(E1 - 1), None, ALU.min).then_inc(experts_ready, 1)
            dve.wait_ge(experts_ready, 1)
            dve.wait_ge(cw_exp, 1)
            chain(dve.tensor_tensor(cw[:], work[:], sel[:], ALU.mult))
            chain(dve.tensor_reduce(top[:, 1, :], cw[:], AX_X, ALU.add))
            chain(dve.reciprocal(top[:, 2, :], top[:, 1, :]))
            chain(dve.tensor_scalar(top[:, 2, :], top[:, 2, :], s.tg[:, 3:4], None, ALU.mult))
            dve.tensor_tensor(cw[:], cw[:], bcast(top[:, 2, :], E1), ALU.mult).then_inc(cw_ready, 1)
            dve.wait_ge(cw_ready, 1)
            for r in range(TOP1):
                chain(dve.tensor_tensor(picked[:, r], chosen[:, r], cw[:], ALU.mult))
            chain(dve.tensor_reduce(slot_f[:], picked[:].rearrange("p r t e -> p (r t) e"), AX_X, ALU.add))
            dve.tensor_scalar(weight_of[:], slot_f[:], UNSPLIT, None, ALU.mult)
            for tile in range(TILES):
                dve.wait_ge(b_ready, tile + 1)
                dve.tensor_tensor(s.x[:, tile, :], s.x[:, tile, :], ps[:, 2 + tile % 2, 0:D], ALU.add).then_inc(b_done, 1)
            dve.wait_ge(b_done, TILES)
            weights.split_up_lo(dve, 0, 0)
            weights.split_up_lo(dve, 1, 1)
            weights.split_down_lo(dve, 0, 0)


def run_experts(nc, s, t, sem, ctx, ps, xg, xt, rows_in, rows_out, weights):
    sb = lambda name, shape, dt=F32: ctx.enter_context(nc.sbuf_tensor(t + name, shape, dt))
    two = lambda name, shape, dt=F32: [sb(f"{name}{i}", shape, dt) for i in range(2)]
    hf = sb("hf", [P, UP_PAIRS, 2, BT])
    hs = two("hs", [P, 2, M, BT], F16)
    yo = two("yo", [P, TPB, D])
    x_loaded, y_stored = ([sem(f"{n}{i}") for i in range(2)] for n in ("x_loaded", "y_stored"))
    up_split, down_split = weights.up_split, weights.down_split
    turned = sem("turned")
    xt_hi, xt_split = sem("xt_hi"), sem("xt_split")
    u_ready = sem("u_ready")
    h_gelu = sem("h_gelu")
    h_hi, h_done = sem("h_hi"), sem("h_done")
    y_ready = sem("y_ready")
    y_done = sem("y_done")
    block = ctx.enter_context(nc.Block())
    U = lambda q: ps[:, q, :].rearrange("p (m k) -> p m k", m=2)
    T = ps[:, UP_PAIRS, :]
    Y = lambda ti: ps[:, UP_PAIRS + 1 + ti, 0:D]

    def ahead(j, par, turn, n, do):
        if not isinstance(j, int) or j + n < NB:
            do(j + n, (par + n) % 2, turn + (par + n) // 2)

    @block.sync
    def _(sp):
        load_up = lambda j, par, turn: weights.load_up(sp, j, par)
        load_down = lambda j, par, turn: weights.load_down(sp, j, par)

        def load_rows(j, par, turn):
            sp.wait_ge(turned, j + 1)
            sp.dma_start(xg[par][:], rows_in[bass.ds(j * BT, BT), :].rearrange("(t p) d -> p t d", p=P)).then_inc(x_loaded[par], 16)

        def store(j, par, turn):
            sp.wait_ge(y_done, TPB * (j + 2))
            sp.dma_start(rows_out[bass.ds(j * BT, BT), :].rearrange("(t p) d -> p t d", p=P), yo[par][:]).then_inc(y_stored[par], 16)

        for j in range(3):
            load_rows(j, j % 2, j // 2)
        load_up(2, 0, 1)

        def slot(j, par, turn):
            if not (isinstance(j, int) and j == 0):
                store(j - 1, 1 - par, turn)
            ahead(j, par, turn, 3, load_up)
            ahead(j, par, turn, 3, load_rows)
            ahead(j, par, turn, 2, load_down)

        run_blocks(sp, slot)
        store(NB - 1, (NB - 1) % 2, 0)
        for par in range(2):
            sp.wait_ge(y_stored[par], 16 * ((NB + 1 - par) // 2))

    @block.scalar
    def _(act):
        act.sem_inc(h_gelu, UP_PAIRS)

        up_part = lambda j, par, turn: weights.split_up_hi(act, j, par, turn)
        down_part = lambda j, par, turn: weights.split_down_hi(act, j, par, turn)

        def rows_part(j, par, turn):
            act.wait_ge(turned, 2 + j + 1)
            act.activation(xt[par][:, 0].rearrange("p c q -> p (c q)"), T, ACT.Copy, scale=SPLIT).then_inc(xt_hi, 1)

        def gelus(j, par, turn):
            for q in range(UP_PAIRS):
                act.wait_ge(u_ready, UP_PAIRS * (j + 2) + q + 1)
                act.wait_ge(h_done, UP_PAIRS * j + q + 1)
                for m in range(2):
                    ins = act.activation(hf[:, q, m, :], U(q)[:, m, :], ACT.Gelu, bias=weights.bue[par][:, 2 * q + m:2 * q + m + 1],
                                         scale=UNSPLIT)
                ins.then_inc(h_gelu, 1)

        rows_part(0, 0, 0)
        rows_part(1, 1, 0)
        gelus(0, 0, 0)

        def slot(j, par, turn):
            ahead(j, par, turn, 2, up_part)
            ahead(j, par, turn, 1, gelus)
            ahead(j, par, turn, 2, rows_part)
            ahead(j, par, turn, 1, down_part)

        run_blocks(act, slot)

    @block.tensor
    def _(pe):
        pe.sem_inc(u_ready, 2 * UP_PAIRS)
        pe.sem_inc(y_ready, 2 * TPB)
        pe.sem_inc(turned, 2)

        def turn_rows(j, par, turn):
            pe.wait_ge(x_loaded[par], 16 * (turn + 1))
            pe.wait_ge(xt_split, j + 1)
            for c in range(C):
                for ti in range(TPB):
                    last = pe.transpose(T[:, c * BT + ti * P:c * BT + (ti + 1) * P],
                                        xg[par][:, ti, c * P:(c + 1) * P], s.ident[:])
            last.then_inc(turned, 1)

        def up(j, par, turn):
            pe.wait_ge(up_split, 2 + j + 1)
            pe.wait_ge(xt_split, 1 + j + 1)
            for q in range(UP_PAIRS):
                pe.wait_ge(h_gelu, UP_PAIRS * j + q + 1)
                for m in (2 * q, 2 * q + 1):
                    last = matmul3(pe, U(q)[:, m % 2, :],
                                   [(tuple(weights.us[par][:, hl, k, m * P:(m + 1) * P] for hl in range(2)),
                                     tuple(xt[par][:, hl, k, :] for hl in range(2))) for k in range(C)])
                last.then_inc(u_ready, 1)

        def down(j, par, turn):
            pe.wait_ge(h_done, UP_PAIRS * (j + 2))
            pe.wait_ge(down_split, 2 + j + 1)
            for ti in range(TPB):
                pe.wait_ge(y_done, TPB * j + ti + 1)
                matmul3(pe, Y(ti),
                        [(tuple(hs[par][:, hl, m, ti * P:(ti + 1) * P] for hl in range(2)),
                          tuple(weights.dsp[par][:, hl, m, :] for hl in range(2))) for m in range(M)]).then_inc(y_ready, 1)

        turn_rows(0, 0, 0)
        turn_rows(1, 1, 0)
        up(0, 0, 0)

        def slot(j, par, turn):
            ahead(j, par, turn, 1, up)
            ahead(j, par, turn, 2, turn_rows)
            down(j, par, turn)

        run_blocks(pe, slot)

    @block.vector
    def _(dve):
        dve.sem_inc(xt_split, 1)
        dve.sem_inc(h_done, UP_PAIRS)
        dve.sem_inc(y_done, TPB)

        up_part = lambda j, par, turn: weights.split_up_lo(dve, j, par)
        down_part = lambda j, par, turn: weights.split_down_lo(dve, j, par)

        def rows_part(j, par, turn):
            dve.wait_ge(xt_hi, j + 1)
            dve.scalar_tensor_tensor(xt[par][:, 1].rearrange("p c q -> p (c q)"), T, SPLIT,
                                     xt[par][:, 0].rearrange("p c q -> p (c q)"),
                                     ALU.mult, ALU.subtract).then_inc(xt_split, 1)

        def hidden(j, par, turn):
            for q in range(UP_PAIRS):
                n = UP_PAIRS * j + q
                dve.wait_ge(h_gelu, UP_PAIRS + n + 1)
                if q == 0:
                    dve.wait_ge(y_ready, TPB * (j + 1))
                dve.tensor_scalar(hs[par][:, 0, 2 * q:2 * q + 2, :], hf[:, q], SPLIT, None, ALU.mult).then_inc(h_hi, 1)
                dve.wait_ge(h_hi, n + 1)
                dve.scalar_tensor_tensor(hs[par][:, 1, 2 * q:2 * q + 2, :], hf[:, q], SPLIT, hs[par][:, 0, 2 * q:2 * q + 2, :],
                                         ALU.mult, ALU.subtract).then_inc(h_done, 1)

        def output(j, par, turn, wait=True):
            if wait:
                dve.wait_ge(y_stored[par], 16 * turn)
            for ti in range(TPB):
                dve.wait_ge(y_ready, TPB * (j + 2) + ti + 1)
                dve.tensor_copy(yo[par][:, ti, :], Y(ti)).then_inc(y_done, 1)

        rows_part(0, 0, 0)
        rows_part(1, 1, 0)
        hidden(0, 0, 0)

        def slot(j, par, turn):
            if not (isinstance(j, int) and j == 0):
                output(j - 1, 1 - par, turn - (1 - par), not (isinstance(j, int) and j <= 2))
            ahead(j, par, turn, 2, up_part)
            ahead(j, par, turn, 1, hidden)
            ahead(j, par, turn, 2, rows_part)
            ahead(j, par, turn, 1, down_part)

        run_blocks(dve, slot)
        output(NB - 1, (NB - 1) % 2, (NB - 1) // 2)


def combine(nc, s, t, sem, sb, rows_out, slot_of, weight_of, out):
    back = sb("back", [P, CHOICES, D])
    fetched = [sem(f"fetched{n}") for n in range(CHOICES // GATHER_GROUP)]
    added, stored = sem("added"), sem("stored")
    with nc.Block() as block:

        @block.gpsimd
        def _(pool):
            for n in range(CHOICES):
                pool.indirect_dma_start(back[:, n, :], None, rows_out[:, :],
                                        bass.IndirectOffsetOnAxis(slot_of[:, n:n + 1], 0)).then_inc(fetched[n // GATHER_GROUP], 16)

        @block.vector
        def _(dve):
            for n in range(CHOICES):
                tile = n % TILES
                if n % GATHER_GROUP == 0:
                    dve.wait_ge(fetched[n // GATHER_GROUP], 16 * GATHER_GROUP)
                    if n >= TILES:
                        dve.wait_ge(added, n + GATHER_GROUP - TILES)
                dve.scalar_tensor_tensor(s.x[:, tile, :], back[:, n, :], weight_of[:, n:n + 1], s.x[:, tile, :],
                                         ALU.mult, ALU.add).then_inc(added, 1)

        @block.sync
        def _(sp):
            for q in range(TILES // GATHER_GROUP):
                tiles = slice(GATHER_GROUP * q, GATHER_GROUP * (q + 1))
                sp.wait_ge(added, CHOICES - TILES + GATHER_GROUP * (q + 1))
                sp.dma_start(out.rearrange("b (t p) d -> p (b t) d", p=P)[:, tiles, :], s.x[:, tiles, :]).then_inc(stored, 16)
            sp.wait_ge(stored, 16 * TILES // GATHER_GROUP)


OUTPUTS = {"out": ((B, SQ, D), F32)}


def build(nc, a, out):
    s = Store()
    with ExitStack() as ctx:
        sb = lambda name, shape, dt=F32: ctx.enter_context(nc.sbuf_tensor(name, shape, dt))
        s.x = sb("x", [P, TILES, D])
        s.w0 = [sb(f"w0_{n}", [P, 2, C, D], F16) for n in "qkvo"]
        s.w1 = [sb(f"w1_{n}", [P, 2, C, D], F16) for n in "qkvo"]
        s.fq, s.fk = sb("fq", [P, 2, C, H * DH], F16), sb("fk", [P, 2, C, H * DH], F16)
        s.fv = sb("fv", [P, 2, C, E0 * DH], F16)
        s.fg = sb("fg", [P, 2, C, 2 * H * E0], F16)
        s.fo = sb("fo", [P, 2, E0 // 2, D], F16)
        s.wg = sb("wg", [P, 2, C, E1], F16)
        s.ident = sb("ident", [P, P])
        s.head_of = sb("head_of", [P, 8])
        s.stage_step = [ctx.enter_context(nc.semaphore(f"stage_step{i}")) for i in range(3)]
        s.rank = sb("rank", [P, E1])
        s.rows_in = nc.dram_tensor("expert_in", (NB * BT, D), F32).ap()
        s.bqk = sb("bqk", [P, 8])
        s.bup = sb("bup", [P, E1, HID // P])
        s.bv, s.bo = sb("bv", [P, 2, D]), sb("bo", [P, 2, D])
        s.bdown = sb("bdown", [E1, D])
        s.causal = sb("causal", [P, TPB, SK])
        s.tg, s.tgu = sb("tg", [P, 4]), sb("tgu", [P, 4])
        s.mv, s.mvs, s.bn = sb("mv", [P, TILES, 2]), sb("mvs", [P, 2]), sb("bn", [P, 6])
        s.xs = sb("xs", [P, D])
        s.var, s.nt, s.rstd = sb("var", [P, TILES]), sb("nt", [P, TILES]), sb("rstd", [P, TILES])
        setup_stage(nc, a, s)
        for stage in STAGES:
            if stage in (0, 1):
                xattn_stage(nc, a, s, stage)
            elif stage == "ffn":
                ffn_stage(nc, a, s)
            elif stage == "moe":
                moe_stage(nc, a, s, out)
            else:
                store_stage(nc, a, s, out)


def store_stage(nc, a, s, out):
    with ExitStack() as ctx:
        done = ctx.enter_context(nc.semaphore("out_stored"))
        block = ctx.enter_context(nc.Block())

        @block.sync
        def _(sp):
            sp.dma_start(out.rearrange("b (t p) d -> p (b t) d", p=P), s.x[:]).then_inc(done, 16)
            sp.wait_ge(done, 16)


STAGES = (0, "ffn", 1, "moe")

_INS = ['x', 'ctx_1024', 'mask_Bx1xS2_bk0', 'mask_SxS2_fk0', 'mask_BxS2_bf0', 'g_xattn', 'g_ffn',
        'L0_xattn_Wq', 'L0_xattn_bq', 'L0_xattn_Wk', 'L0_xattn_bk', 'L0_xattn_Wv', 'L0_xattn_bv',
        'L0_xattn_Wo', 'L0_xattn_bo', 'L0_ffn_Wq', 'L0_ffn_Wk', 'L0_ffn_Wv', 'L0_ffn_Ws', 'L0_ffn_Wd',
        'L0_ffn_Wo', 'L1_xattn_W_q', 'L1_xattn_b_q', 'L1_xattn_W_k', 'L1_xattn_b_k', 'L1_xattn_W_v',
        'L1_xattn_b_v', 'L1_xattn_W_o', 'L1_xattn_b_o', 'L1_ffn_Wg', 'L1_ffn_Wup', 'L1_ffn_bup',
        'L1_ffn_Wdown', 'L1_ffn_bdown']


def kernel(**inputs):
    import numpy as _np
    import concourse.bacc as _bacc
    from concourse import mybir as _mybir
    from concourse.bass_utils import run_bass_kernel_spmd as _run

    nc = _bacc.Bacc("TRN2", target_bir_lowering=False, num_devices=1)
    arrays, drams = {}, {}
    for name in _INS:
        v = _np.ascontiguousarray(inputs[name])
        arrays[f"in_{name}"] = v
        drams[name] = nc.dram_tensor(f"in_{name}", v.shape, _mybir.dt.from_np(v.dtype), kind="ExternalInput").ap()
    out = nc.dram_tensor("out_0", (B, SQ, D), F32, kind="ExternalOutput").ap()
    build(nc, drams, out)
    r = _run(nc, [arrays], core_ids=[0])
    return r.results[0]["out_0"]
```
